# Optimizing a Trainium2 kernel written in Bass

```python
import numpy as np
import jax
import jax.numpy as jnp

def _softmax(x, axis=-1):
    return jax.nn.softmax(x, axis=axis)

def _gelu(x):
    return jax.nn.gelu(x, approximate=True)

def _silu(x):
    return jax.nn.silu(x)

def _sigmoid(x):
    return jax.nn.sigmoid(x)

def _layernorm(x, axis=-1, eps=1e-05):
    m = jnp.mean(x, axis=axis, keepdims=True)
    v = jnp.var(x, axis=axis, keepdims=True)
    return (x - m) / jnp.sqrt(v + eps)

def _scatter_add(tgt, idx, src, axis=0):
    return tgt.at[idx].add(src)

def _segment_sum(src, seg, n):
    return jax.ops.segment_sum(src, seg, n)
kernel_name = 'mk_flamingo_gated_d2_seqx_r4_18d514'

def setup_inputs(seed: int=0):
    np.random.seed(seed)
    _w = jnp.asarray

    def _rec_inputs():
        import jax
        import jax.numpy as jnp
        _rk = jax.random.key(seed)
        x = 0.0003765 + 1 * jax.random.normal(jax.random.fold_in(_rk, 1), (16, 100, 256), jnp.float32)
        _lenS = 100 - jax.random.randint(jax.random.fold_in(_rk, 7), (16,), 0, max(1, 100 // 4) + 1, jnp.int32)
        _lenS2 = 361 - jax.random.randint(jax.random.fold_in(_rk, 8), (16,), 0, max(1, 361 // 4) + 1, jnp.int32)
        _ctx_1024P = jax.random.normal(jax.random.fold_in(_rk, 11), (16, 16, 256), jnp.float32)
        _ctx_1024c = jax.random.dirichlet(jax.random.fold_in(_rk, 511), 0.3 * jnp.ones((16,), jnp.float32), (16, 361))
        _ctx_1024t = jnp.einsum('bsk,bkd->bsd', _ctx_1024c, _ctx_1024P)
        _ctx_1024t = _ctx_1024t * jax.lax.rsqrt(jnp.mean(jnp.square(_ctx_1024t)) + 1e-12) * 0.953939
        ctx_1024 = -0.000292821 + 1.00034 * (_ctx_1024t + 0.3 * jax.random.normal(jax.random.fold_in(_rk, 611), (16, 361, 256), jnp.float32))
        _validS = jnp.arange(100)[None, :] < _lenS[:, None]
        _validS2 = jnp.arange(361)[None, :] < _lenS2[:, None]
        _causal = jnp.tril(jnp.ones((100, 100), dtype=bool))
        mask_BxSxS2_bk1 = jnp.broadcast_to(_validS2[:, None, :], (16, 100, 361))
        _g = jax.random.normal(jax.random.fold_in(_rk, 9001), (2, 2), jnp.float32)
        _g = jnp.sign(_g) * jnp.maximum(jnp.abs(_g), 1.0) + (_g == 0) * 1.0
        g_xattn = _g[0]
        g_ffn = _g[1]
        return (x, ctx_1024, _lenS2, mask_BxSxS2_bk1, g_xattn, g_ffn)
    x, ctx_1024, _lenS2, mask_BxSxS2_bk1, g_xattn, g_ffn = _rec_inputs()

    def _L0_xattn_setup():
        import jax, jax.numpy as jnp
        import numpy as np
        B, S, D, H = (2, 512, 256, 16)
        DH = D // H
        key = jax.random.key(seed)
        ks = jax.random.split(key, 12)
        scale = 1.0 / np.sqrt(D)
        inp = {'key': jax.random.normal(ks[0], (B, S, D), jnp.float32), 'value': jax.random.normal(ks[1], (B, S, D), jnp.float32), 'query': jax.random.normal(ks[2], (B, S, D), jnp.float32), 'mask': jax.random.randint(ks[3], (B, S, S), 0, 2) == 1, 'Wq': jax.random.normal(ks[4], (D, D), jnp.float32) * scale, 'bq': jnp.zeros((D,), jnp.float32), 'Wk': jax.random.normal(ks[5], (D, D), jnp.float32) * scale, 'bk': jnp.zeros((D,), jnp.float32), 'Wv': jax.random.normal(ks[6], (D, D), jnp.float32) * scale, 'bv': jnp.zeros((D,), jnp.float32), 'Wo': jax.random.normal(ks[7], (D, D), jnp.float32) * scale, 'bo': jnp.zeros((D,), jnp.float32)}
        return inp
    _L0_xattn_all = _L0_xattn_setup()
    _L0_xattn_in = {k: v for k, v in _L0_xattn_all.items() if k in ('Wq', 'bq', 'Wk', 'bk', 'Wv', 'bv', 'Wo', 'bo')}
    del _L0_xattn_all

    def _L0_ffn_setup():
        import math
        import jax, jax.numpy as jnp
        import numpy as np
        B, T, D, H, E, K, S = (4, 1024, 256, 512, 16, 2, 2)
        ROUTE_SCALE = 1.0

        def _swiglu(x, w1, w3, w2):
            return jax.nn.silu(x @ w1) * (x @ w3) @ w2
        key = jax.random.key(seed)
        ks = jax.random.split(key, 9)
        s = 0.02
        return {'x': jax.random.normal(ks[0], (B, T, D), jnp.float32), 'gate_w': jax.random.normal(ks[1], (D, E), jnp.float32) * s, 'gate_b': jnp.zeros((E,), jnp.float32), 'ew1': jax.random.normal(ks[2], (E, D, H), jnp.float32) * s, 'ew3': jax.random.normal(ks[3], (E, D, H), jnp.float32) * s, 'ew2': jax.random.normal(ks[4], (E, H, D), jnp.float32) * s, 'sw1': jax.random.normal(ks[5], (S, D, H), jnp.float32) * s, 'sw3': jax.random.normal(ks[6], (S, D, H), jnp.float32) * s, 'sw2': jax.random.normal(ks[7], (S, H, D), jnp.float32) * s}
    _L0_ffn_all = _L0_ffn_setup()
    _L0_ffn_in = {k: v for k, v in _L0_ffn_all.items() if k in ('gate_w', 'gate_b', 'ew1', 'ew3', 'ew2', 'sw1', 'sw3', 'sw2')}
    del _L0_ffn_all

    def _L1_xattn_setup():
        import jax, jax.numpy as jnp
        import numpy as np
        DIM, HEADS, HEAD_DIM = (256, 16, 64)
        B, L, S = (4, 512, 512)
        EPS = 1e-05
        NEG_INF = -1000000000.0

        def rms_norm(x, w):
            var = jnp.mean(jnp.square(x), axis=-1, keepdims=True)
            return x * jax.lax.rsqrt(var + EPS) * w
        key = jax.random.key(seed)
        ks = jax.random.split(key, 9)
        hd = HEADS * HEAD_DIM
        scale = 1.0 / np.sqrt(DIM)
        return {'q': jax.random.normal(ks[0], (B, L, DIM), dtype=jnp.float32), 'kv': jax.random.normal(ks[1], (B, S, DIM), dtype=jnp.float32), 'x_seqlens': jax.random.randint(ks[2], (B,), 1, S + 1, dtype=jnp.int32), 'Wq': jax.random.normal(ks[3], (DIM, hd), dtype=jnp.float32) * scale, 'Wk': jax.random.normal(ks[4], (DIM, hd), dtype=jnp.float32) * scale, 'Wv': jax.random.normal(ks[5], (DIM, hd), dtype=jnp.float32) * scale, 'Wo': jax.random.normal(ks[6], (hd, DIM), dtype=jnp.float32) * (1.0 / np.sqrt(hd)), 'q_norm_w': jnp.ones((HEAD_DIM,), dtype=jnp.float32), 'k_norm_w': jnp.ones((HEAD_DIM,), dtype=jnp.float32)}
    _L1_xattn_all = _L1_xattn_setup()
    _L1_xattn_in = {k: v for k, v in _L1_xattn_all.items() if k in ('Wq', 'Wk', 'Wv', 'Wo', 'q_norm_w', 'k_norm_w')}
    del _L1_xattn_all

    def _L1_ffn_setup():
        import jax, jax.numpy as jnp
        import numpy as np
        B, S, H = (8, 256, 256)
        FF = 1024
        E = 8
        TOP_K = 2
        LN_EPS = 1e-12

        def _layernorm(x, w, b):
            mu = jnp.mean(x, axis=-1, keepdims=True)
            var = jnp.mean(jnp.square(x - mu), axis=-1, keepdims=True)
            return (x - mu) * jax.lax.rsqrt(var + LN_EPS) * w + b
        key = jax.random.key(seed)
        ks = jax.random.split(key, 8)
        sc_h = 1.0 / np.sqrt(H)
        sc_ff = 1.0 / np.sqrt(FF)
        return {'hidden_states': jax.random.normal(ks[0], (B, S, H), jnp.float32), 'router_w': jax.random.normal(ks[1], (E, H), jnp.float32) * sc_h, 'router_b': jnp.zeros((E,), jnp.float32), 'w1': jax.random.normal(ks[2], (E, FF, H), jnp.float32) * sc_h, 'b1': jax.random.normal(ks[3], (E, FF), jnp.float32) * 0.01, 'w2': jax.random.normal(ks[4], (E, H, FF), jnp.float32) * sc_ff, 'b2': jax.random.normal(ks[5], (E, H), jnp.float32) * 0.01, 'ln_w': jnp.ones((H,), jnp.float32), 'ln_b': jnp.zeros((H,), jnp.float32)}
    _L1_ffn_all = _L1_ffn_setup()
    _L1_ffn_in = {k: v for k, v in _L1_ffn_all.items() if k in ('router_w', 'router_b', 'w1', 'b1', 'w2', 'b2', 'ln_w', 'ln_b')}
    del _L1_ffn_all
    return {'x': x, 'ctx_1024': ctx_1024, '_lenS2': _lenS2, 'mask_BxSxS2_bk1': mask_BxSxS2_bk1, 'g_xattn': g_xattn, 'g_ffn': g_ffn, 'L0_xattn_Wq': _L0_xattn_in['Wq'], 'L0_xattn_bq': _L0_xattn_in['bq'], 'L0_xattn_Wk': _L0_xattn_in['Wk'], 'L0_xattn_bk': _L0_xattn_in['bk'], 'L0_xattn_Wv': _L0_xattn_in['Wv'], 'L0_xattn_bv': _L0_xattn_in['bv'], 'L0_xattn_Wo': _L0_xattn_in['Wo'], 'L0_xattn_bo': _L0_xattn_in['bo'], 'L0_ffn_gate_w': _L0_ffn_in['gate_w'], 'L0_ffn_gate_b': _L0_ffn_in['gate_b'], 'L0_ffn_ew1': _L0_ffn_in['ew1'], 'L0_ffn_ew3': _L0_ffn_in['ew3'], 'L0_ffn_ew2': _L0_ffn_in['ew2'], 'L0_ffn_sw1': _L0_ffn_in['sw1'], 'L0_ffn_sw3': _L0_ffn_in['sw3'], 'L0_ffn_sw2': _L0_ffn_in['sw2'], 'L1_xattn_Wq': _L1_xattn_in['Wq'], 'L1_xattn_Wk': _L1_xattn_in['Wk'], 'L1_xattn_Wv': _L1_xattn_in['Wv'], 'L1_xattn_Wo': _L1_xattn_in['Wo'], 'L1_xattn_q_norm_w': _L1_xattn_in['q_norm_w'], 'L1_xattn_k_norm_w': _L1_xattn_in['k_norm_w'], 'L1_ffn_router_w': _L1_ffn_in['router_w'], 'L1_ffn_router_b': _L1_ffn_in['router_b'], 'L1_ffn_w1': _L1_ffn_in['w1'], 'L1_ffn_b1': _L1_ffn_in['b1'], 'L1_ffn_w2': _L1_ffn_in['w2'], 'L1_ffn_b2': _L1_ffn_in['b2'], 'L1_ffn_ln_w': _L1_ffn_in['ln_w'], 'L1_ffn_ln_b': _L1_ffn_in['ln_b']}

def reference(x, ctx_1024, _lenS2, mask_BxSxS2_bk1, g_xattn, g_ffn, L0_xattn_Wq, L0_xattn_bq, L0_xattn_Wk, L0_xattn_bk, L0_xattn_Wv, L0_xattn_bv, L0_xattn_Wo, L0_xattn_bo, L0_ffn_gate_w, L0_ffn_gate_b, L0_ffn_ew1, L0_ffn_ew3, L0_ffn_ew2, L0_ffn_sw1, L0_ffn_sw3, L0_ffn_sw2, L1_xattn_Wq, L1_xattn_Wk, L1_xattn_Wv, L1_xattn_Wo, L1_xattn_q_norm_w, L1_xattn_k_norm_w, L1_ffn_router_w, L1_ffn_router_b, L1_ffn_w1, L1_ffn_b1, L1_ffn_w2, L1_ffn_b2, L1_ffn_ln_w, L1_ffn_ln_b):
    import jax
    import jax.numpy as jnp

    def _L0_xattn_ref(key, value, query, mask, Wq, bq, Wk, bk, Wv, bv, Wo, bo):
        import jax, jax.numpy as jnp
        import numpy as np
        B, S, D, H = (2, 512, 256, 16)
        DH = D // H
        b, s, d = query.shape
        dh = d // H

        def split_heads(x):
            return x.reshape(b, -1, H, dh).transpose(0, 2, 1, 3)
        q = split_heads(query @ Wq + bq) / jnp.sqrt(jnp.float32(dh))
        k = split_heads(key @ Wk + bk)
        v = split_heads(value @ Wv + bv)
        scores = jnp.einsum('bhqd,bhkd->bhqk', q, k)
        scores = jnp.where(mask[:, None, :, :], jnp.float32(-1e+18), scores)
        attn = jax.nn.softmax(scores, axis=-1)
        ctx = jnp.einsum('bhqk,bhkd->bhqd', attn, v)
        ctx = ctx.transpose(0, 2, 1, 3).reshape(b, s, d)
        return ctx @ Wo + bo

    def _L0_ffn_ref(x, gate_w, gate_b, ew1, ew3, ew2, sw1, sw3, sw2):
        import math
        import jax, jax.numpy as jnp
        import numpy as np
        B, T, D, H, E, K, S = (4, 1024, 256, 512, 16, 2, 2)
        ROUTE_SCALE = 1.0

        def _swiglu(x, w1, w3, w2):
            return jax.nn.silu(x @ w1) * (x @ w3) @ w2
        Bx, Tx, Dx = x.shape
        flat = x.reshape(-1, Dx)
        N = flat.shape[0]
        n_experts = gate_w.shape[1]
        logits = flat @ gate_w
        scores = jax.nn.softmax(logits.astype(jnp.float32), -1) + gate_b
        _, topi = jax.lax.top_k(scores, K)
        weights = jnp.take_along_axis(logits, topi, axis=-1) * ROUTE_SCALE
        weights = weights.astype(flat.dtype)
        capacity = math.ceil(N * K / n_experts * 1.25)

        def per_expert(gid, w1, w3, w2):
            match = topi == gid
            assigned = match.any(-1)
            w_tok = jnp.sum(jnp.where(match, weights, 0.0), -1)
            wm = jnp.where(assigned, w_tok, -jnp.inf)
            vals, idx = jax.lax.top_k(wm, capacity)
            valid = assigned[idx]
            xs = flat[idx]
            y = _swiglu(xs, w1, w3, w2) * jnp.where(valid, vals, 0.0)[:, None]
            return (idx, y)
        idxs, ys = jax.vmap(per_expert)(jnp.arange(n_experts), ew1, ew3, ew2)
        out = jnp.zeros_like(flat).at[idxs.reshape(-1)].add(ys.reshape(-1, Dx))
        shared = jax.vmap(lambda w1, w3, w2: _swiglu(flat, w1, w3, w2))(sw1, sw3, sw2)
        out = out + shared.mean(0)
        return out.reshape(Bx, Tx, Dx)

    def _L1_xattn_ref(q, kv, x_seqlens, Wq, Wk, Wv, Wo, q_norm_w, k_norm_w):
        import jax, jax.numpy as jnp
        import numpy as np
        DIM, HEADS, HEAD_DIM = (256, 16, 64)
        B, L, S = (4, 512, 512)
        EPS = 1e-05
        NEG_INF = -1000000000.0

        def rms_norm(x, w):
            var = jnp.mean(jnp.square(x), axis=-1, keepdims=True)
            return x * jax.lax.rsqrt(var + EPS) * w
        b, l, _ = q.shape
        s = kv.shape[1]
        qh = (q @ Wq).reshape(b, l, HEADS, HEAD_DIM).transpose(0, 2, 1, 3)
        kh = (kv @ Wk).reshape(b, s, HEADS, HEAD_DIM).transpose(0, 2, 1, 3)
        vh = (kv @ Wv).reshape(b, s, HEADS, HEAD_DIM).transpose(0, 2, 1, 3)
        qh = rms_norm(qh, q_norm_w)
        kh = rms_norm(kh, k_norm_w)
        mask = (jnp.arange(s, dtype=jnp.int32)[None, :] < x_seqlens[:, None])[:, None, None, :]
        scores = jnp.einsum('bhld,bhsd->bhls', qh, kh) * (1.0 / np.sqrt(HEAD_DIM))
        scores = jnp.where(mask, scores, NEG_INF)
        attn = jax.nn.softmax(scores, axis=-1)
        o = jnp.einsum('bhls,bhsd->bhld', attn, vh)
        o = o.transpose(0, 2, 1, 3).reshape(b, l, HEADS * HEAD_DIM)
        return o @ Wo

    def _L1_ffn_ref(hidden_states, router_w, router_b, w1, b1, w2, b2, ln_w, ln_b):
        import jax, jax.numpy as jnp
        import numpy as np
        B, S, H = (8, 256, 256)
        FF = 1024
        E = 8
        TOP_K = 2
        LN_EPS = 1e-12

        def _layernorm(x, w, b):
            mu = jnp.mean(x, axis=-1, keepdims=True)
            var = jnp.mean(jnp.square(x - mu), axis=-1, keepdims=True)
            return (x - mu) * jax.lax.rsqrt(var + LN_EPS) * w + b
        b, s, h = hidden_states.shape
        flat = hidden_states.reshape(-1, h)
        logits = flat @ router_w.T + router_b
        topk_vals, topk_idx = jax.lax.top_k(logits, TOP_K)
        topk_w = jax.nn.softmax(topk_vals, axis=-1)
        out = jnp.zeros_like(flat)
        n_exp = w1.shape[0]
        for e in range(n_exp):
            cw = jnp.sum(jnp.where(topk_idx == e, topk_w, 0.0), axis=-1)
            y = jax.nn.gelu(flat @ w1[e].T + b1[e], approximate=False)
            y = y @ w2[e].T + b2[e]
            out = out + y * cw[:, None]
        out = out.reshape(b, s, h) + hidden_states
        return _layernorm(out, ln_w, ln_b)
    x = x + jnp.tanh(g_xattn[0]) * _L0_xattn_ref(ctx_1024, ctx_1024, _layernorm(x, axis=-1), mask_BxSxS2_bk1, L0_xattn_Wq, L0_xattn_bq, L0_xattn_Wk, L0_xattn_bk, L0_xattn_Wv, L0_xattn_bv, L0_xattn_Wo, L0_xattn_bo)
    x = x + jnp.tanh(g_ffn[0]) * _L0_ffn_ref(_layernorm(x, axis=-1), L0_ffn_gate_w, L0_ffn_gate_b, L0_ffn_ew1, L0_ffn_ew3, L0_ffn_ew2, L0_ffn_sw1, L0_ffn_sw3, L0_ffn_sw2)
    x = x + jnp.tanh(g_xattn[1]) * _L1_xattn_ref(_layernorm(x, axis=-1), ctx_1024, _lenS2, L1_xattn_Wq, L1_xattn_Wk, L1_xattn_Wv, L1_xattn_Wo, L1_xattn_q_norm_w, L1_xattn_k_norm_w)
    x = x + jnp.tanh(g_ffn[1]) * _L1_ffn_ref(_layernorm(x, axis=-1), L1_ffn_router_w, L1_ffn_router_b, L1_ffn_w1, L1_ffn_b1, L1_ffn_w2, L1_ffn_b2, L1_ffn_ln_w, L1_ffn_ln_b)
    return x

_drawn_inputs = setup_inputs


def setup_inputs(seed=0):
    import zlib

    import numpy as np

    out = dict(_drawn_inputs(seed))
    spreads = {'g_ffn': (-1.0, 0.2),
     'L0_xattn_bq': (0.0, 0.1),
     'L0_xattn_bk': (0.0, 0.8),
     'L0_xattn_bv': (0.0, 0.1),
     'L0_xattn_bo': (0.0, 0.1),
     'L0_ffn_gate_b': (0.0, 0.1),
     'L1_xattn_q_norm_w': (1.0, 0.2),
     'L1_xattn_k_norm_w': (1.0, 0.2),
     'L1_ffn_router_b': (0.0, 0.1),
     'L1_ffn_ln_w': (1.0, 0.2),
     'L1_ffn_ln_b': (0.0, 0.1)}
    factors = {'L1_ffn_b1': 8.0, 'L1_ffn_b2': 5.804}
    for name, (base, spread) in spreads.items():
        noise = np.random.default_rng([zlib.crc32(name.encode()), seed]).standard_normal(out[name].shape)
        drawn = base * np.exp(spread * noise) if base else spread * noise
        out[name] = jnp.asarray(drawn.astype(out[name].dtype))
    for name, factor in factors.items():
        out[name] = (out[name] * factor).astype(out[name].dtype)
    return out
```

```python
from contextlib import ExitStack

import concourse.bass as bass
from concourse import mybir

ALU = mybir.AluOpType
ACT = mybir.ActivationFunctionType
AX = mybir.AxisListType
F32 = mybir.dt.float32
BF16 = mybir.dt.bfloat16
I32 = mybir.dt.int32
U8 = mybir.dt.uint8

P = 128
B, S, D = 16, 100, 256
N = B * S
KD = D // P
KEYS = 361
KEY_TILES = [(0, 128), (128, 128), (256, KEYS - 256)]
HEADS = 16
LN_EPS, RMS_EPS, LAST_EPS = 1e-5, 1e-5, 1e-12
CREDIT = 1
MASKED = 1e18
BIG = 1e30

E0, FF0, SHARED = 16, 512, 2
CAP0 = -(-N * 2 // E0 * 5 // 4)
HALF0 = CAP0 // 2
E1, FF1 = 8, 1024
BLK1 = 256
NBLK1 = (2 * N + E1 * (BLK1 - 1)) // BLK1
MAXB1 = -(-N // BLK1)


class Steps:

    def __init__(self, eng, sem, base=0):
        self.eng, self.sem, self.base, self.n = eng, sem, base, 0

    def then(self, ins):
        self.n += 1
        ins.then_inc(self.sem, 1)
        self.eng.wait_ge(self.sem, self.base + self.n)


def bcast(ap, n):
    return ap.unsqueeze(len(ap.shape)).to_broadcast([*ap.shape, n])


def spread(ap, n):
    return ap.unsqueeze(1).to_broadcast([ap.shape[0], n, *ap.shape[1:]])


class Core:

    def __init__(self, nc, ctx, ins, out):
        self.nc, self.ins, self.out = nc, ins, out

        def sb(name, shape, dt=F32):
            return ctx.enter_context(nc.sbuf_tensor(name, shape, dt))

        self.x = sb("x_tokens", [S, B, D])
        self.xn = sb("x_normed", [S, B, D])
        self.xnT = sb("x_normed_T", [P, KD, N])
        self.ident = sb("identity", [P, P])
        self.ones = sb("ones", [P, P])
        self.tri = sb("tri_before", [P, P])
        self.gates = sb("gates", [P, 4])
        self.half = sb("minus_half", [P, 64])
        self.rows = nc.dram_tensor("rows_dram", [N, D], F32, kind="Internal").ap()
        self.result0 = nc.dram_tensor("results0_dram", [E0 * CAP0 + P, D], F32, kind="Internal").ap()
        self.result1 = nc.dram_tensor("results1_dram", [NBLK1 * BLK1, D], F32, kind="Internal").ap()
        self.bounce = nc.dram_tensor("turn_dram", [3, 2, P, S], F32, kind="Internal").ap()


class Phase:

    def __init__(self, core, name):
        self.core, self.nc, self.name, self.ctx = core, core.nc, name, ExitStack()
        self.sems, self.all_sems = [], []

    def __enter__(self):
        return self

    def __exit__(self, *a):
        self.nc.clear_and_free_semaphores(self.all_sems)
        self.nc.all_engine_barrier()
        return self.ctx.__exit__(*a)

    def sb(self, name, shape, dt=F32):
        return self.ctx.enter_context(self.nc.sbuf_tensor(f"{self.name}_{name}", shape, dt))

    def ps(self, name, shape=(P, 512), dt=F32):
        return self.ctx.enter_context(self.nc.psum_tensor(f"{self.name}_{name}", list(shape), dt))

    def sem(self, name):
        s = self.plain(name)
        self.sems.append(s)
        return s

    def plain(self, name):
        s = self.nc.alloc_semaphore(f"{self.name}_{name}")
        self.all_sems.append(s)
        return s

    def credit(self, sems=None):
        with self.nc.Block() as block:
            @block.sync
            def _(sync):
                for s in sems or self.sems:
                    sync.sem_inc(s, CREDIT)


def setup_phase(core):
    nc = core.nc
    with Phase(core, "setup") as ph:
        zeros = ph.sb("zeros", [P, D])
        g_raw = ph.sb("g_raw", [P, 4])
        loaded, cleared = ph.sem("loaded"), ph.sem("cleared")
        zeros_ready, blanks, shapes = ph.sem("zeros_ready"), ph.sem("blanks"), ph.sem("shapes")
        gates_ready = ph.sem("gates_ready")
        with nc.Block() as block:
            @block.sync
            def _(sync):
                sync.dma_start(core.x[:], core.ins["x"].rearrange("b s d -> s b d")).then_inc(loaded, 16)
                for j, g in enumerate(("g_xattn", "g_ffn")):
                    sync.dma_start(g_raw[:, 2 * j:2 * j + 2], core.ins[g].partition_broadcast(P)).then_inc(loaded, 16)
                sync.wait_ge(zeros_ready, 1)
                sync.dma_start(core.result0[E0 * CAP0:], zeros[:]).then_inc(cleared, 16)
                sync.wait_ge(cleared, 16)
                sync.wait_ge(loaded, 48)

            @block.gpsimd
            def _(pool):
                pool.memset(core.ident[:], 0.0).then_inc(blanks, 1)
                pool.memset(core.tri[:], 0.0).then_inc(blanks, 1)
                pool.memset(core.ones[:], 1.0).then_inc(blanks, 1)
                pool.memset(core.half[:], -0.5).then_inc(blanks, 1)
                pool.wait_ge(blanks, 4)
                pool.affine_select(out=core.ident[:], in_=core.ident[:], compare_op=ALU.not_equal, fill=1.0,
                                   base=0, pattern=[[-1, P]], channel_multiplier=1).then_inc(shapes, 1)
                pool.affine_select(out=core.tri[:], in_=core.tri[:], compare_op=ALU.is_ge, fill=1.0,
                                   base=0, pattern=[[-1, P]], channel_multiplier=1).then_inc(shapes, 1)
                pool.wait_ge(shapes, 2)

            @block.vector
            def _(dve):
                nc.vector.memset(zeros[:], 0.0).then_inc(zeros_ready, 1)

            @block.scalar
            def _(act):
                act.wait_ge(loaded, 48)
                nc.scalar.activation(core.gates[:], g_raw[:], ACT.Tanh).then_inc(gates_ready, 1)
                act.wait_ge(gates_ready, 1)


def norm_phase(core, name, router=None):
    nc = core.nc
    with Phase(core, name) as ph:
        stats = ph.sb("stats", [S, B, 6])
        work = ph.sb("work", [S, 4, B])
        mean, rstd, t0, t1 = (work[:, k, :] for k in range(4))
        stage = ph.sb("stage", [S, 2, D])
        turned = ph.sb("turned", [P, 2, KD, S])
        psT = [ph.ps(f"psT{j}") for j in range(2)]
        psL = [ph.ps(f"psL{j}") for j in range(2)]
        stats_done, moments, rstd_ready = ph.sem("stats_done"), ph.sem("moments"), ph.sem("rstd_ready")
        normed, turned_ps, copied = ph.sem("normed"), ph.sem("turned_ps"), ph.sem("copied")
        scored, scores_copied, w_loaded = ph.sem("scored"), ph.sem("scores_copied"), ph.sem("w_loaded")
        pool_steps, kept = ph.sem("pool_steps"), ph.sem("kept")
        if router:
            w_dram, b_dram, logits = router
            E = logits.shape[2]
            w_sb = ph.sb("w", [P, KD, E])
            b_sb = ph.sb("b", [S, E])

        ph.credit()
        with nc.Block() as block:
            if router:
                @block.sync
                def _(sync):
                    sync.dma_start(w_sb[:], w_dram.rearrange("(k p) e -> p k e", p=P)).then_inc(w_loaded, 16)
                    if b_dram is not None:
                        sync.dma_start(b_sb[:], b_dram.partition_broadcast(S)).then_inc(w_loaded, 16)

            @block.vector
            def _(dve):
                with dve.Fori(0, B) as i:
                    nc.vector.bn_stats(stats[:, i, :], core.x[:, i, :]).then_inc(stats_done, 1)
                dve.wait_ge(stats_done, CREDIT + B)
                step = Steps(dve, moments, CREDIT)
                me, ve, mo, vo = (stats[:, :, k] for k in (1, 2, 4, 5))
                step.then(nc.vector.tensor_tensor(mean, me, mo, ALU.add))
                step.then(nc.vector.tensor_scalar(mean, mean, 0.5, None, ALU.mult))
                step.then(nc.vector.tensor_tensor(t0, me, mo, ALU.subtract))
                step.then(nc.vector.scalar_tensor_tensor(t0, t0, 0.25, t0, ALU.mult, ALU.mult))
                step.then(nc.vector.tensor_tensor(t1, ve, vo, ALU.add))
                step.then(nc.vector.scalar_tensor_tensor(t1, t1, 1.0 / D, t0, ALU.mult, ALU.add))
                dve.wait_ge(rstd_ready, CREDIT + 1)
                with dve.Fori(0, B // 2) as j:
                    for q in range(2):
                        dve.wait_ge(turned_ps, CREDIT + 2 * j)
                        dve.wait_ge(kept, CREDIT + 2 * j)
                        nc.vector.tensor_scalar(stage[:, q, :], core.x[:, 2 * j + q, :], work[:, 0, bass.ds(2 * j + q, 1)],
                                                work[:, 1, bass.ds(2 * j + q, 1)], ALU.subtract, ALU.mult).then_inc(normed, 1)
                    if router:
                        for q in range(2):
                            dve.wait_ge(scored, CREDIT + 2 * j + q + 1)
                            if b_dram is not None:
                                dve.wait_ge(w_loaded, CREDIT + 32)
                                nc.vector.tensor_tensor(logits[:, 2 * j + q, :], psL[q][0:S, 0:E], b_sb[:], ALU.add).then_inc(scores_copied, 1)
                            else:
                                nc.vector.tensor_copy(logits[:, 2 * j + q, :], psL[q][0:S, 0:E]).then_inc(scores_copied, 1)

            @block.gpsimd
            def _(pool):
                step = Steps(pool, pool_steps, CREDIT)
                pool.wait_ge(moments, CREDIT + 6)
                step.then(pool.tensor_scalar(t1, t1, LN_EPS, None, ALU.add))
                pool.tensor_tensor(rstd, t1, core.half[0:S, 0:B], ALU.pow).then_inc(rstd_ready, 1)

            @block.tensor
            def _(pe):
                if router:
                    pe.wait_ge(w_loaded, CREDIT + (32 if b_dram is not None else 16))
                with pe.Fori(0, B // 2) as j:
                    for q in range(2):
                        pe.wait_ge(normed, CREDIT + 2 * j + q + 1)
                        pe.wait_ge(copied, CREDIT + 2 * j)
                        for k in range(KD):
                            last = nc.tensor.transpose(psT[q][:, k * S:(k + 1) * S], stage[:, q, k * P:(k + 1) * P],
                                                       core.ident[0:S, 0:S])
                        last.then_inc(turned_ps, 1)
                    if router:
                        for q in range(2):
                            pe.wait_ge(copied, CREDIT + 2 * j + q + 1)
                            pe.wait_ge(scores_copied, CREDIT + 2 * j)
                            for k in range(KD):
                                last = nc.tensor.matmul(psL[q][0:S, 0:E], turned[:, q, k, :], w_sb[:, k, :],
                                                        start=k == 0, stop=k == KD - 1)
                            last.then_inc(scored, 1)

            @block.scalar
            def _(act):
                with act.Fori(0, B // 2) as j:
                    for q in range(2):
                        act.wait_ge(normed, CREDIT + 2 * j + q + 1)
                        nc.scalar.copy(core.xn[:, 2 * j + q, :], stage[:, q, :]).then_inc(kept, 1)
                    for q in range(2):
                        act.wait_ge(turned_ps, CREDIT + 2 * j + q + 1)
                        if router:
                            act.wait_ge(scored, CREDIT + 2 * j)
                        src = psT[q][:, 0:KD * S].rearrange("p (k s) -> p k s", k=KD)
                        nc.scalar.copy(core.xnT[:, :, bass.ds((2 * j + q) * S, S)], src)
                        nc.scalar.copy(turned[:, q, :, :], src).then_inc(copied, 1)


def attention_phase(core, layer):
    nc, ins = core.nc, core.ins
    pre = f"L{layer}_xattn_"
    DH = 16 if layer == 0 else 64
    W = HEADS * DH
    WC = W // P
    HALVES = max(1, W // 512)
    HW = min(W, 512)
    with Phase(core, f"attn{layer}") as ph:
        wq, wk, wv = (ph.sb(n, [P, KD, W]) for n in ("wq", "wk", "wv"))
        wo = ph.sb("wo", [P, WC, D])
        ctxT = ph.sb("ctxT", [P, KD, KEYS])
        kT = ph.sb("kT", [P, WC, KEYS])
        v = ph.sb("v", [P, 3, W])
        off = ph.sb("off", [S, KEYS])
        masked = ph.sb("masked", [S, 2, KEYS])
        probs = ph.sb("probs", [S, 2, KEYS])
        probsT = ph.sb("probsT", [P, 2, 3, S])
        least = ph.sb("least", [S, HEADS])
        total = ph.sb("total", [S, HEADS])
        inv = ph.sb("inv", [S, HEADS])
        o = ph.sb("o", [S, W])
        oT = ph.sb("oT", [P, WC, S])
        psP = [ph.ps(f"psP{j}") for j in range(2)]
        psS = [ph.ps(f"psS{j}") for j in range(2)]
        psT = [ph.ps(f"psT{j}") for j in range(2)]
        psO = ph.ps("psO", [P, 2, 512])
        loaded, ctx_in, mask_in = ph.sem("loaded"), ph.sem("ctx_in"), ph.sem("mask_in")
        proj_ready, proj_taken = ph.sem("proj_ready"), ph.sem("proj_taken")
        off_ready = ph.sem("off_ready")
        scored, masked_ready, probs_ready = ph.sem("scored"), ph.sem("masked_ready"), ph.sem("probs_ready")
        probs_turned, probsT_ready, head_done = ph.sem("probs_turned"), ph.sem("probsT_ready"), ph.sem("head_done")
        inv_ready, o_ready, o_turned, oT_ready = ph.sem("inv_ready"), ph.sem("o_ready"), ph.sem("o_turned"), ph.sem("oT_ready")
        out_ready, x_steps, cleared, ready = ph.sem("out_ready"), ph.sem("x_steps"), ph.sem("cleared"), ph.sem("ready")
        sync_passed, pool_passed, mask_passed = ph.sem("sync_passed"), ph.sem("pool_passed"), ph.sem("mask_passed")
        const_steps, o_scaled = ph.sem("const_steps"), ph.sem("o_scaled")
        if layer == 0:
            raw_mask = ph.sb("raw_mask", [S, KEYS], U8)
            bq, bk = ph.sb("bq", [P, WC]), ph.sb("bk", [P, WC])
            bv, bo = ph.sb("bv", [S, D]), ph.sb("bo", [S, D])
            qT = ph.sb("qT", [P, 2, WC, S])
            ints_ready = ph.sem("ints_ready")
            row_i = ph.sb("row_i", [P, 1], I32)
            pick = ph.sb("pick", [P, 2])
            bqp = ph.sb("bqp", [P, 2, WC])
            NPROJ = 2 * WC + 3
            consts = 8
        else:
            qT = ph.sb("qT", [P, WC, S])
            raw = ph.sb("raw", [P, 4, W])
            square = ph.sb("square", [P, 2, HW])
            sums = ph.sb("sums", [P, 4, HEADS])
            rms = ph.sb("rms", [P, 4, HEADS])
            lens_i, lens = ph.sb("lens_i", [S, B], I32), ph.sb("lens", [S, B])
            key_i = ph.sb("key_i", [S, KEYS], I32)
            key_no = ph.sb("key_no", [S, KEYS])
            wcol, wk_col = ph.sb("wcol", [P, 1]), ph.sb("wk_col", [P, 1])
            NPROJ = 8 * HALVES - HALVES
            summed, rms_steps, scaled = ph.sem("summed"), ph.sem("rms_steps"), ph.sem("scaled")
            xq_ready, ints_ready = ph.sem("xq_ready"), ph.sem("ints_ready")
            xq = ph.sb("xq", [P, KD, S])
            turned, turned_copied = ph.sem("turned"), ph.sem("turned_copied")
            NTURN = WC + 2
            consts = 9
        XS = 2 if layer == 0 else 1
        ph.credit()

        def head_rows(h):
            if layer == 0:
                c, r = divmod(h, P // DH)
                return c, 32 * (r // 2), 32, r % 2
            return h // 2, 64 * (h % 2), 64, 0

        with nc.Block() as block:
            @block.sync
            def _(sync):
                for w, name in ((wq, "Wq"), (wk, "Wk"), (wv, "Wv")):
                    sync.dma_start(w[:], ins[pre + name].rearrange("(k p) n -> p k n", p=P)).then_inc(loaded, 16)
                sync.dma_start(wo[:], ins[pre + "Wo"].rearrange("(k p) n -> p k n", p=P)).then_inc(loaded, 16)
                if layer == 0:
                    for b, name in ((bq, "bq"), (bk, "bk")):
                        sync.dma_start(b[:], ins[pre + name]).then_inc(loaded, 16)
                    for b, name in ((bv, "bv"), (bo, "bo")):
                        sync.dma_start(b[:], ins[pre + name].partition_broadcast(S)).then_inc(loaded, 16)
                else:
                    for half in range(2):
                        for b, name in ((wcol, "q_norm_w"), (wk_col, "k_norm_w")):
                            sync.dma_start(b[64 * half:64 * half + 64, :],
                                           ins[pre + name].rearrange("(p a) -> p a", a=1)).then_inc(loaded, 16)
                    sync.dma_start(lens_i[:], ins["_lenS2"].partition_broadcast(S)).then_inc(loaded, 16)
                with sync.Fori(0, B) as i:
                    sync.wait_ge(proj_ready, CREDIT + i * NPROJ)
                    sync.sem_inc(sync_passed, 1)
                    sync.dma_start(ctxT[:], ins["ctx_1024"][bass.ds(i, 1)].rearrange("b (k p) n -> p (b k) n", p=P)).then_inc(ctx_in, 16)
                    if layer == 0:
                        sync.wait_ge(off_ready, CREDIT + i)
                        sync.sem_inc(sync_passed, 1)
                        sync.dma_start(raw_mask[:], ins["mask_BxSxS2_bk1"][bass.ds(i, 1)].rearrange("b s n -> (b s) n")).then_inc(mask_in, 16)

            @block.tensor
            def _(pe):
                pe.wait_ge(loaded, CREDIT + 16 * consts)
                pe.wait_ge(cleared, CREDIT + 1)
                with pe.Fori(0, B) as i:
                    made = [0]

                    def proj_bank():
                        j = made[0]
                        pe.wait_ge(proj_taken, CREDIT + i * NPROJ + max(j - 1, 0))
                        made[0] += 1
                        return psP[j % 2]

                    pe.wait_ge(ctx_in, CREDIT + 16 * (i + 1))
                    pe.wait_ge(x_steps, CREDIT + i * XS)
                    if layer == 0:
                        for c in range(WC):
                            ps = proj_bank()
                            for k in range(KD):
                                last = nc.tensor.matmul(ps[:, 0:S], wq[:, k, c * P:(c + 1) * P],
                                                        core.xnT[:, k, bass.ds(i * S, S)], start=k == 0, stop=k == KD - 1)
                            last.then_inc(proj_ready, 1)
                        for c in range(WC):
                            ps = proj_bank()
                            for k in range(KD):
                                last = nc.tensor.matmul(ps[:, 0:KEYS], wk[:, k, c * P:(c + 1) * P], ctxT[:, k, :],
                                                        start=k == 0, stop=k == KD - 1)
                            last.then_inc(proj_ready, 1)
                    else:
                        pe.wait_ge(xq_ready, CREDIT + i + 1)
                        for a in range(HALVES):
                            ps = proj_bank()
                            for k in range(KD):
                                last = nc.tensor.matmul(ps[0:S, :], xq[:, k, :], wq[:, k, a * HW:(a + 1) * HW],
                                                        start=k == 0, stop=k == KD - 1)
                            last.then_inc(proj_ready, 1)
                        for t, (k0, n) in enumerate(KEY_TILES):
                            for a in range(HALVES):
                                ps = proj_bank()
                                for k in range(KD):
                                    last = nc.tensor.matmul(ps[0:n, :], ctxT[:, k, k0:k0 + n], wk[:, k, a * HW:(a + 1) * HW],
                                                            start=k == 0, stop=k == KD - 1)
                                last.then_inc(proj_ready, 1)
                    for t, (k0, n) in enumerate(KEY_TILES):
                        for a in range(HALVES):
                            ps = proj_bank()
                            for k in range(KD):
                                last = nc.tensor.matmul(ps[0:n, 0:HW], ctxT[:, k, k0:k0 + n], wv[:, k, a * HW:(a + 1) * HW],
                                                        start=k == 0, stop=k == KD - 1)
                            last.then_inc(proj_ready, 1)
                    assert made[0] == NPROJ
                    if layer == 1:
                        pe.wait_ge(proj_taken, CREDIT + (i + 1) * NPROJ)
                        pe.wait_ge(scaled, CREDIT + i * 4 + 4)
                        for j in range(NTURN):
                            pe.wait_ge(turned_copied, CREDIT + i * NTURN + max(j - 1, 0))
                            if j < WC:
                                for t, (k0, n) in enumerate(KEY_TILES):
                                    last = nc.tensor.transpose(psP[j % 2][:, k0:k0 + n], raw[0:n, t, j * P:(j + 1) * P],
                                                               core.ident[0:n, 0:n])
                            else:
                                for q in range(4):
                                    c = 4 * (j - WC) + q
                                    last = nc.tensor.transpose(psP[j % 2][:, q * S:(q + 1) * S], raw[0:S, 3, c * P:(c + 1) * P],
                                                               core.ident[0:S, 0:S])
                            last.then_inc(turned, 1)
                        pe.wait_ge(turned_copied, CREDIT + (i + 1) * NTURN)
                    else:
                        pe.wait_ge(proj_taken, CREDIT + (i + 1) * NPROJ)

                    def scores(h):
                        c, r, n, copy = head_rows(h)
                        q = qT[r:r + n, copy, c, :] if layer == 0 else qT[r:r + n, c, :]
                        pe.wait_ge(masked_ready, CREDIT + i * HEADS + max(h - 1, 0))
                        nc.tensor.matmul(psS[h % 2][0:S, 0:KEYS], q, kT[r:r + n, c, :], start=True, stop=True).then_inc(scored, 1)

                    def turn(h):
                        pe.wait_ge(probs_ready, CREDIT + i * HEADS + h + 1)
                        pe.wait_ge(probsT_ready, CREDIT + i * HEADS + max(h - 1, 0))
                        for t, (k0, n) in enumerate(KEY_TILES):
                            last = nc.tensor.transpose(psT[h % 2][0:n, t * S:(t + 1) * S], probs[:, h % 2, k0:k0 + n],
                                                       core.ident[0:S, 0:S])
                        last.then_inc(probs_turned, 1)

                    def values(h):
                        pe.wait_ge(probsT_ready, CREDIT + i * HEADS + h + 1)
                        a, col = divmod(h * DH, 512)
                        for t, (k0, n) in enumerate(KEY_TILES):
                            last = nc.tensor.matmul(psO[0:S, a, col:col + DH], probsT[0:n, h % 2, t, :],
                                                    v[0:n, t, h * DH:(h + 1) * DH], start=t == 0, stop=t == 2)
                        last.then_inc(head_done, 1)

                    pe.wait_ge(o_ready, CREDIT + i * HALVES)
                    scores(0)
                    for h in range(HEADS + 1):
                        if h + 1 < HEADS:
                            scores(h + 1)
                        if h < HEADS:
                            turn(h)
                        if h >= 1:
                            values(h - 1)
                    pe.wait_ge(o_ready, CREDIT + (i + 1) * HALVES)
                    for a in range(HALVES):
                        for c in range(4 * a, min(4 * a + 4, WC)):
                            last = nc.tensor.transpose(psP[a][:, (c % 4) * S:(c % 4 + 1) * S], o[:, c * P:(c + 1) * P],
                                                       core.ident[0:S, 0:S])
                        last.then_inc(o_turned, 1)
                    pe.wait_ge(oT_ready, CREDIT + (i + 1) * HALVES)
                    for c in range(WC):
                        last = nc.tensor.matmul(psP[0][0:S, 0:D], oT[:, c, :], wo[:, c, :], start=c == 0, stop=c == WC - 1)
                    last.then_inc(out_ready, 1)

            @block.scalar
            def _(act):
                act.wait_ge(ready, CREDIT + 1)
                with act.Fori(0, B) as i:
                    j = 0

                    def take(out, in_, **kw):
                        nonlocal j
                        act.wait_ge(proj_ready, CREDIT + i * NPROJ + j + 1)
                        j += 1
                        return nc.scalar.activation(out, in_, ACT.Identity, **kw)

                    if layer == 0:
                        act.wait_ge(head_done, CREDIT + i * HEADS)
                        for c in range(WC):
                            take(qT[:, 0, c, :], psP[c % 2][:, 0:S], scale=pick[:, 0:1], bias=bqp[:, 0, c:c + 1])
                            nc.scalar.activation(qT[:, 1, c, :], psP[c % 2][:, 0:S], ACT.Identity, scale=pick[:, 1:2],
                                                 bias=bqp[:, 1, c:c + 1]).then_inc(proj_taken, 1)
                        for c in range(WC):
                            take(kT[:, c, :], psP[j % 2][:, 0:KEYS], bias=bk[:, c:c + 1]).then_inc(proj_taken, 1)
                    else:
                        act.wait_ge(proj_ready, CREDIT + i * NPROJ)
                        nc.scalar.copy(xq[:], core.xnT[:, :, bass.ds(i * S, S)]).then_inc(xq_ready, 1)
                        act.wait_ge(turned, CREDIT + i * NTURN)
                        for t in (3, 0, 1, 2):
                            n = S if t == 3 else KEY_TILES[t][1]
                            for a in range(HALVES):
                                bank = psP[j % 2][0:n, :]
                                act.wait_ge(summed, CREDIT + i * 4 * HALVES + max(j - 1, 0))
                                take(raw[0:n, t, a * HW:(a + 1) * HW], bank)
                                nc.scalar.activation(square[0:n, a, :], bank, ACT.Square).then_inc(proj_taken, 1)
                        act.wait_ge(head_done, CREDIT + i * HEADS)
                    for t, (k0, n) in enumerate(KEY_TILES):
                        for a in range(HALVES):
                            take(v[0:n, t, a * HW:(a + 1) * HW], psP[j % 2][0:n, 0:HW]).then_inc(proj_taken, 1)
                    assert j == NPROJ
                    for h in range(HEADS):
                        act.wait_ge(masked_ready, CREDIT + i * HEADS + h + 1)
                        act.wait_ge(probs_turned, CREDIT + i * HEADS + max(h - 1, 0))
                        nc.scalar.activation(probs[:, h % 2, :], masked[:, h % 2, :], ACT.Exp, bias=least[:, h:h + 1],
                                             scale=-1.0, accum_out=total[:, h:h + 1]).then_inc(probs_ready, 1)

            @block.gpsimd
            def _(pool):
                if layer == 0:
                    pool.iota(row_i[:], [[0, 1]], base=0, channel_multiplier=1).then_inc(ints_ready, 1)
                else:
                    pool.iota(key_i[:], [[1, KEYS]], base=0, channel_multiplier=0).then_inc(ints_ready, 1)
                    with pool.Fori(0, B) as i:
                        step = Steps(pool, rms_steps, CREDIT + i * 8)
                        for n, t in enumerate((3, 0, 1, 2)):
                            rows = S if t == 3 else KEY_TILES[t][1]
                            pool.wait_ge(summed, CREDIT + (i * 4 + n + 1) * HALVES)
                            pool.sem_inc(pool_passed, 1)
                            step.then(pool.tensor_scalar(rms[0:rows, t, :], sums[0:rows, t, :], 1.0 / DH, RMS_EPS, ALU.mult, ALU.add))
                            step.then(pool.tensor_tensor(rms[0:rows, t, :], rms[0:rows, t, :], core.half[0:rows, 0:HEADS], ALU.pow))

            @block.vector
            def _(dve):
                gate = core.gates[0:S, layer:layer + 1]
                dve.wait_ge(loaded, CREDIT + 16 * consts)
                dve.wait_ge(ints_ready, CREDIT + 1)
                step = Steps(dve, const_steps, CREDIT)
                if layer == 0:
                    step.then(nc.vector.tensor_scalar(row_i[:], row_i[:], 4, 1, ALU.logical_shift_right, ALU.bitwise_and))
                    step.then(nc.vector.tensor_copy(pick[:, 1:2], row_i[:]))
                    step.then(nc.vector.tensor_scalar(pick[:, 0:1], pick[:, 1:2], DH ** -0.5, -DH ** -0.5, ALU.mult, ALU.add))
                    step.then(nc.vector.tensor_scalar(pick[:, 1:2], pick[:, 1:2], -DH ** -0.5, None, ALU.mult))
                    for j in range(2):
                        step.then(nc.vector.tensor_scalar(bqp[:, j, :], bq[:], pick[:, j:j + 1], None, ALU.mult))
                    step.then(nc.vector.tensor_scalar(bo[:], bo[:], gate, None, ALU.mult))
                else:
                    step.then(nc.vector.scalar_tensor_tensor(wcol[:], wcol[:], -DH ** -0.5, wk_col[:], ALU.mult, ALU.mult))
                    step.then(nc.vector.tensor_copy(lens[:], lens_i[:]))
                    step.then(nc.vector.tensor_copy(key_no[:], key_i[:]))
                for j in range(2):
                    step.then(nc.vector.memset(psT[j][:], 0.0))
                dve.sem_inc(ready, 1)
                dve.sem_inc(cleared, 1)
                with dve.Fori(0, B) as i:
                    if layer == 0:
                        dve.wait_ge(mask_in, CREDIT + 16 * (i + 1))
                        nc.vector.tensor_scalar(off[:], raw_mask[:], MASKED, None, ALU.mult).then_inc(off_ready, 1)
                    else:
                        nc.vector.tensor_scalar(off[:], key_no[:], lens[:, bass.ds(i, 1)], MASKED, ALU.is_ge, ALU.mult).then_inc(off_ready, 1)
                        order = (3, 0, 1, 2)
                        for j, t in enumerate(order):
                            rows = S if t == 3 else KEY_TILES[t][1]
                            for a in range(HALVES):
                                dve.wait_ge(proj_taken, CREDIT + i * NPROJ + j * HALVES + a + 1)
                                nc.vector.tensor_reduce(sums[0:rows, t, a * 8:(a + 1) * 8],
                                                        square[0:rows, a, :].rearrange("p (h d) -> p h d", d=DH),
                                                        AX.X, ALU.add).then_inc(summed, 1)
                        for j, t in enumerate(order):
                            rows = S if t == 3 else KEY_TILES[t][1]
                            dve.wait_ge(rms_steps, CREDIT + i * 8 + 2 * (j + 1))
                            nc.vector.tensor_tensor(raw[0:rows, t, :].rearrange("p (h d) -> p h d", d=DH),
                                                    raw[0:rows, t, :].rearrange("p (h d) -> p h d", d=DH),
                                                    bcast(rms[0:rows, t, :], DH), ALU.mult).then_inc(scaled, 1)
                        dve.wait_ge(head_done, CREDIT + i * HEADS)
                        for j in range(NTURN):
                            dve.wait_ge(turned, CREDIT + i * NTURN + j + 1)
                            if j < WC:
                                nc.vector.tensor_copy(kT[:, j, :], psP[j % 2][:, 0:KEYS]).then_inc(turned_copied, 1)
                            else:
                                c = 4 * (j - WC)
                                nc.vector.tensor_scalar(qT[:, c:c + 4, :], psP[j % 2][:, 0:4 * S].rearrange("p (c s) -> p c s", c=4),
                                                        wcol[:], None, ALU.mult).then_inc(turned_copied, 1)

                    def mask(h):
                        dve.wait_ge(scored, CREDIT + i * HEADS + h + 1)
                        if h == 0:
                            dve.wait_ge(off_ready, CREDIT + i + 1)
                        dve.wait_ge(probs_ready, CREDIT + i * HEADS + max(h - 1, 0))
                        dve.sem_inc(mask_passed, 1)
                        nc.vector.tensor_tensor_reduce(masked[:, h % 2, :], psS[h % 2][0:S, 0:KEYS], off[:], 1.0, 3e38,
                                                       ALU.add, ALU.min, least[:, h:h + 1]).then_inc(masked_ready, 1)

                    def copy_probs(h):
                        dve.wait_ge(probs_turned, CREDIT + i * HEADS + h + 1)
                        dve.wait_ge(head_done, CREDIT + i * HEADS + max(h - 1, 0))
                        nc.vector.tensor_copy(probsT[:, h % 2, :, :],
                                              psT[h % 2][:, 0:3 * S].rearrange("p (t s) -> p t s", t=3)).then_inc(probsT_ready, 1)

                    mask(0)
                    for h in range(HEADS):
                        if h + 1 < HEADS:
                            mask(h + 1)
                        copy_probs(h)
                    dve.wait_ge(probs_ready, CREDIT + (i + 1) * HEADS)
                    nc.vector.reciprocal(inv[:], total[:]).then_inc(inv_ready, 1)
                    dve.wait_ge(inv_ready, CREDIT + i + 1)
                    dve.wait_ge(head_done, CREDIT + (i + 1) * HEADS)
                    dve.wait_ge(o_turned, CREDIT + i * HALVES)
                    for a in range(HALVES):
                        nh = HW // DH
                        ins_ = nc.vector.tensor_tensor(o[:, a * HW:(a + 1) * HW].rearrange("p (h d) -> p h d", d=DH),
                                                       psO[0:S, a, 0:HW].rearrange("p (h d) -> p h d", d=DH),
                                                       bcast(inv[:, a * nh:(a + 1) * nh], DH), ALU.mult)
                        if layer == 0:
                            ins_.then_inc(o_scaled, 1)
                            dve.wait_ge(o_scaled, CREDIT + i + 1)
                            nc.vector.tensor_tensor(o[:], o[:], bv[:], ALU.add).then_inc(o_ready, 1)
                        else:
                            ins_.then_inc(o_ready, 1)
                    for a in range(HALVES):
                        dve.wait_ge(o_turned, CREDIT + i * HALVES + a + 1)
                        n = min(4, WC)
                        nc.vector.tensor_copy(oT[:, 4 * a:4 * a + n, :],
                                              psP[a][:, 0:n * S].rearrange("p (c s) -> p c s", c=n)).then_inc(oT_ready, 1)
                    dve.wait_ge(out_ready, CREDIT + i + 1)
                    row = core.x[:, bass.ds(i, 1), :].rearrange("p a d -> p (a d)")
                    nc.vector.scalar_tensor_tensor(row, psP[0][0:S, 0:D], gate, row, ALU.mult, ALU.add).then_inc(x_steps, 1)
                    if layer == 0:
                        dve.wait_ge(x_steps, CREDIT + i * XS + 1)
                        nc.vector.tensor_tensor(row, row, bo[:], ALU.add).then_inc(x_steps, 1)



def slot_shape(layer):
    return (HALF0, 2 * E0) if layer == 0 else (P, NBLK1 * BLK1 // P)


def route_phase(core, layer, logits, weights, slots, place, blocks=None):
    nc, ins = core.nc, core.ins
    E = E0 if layer == 0 else E1
    with Phase(core, f"route{layer}") as ph:
        sc, hot1, hot2, work = (ph.sb(n, [S, B, E]) for n in ("sc", "hot1", "hot2", "work"))
        rev, rev_i = ph.sb("rev", [P, E]), ph.sb("rev_i", [P, E], I32)
        top = ph.sb("top", [S, 8, B])
        m1, m2, r1, r2, t0, t1, t2, t3 = (top[:, k, :] for k in range(8))
        steps, ints, exped, asked_exp, loaded = (ph.sem(n) for n in ("steps", "ints", "exped", "asked_exp", "loaded"))
        counted, to_count = ph.sem("counted"), ph.sem("to_count")
        gate_b = ph.sb("gate_b", [S, E])
        if layer == 0:
            trash_i, trash = ph.sb("trash_i", [P, 1], I32), ph.sb("trash", [P, 1])
            turned = ph.sb("turned", [P, 3, 2, S])
            wT = ph.sb("wT", [E0, N])
            hotT = ph.sb("hotT", [E0, 2, N])
            stage = ph.sb("stage", [E0, 2, S])
            before = ph.sb("before", [S, 2 * N])
            above = ph.sb("above", [S, 2, 4, 400], BF16)
            rank = ph.sb("rank", [S, 2, B])
            staged, selected, ranked, before_ready = (ph.sem(n) for n in ("staged", "selected", "ranked", "before_ready"))
            out_turned, bounced, back, blank = (ph.sem(n) for n in ("out_turned", "bounced", "back", "blank"))
        else:
            part_i = ph.sb("part_i", [S, B], I32)
            tot = ph.sb("tot", [P, 3, B, E1])
            cnt = ph.sb("cnt", [P, 6, E1])
            jrow_i, jrow = ph.sb("jrow_i", [P, NBLK1], I32), ph.sb("jrow", [P, NBLK1])
            cmp = ph.sb("cmp", [P, NBLK1, E1])
            be = ph.sb("be", [P, 2, NBLK1])
            row_i, row = ph.sb("row_i", [P, 1], I32), ph.sb("row", [P, 1])
        carried = []
        with ExitStack() as first:
            psA, psB = (first.enter_context(nc.psum_tensor(f"route{layer}_{n}", [P, 512], F32)) for n in ("psA", "psB"))
            with nc.Block() as block:
                @block.sync
                def _(sync):
                    if layer == 0:
                        sync.dma_start(gate_b[:], ins["L0_ffn_gate_b"].partition_broadcast(S)).then_inc(loaded, 16)
                        sync.wait_ge(out_turned, 2)
                        for q in range(3):
                            for h in range(2):
                                sync.dma_start(core.bounce[q, h], turned[:, q, h, :]).then_inc(bounced, 16)
                        sync.wait_ge(bounced, 96)
                        back_view = core.bounce.rearrange("q h (t e) m -> q e (h t) m", e=E0)
                        sync.dma_start(wT[:].rearrange("e (t m) -> e t m", m=S), back_view[0]).then_inc(back, 16)
                        for k in range(2):
                            sync.dma_start(hotT[:, k, :].rearrange("e (t m) -> e t m", m=S), back_view[1 + k]).then_inc(back, 16)
                        sync.wait_ge(back, 48)

                @block.gpsimd
                def _(pool):
                    pool.iota(rev_i[:], [[-1, E]], base=E, channel_multiplier=0).then_inc(ints, 1)
                    if layer == 0:
                        pool.iota(trash_i[:], [[0, 1]], base=E0 * CAP0, channel_multiplier=1).then_inc(ints, 1)
                        pool.memset(before[:], 0.0).then_inc(blank, 1)
                        pool.wait_ge(blank, 1)
                        pool.affine_select(out=before[:], in_=before[:], compare_op=ALU.is_ge, fill=-1e-38,
                                           base=-N, pattern=[[1, 2 * N]], channel_multiplier=-1).then_inc(before_ready, 1)
                    else:
                        pool.iota(jrow_i[:], [[1, NBLK1]], base=0, channel_multiplier=0).then_inc(ints, 1)
                        pool.iota(row_i[:], [[0, 1]], base=0, channel_multiplier=1).then_inc(ints, 1)

                @block.scalar
                def _(act):
                    act.wait_ge(asked_exp, 1)
                    if layer == 0:
                        nc.scalar.activation(sc[:], work[:], ACT.Exp).then_inc(exped, 1)
                        act.wait_ge(counted, 1)
                        for q in range(3):
                            ps = (psA, psB)[q // 2]
                            ins_ = nc.scalar.copy(turned[:, q, :, :], ps[:, (q % 2) * 2 * S:(q % 2 + 1) * 2 * S].rearrange("p (h s) -> p h s", h=2))
                            if q:
                                ins_.then_inc(out_turned, 1)
                    else:
                        nc.scalar.activation(t1, t0, ACT.Exp).then_inc(exped, 1)

                @block.tensor
                def _(pe):
                    pe.wait_ge(to_count, 1)
                    if layer == 0:
                        for q, src in enumerate((work, hot1, hot2)):
                            for h in range(2):
                                a = ((q % 2) * 2 + h) * S
                                last = nc.tensor.transpose((psA, psB)[q // 2][:, a:a + S],
                                                           src[:, 8 * h:8 * h + 8, :].rearrange("p t e -> p (t e)"), core.ident[0:S, 0:S])
                    else:
                        a = work[:].rearrange("p t e -> p (t e)")
                        nc.tensor.matmul(psA[0:S, 0:B * E1], core.tri[0:S, 0:S], a, start=True, stop=True)
                        last = nc.tensor.matmul(psB[:, 0:B * E1], core.ones[0:S, :], a, start=True, stop=True)
                    last.then_inc(counted, 1)

                @block.vector
                def _(dve):
                    v = nc.vector
                    step = Steps(dve, steps)
                    carried.append(step)
                    dve.wait_ge(ints, 2 if layer == 0 else 3)
                    step.then(v.tensor_copy(rev[:], rev_i[:]))
                    if layer == 0:
                        step.then(v.tensor_copy(trash[:], trash_i[:]))
                        step.then(v.tensor_reduce(m1, logits, AX.X, ALU.max))
                        v.tensor_tensor(work[:], logits, bcast(m1, E), ALU.subtract).then_inc(asked_exp, 1)
                        dve.wait_ge(exped, 1)
                        step.then(v.tensor_reduce(t0, sc[:], AX.X, ALU.add))
                        step.then(v.reciprocal(t0, t0))
                        step.then(v.tensor_tensor(sc[:], sc[:], bcast(t0, E), ALU.mult))
                        dve.wait_ge(loaded, 16)
                        step.then(v.tensor_tensor(sc[:], sc[:], spread(gate_b[:], B), ALU.add))
                    else:
                        step.then(v.tensor_copy(jrow[:], jrow_i[:]))
                        step.then(v.tensor_copy(row[:], row_i[:]))
                        step.then(v.tensor_copy(sc[:], logits))
                    for m, r, hot in ((m1, r1, hot1), (m2, r2, hot2)):
                        step.then(v.tensor_reduce(m, sc[:], AX.X, ALU.max))
                        step.then(v.tensor_tensor(work[:], sc[:], bcast(m, E), ALU.is_equal))
                        step.then(v.tensor_tensor(work[:], work[:], spread(rev[0:S, :], B), ALU.mult))
                        step.then(v.tensor_reduce(r, work[:], AX.X, ALU.max))
                        step.then(v.tensor_tensor(hot[:], spread(rev[0:S, :], B), bcast(r, E), ALU.is_equal))
                        step.then(v.scalar_tensor_tensor(sc[:], hot[:], -BIG, sc[:], ALU.mult, ALU.add))
                    if layer == 0:
                        for k, hot in enumerate((hot1, hot2)):
                            step.then(v.tensor_tensor(work[:], hot[:], logits, ALU.mult))
                            step.then(v.tensor_reduce(weights[:, k, :], work[:], AX.X, ALU.add))
                        step.then(v.tensor_tensor(sc[:], hot1[:], hot2[:], ALU.add))
                        step.then(v.tensor_tensor(work[:], sc[:], logits, ALU.mult))
                        step.then(v.tensor_scalar(sc[:], sc[:], -1.0, BIG, ALU.add, ALU.mult))
                        v.tensor_tensor(work[:], work[:], sc[:], ALU.add).then_inc(to_count, 1)
                    else:
                        v.tensor_tensor(t0, m2, m1, ALU.subtract).then_inc(asked_exp, 1)
                        dve.wait_ge(exped, 1)
                        step.then(v.tensor_scalar(t2, t1, 1.0, None, ALU.add))
                        step.then(v.reciprocal(weights[:, 0, :], t2))
                        step.then(v.tensor_tensor(weights[:, 1, :], t1, weights[:, 0, :], ALU.mult))
                        v.tensor_tensor(work[:], hot1[:], hot2[:], ALU.add).then_inc(to_count, 1)
                        dve.wait_ge(counted, 1)
                        each = psB[:, 0:B * E1].rearrange("p (t e) -> p t e", e=E1)
                        inside = psA[0:S, 0:B * E1].rearrange("p (t e) -> p t e", e=E1)
                        step.then(v.tensor_copy(tot[:, 0], each))
                        a, b = 0, 1
                        for sh in (1, 2, 4, 8):
                            step.then(v.tensor_copy(tot[:, b, 0:sh], tot[:, a, 0:sh]))
                            step.then(v.tensor_tensor(tot[:, b, sh:], tot[:, a, sh:], tot[:, a, 0:B - sh], ALU.add))
                            a, b = b, a
                        count, nb, c0, c1, start, base = (cnt[:, k, :] for k in range(6))
                        step.then(v.tensor_copy(count, tot[:, a, B - 1]))
                        step.then(v.tensor_tensor(tot[:, 2], tot[:, a], each, ALU.subtract))
                        step.then(v.tensor_scalar(nb, count, 0.0, None, ALU.is_gt))
                        for j in range(1, MAXB1):
                            step.then(v.scalar_tensor_tensor(nb, count, float(BLK1 * j), nb, ALU.is_gt, ALU.add))
                        step.then(v.tensor_copy(c0, nb))
                        for sh in (1, 2, 4):
                            step.then(v.tensor_copy(c1[:, 0:sh], c0[:, 0:sh]))
                            step.then(v.tensor_tensor(c1[:, sh:], c0[:, sh:], c0[:, 0:E1 - sh], ALU.add))
                            c0, c1 = c1, c0
                        step.then(v.tensor_tensor(start, c0, nb, ALU.subtract))
                        step.then(v.tensor_scalar(base, start, float(BLK1), None, ALU.mult))
                        step.then(v.tensor_tensor(work[:], tot[0:S, 2], inside, ALU.add))
                        step.then(v.tensor_tensor(work[:], work[:], spread(base[0:S, :], B), ALU.add))
                        for k, hot in enumerate((hot1, hot2)):
                            step.then(v.tensor_tensor(sc[:], hot[:], work[:], ALU.mult))
                            step.then(v.tensor_reduce(t3, sc[:], AX.X, ALU.add))
                            step.then(v.tensor_copy(slots[:, k, :], t3))
                            for j, (op, by) in enumerate(((ALU.bitwise_and, P - 1), (ALU.logical_shift_right, 7))):
                                step.then(v.tensor_scalar(part_i[:], slots[:, k, :], by, None, op))
                                step.then(v.tensor_copy(place[:, j, k, :], part_i[:]))
                        step.then(v.tensor_tensor(cmp[:], bcast(jrow[:], E1), spread(c0, NBLK1), ALU.is_ge))
                        step.then(v.tensor_reduce(be[:, 0, :], cmp[:], AX.X, ALU.add))
                        step.then(v.tensor_scalar(be[:, 0, :], be[:, 0, :], float(E1 - 1), None, ALU.min))
                        step.then(v.tensor_scalar(be[:, 1, :], be[:, 0, :], float(P), row[:, 0:1], ALU.mult, ALU.add))
                        step.then(v.tensor_copy(blocks[:, 0, :], be[:, 1, :]))
                        step.then(v.tensor_copy(blocks[:, 1, :], be[:, 0, :]))
        if layer == 1:
            return

        psW = [ph.ps(f"psW{k}", [P, 4, 512]) for k in range(2)]
        ph.credit((staged, selected, ranked))
        with nc.Block() as block:
            @block.scalar
            def _(act):
                with act.Fori(0, B) as t:
                    act.wait_ge(selected, CREDIT + 2 * t)
                    nc.scalar.copy(stage[:], hotT[:, :, bass.ds(t * S, S)]).then_inc(staged, 1)

            @block.tensor
            def _(pe):
                with pe.Fori(0, B) as t:
                    pe.wait_ge(staged, CREDIT + t + 1)
                    for k in range(2):
                        pe.wait_ge(ranked, CREDIT + 2 * t)
                        for a in range(4):
                            last = nc.tensor.matmul(psW[k][0:S, a, 0:400], stage[:, k, :], wT[:, 400 * a:400 * a + 400],
                                                    start=True, stop=True)
                        last.then_inc(selected, 1)

            @block.vector
            def _(dve):
                v = nc.vector
                with dve.Fori(0, B) as t:
                    for k in range(2):
                        dve.wait_ge(ranked, CREDIT + 2 * t)
                        dve.wait_ge(selected, CREDIT + 2 * t + k + 1)
                        v.scalar_tensor_tensor(above[:, k], psW[k][0:S, :, 0:400], weights[:, k, bass.ds(t, 1)],
                                               before[:, bass.ds(N - t * S, N)].rearrange("p (a m) -> p a m", a=4),
                                               ALU.subtract, ALU.is_gt, accum_out=rank[:, k, bass.ds(t, 1)]).then_inc(ranked, 1)
                dve.wait_ge(ranked, CREDIT + 2 * B)
                step = Steps(dve, steps, carried[0].n)
                for k, r in enumerate((r1, r2)):
                    step.then(v.tensor_scalar(t1, rank[:, k, :], float(HALF0), None, ALU.is_ge))
                    step.then(v.scalar_tensor_tensor(place[:, 0, k, :], t1, -float(HALF0), rank[:, k, :], ALU.mult, ALU.add))
                    step.then(v.scalar_tensor_tensor(t2, r, -2.0, t1, ALU.mult, ALU.add))
                    step.then(v.tensor_scalar(t3, rank[:, k, :], float(CAP0), 2.0 * E0, ALU.is_ge, ALU.mult))
                    step.then(v.scalar_tensor_tensor(place[:, 1, k, :], t2, 2.0 * E0, t3, ALU.add, ALU.add))
                    step.then(v.tensor_scalar(t0, r, -float(CAP0), float(E0 * CAP0), ALU.mult, ALU.add))
                    step.then(v.tensor_tensor(t0, t0, rank[:, k, :], ALU.add))
                    step.then(v.tensor_scalar(t1, rank[:, k, :], float(CAP0), None, ALU.is_lt))
                    step.then(v.tensor_scalar(t0, t0, trash[0:S, :], None, ALU.subtract))
                    step.then(v.tensor_tensor(t0, t0, t1, ALU.mult))
                    step.then(v.tensor_scalar(t0, t0, trash[0:S, :], None, ALU.add))
                    step.then(v.tensor_copy(slots[:, k, :], t0))
                    step.then(v.tensor_tensor(weights[:, k, :], weights[:, k, :], t1, ALU.mult))


def invert_phase(core, layer, place, tokens):
    nc = core.nc
    LO, HI = slot_shape(layer)
    with Phase(core, f"invert{layer}") as ph:
        lo_i, lo_row = ph.sb("lo_i", [S, P], I32), ph.sb("lo_row", [S, P])
        id_i, ids = ph.sb("id_i", [S, B], I32), ph.sb("ids", [S, B])
        hot_lo, hot_hi = ph.sb("hot_lo", [S, 2 * B, LO]), ph.sb("hot_hi", [S, 2 * B, HI])
        psI = ph.ps("psI")
        ints, steps, hot_ready, found, stored = (ph.sem(n) for n in ("ints", "steps", "hot_ready", "found", "stored"))
        with nc.Block() as block:
            @block.sync
            def _(sync):
                sync.dma_start(core.rows.rearrange("(b s) d -> s b d", s=S), core.xn[:]).then_inc(stored, 16)
                sync.wait_ge(stored, 16)

            @block.gpsimd
            def _(pool):
                pool.iota(lo_i[:], [[1, P]], base=0, channel_multiplier=0).then_inc(ints, 1)
                pool.iota(id_i[:], [[S, B]], base=0, channel_multiplier=1).then_inc(ints, 1)

            @block.vector
            def _(dve):
                v = nc.vector
                step = Steps(dve, steps)
                dve.wait_ge(ints, 2)
                step.then(v.tensor_copy(lo_row[:], lo_i[:]))
                step.then(v.tensor_copy(ids[:], id_i[:]))
                lo, hi = (place[:, j].rearrange("p k t -> p (k t)") for j in range(2))
                v.tensor_tensor(hot_lo[:], spread(lo_row[:, 0:LO], 2 * B), bcast(lo, LO), ALU.is_equal).then_inc(hot_ready, 1)
                step.then(v.tensor_tensor(hot_hi[:], spread(lo_row[:, 0:HI], 2 * B), bcast(hi, HI), ALU.is_equal))
                for k in range(2):
                    h = hot_hi[:, k * B:(k + 1) * B, :]
                    v.tensor_tensor(h, h, bcast(ids[:], HI), ALU.mult).then_inc(hot_ready, 1)
                dve.wait_ge(found, 1)
                step.then(v.tensor_copy(tokens[0:LO, 0:HI], psI[0:LO, 0:HI]))

            @block.tensor
            def _(pe):
                pe.wait_ge(hot_ready, 3)
                for j in range(2 * B):
                    last = nc.tensor.matmul(psI[0:LO, 0:HI], hot_lo[:, j, :], hot_hi[:, j, :], start=j == 0, stop=j == 2 * B - 1)
                last.then_inc(found, 1)


def shared_phase(core, acc):
    nc, ins = core.nc, core.ins
    FC, Q = FF0 // P, 4
    NH = 2 * FC
    with Phase(core, "shared") as ph:
        w1, w3 = (ph.sb(n, [P, SHARED, KD, FF0]) for n in ("w1", "w3"))
        w2 = ph.sb("w2", [P, SHARED, FC, D])
        act1 = ph.sb("act1", [P, 2, Q * S])
        hid = ph.sb("hid", [P, NH, Q * S])
        ps1, ps3, psY = ([ph.ps(f"{n}{j}") for j in range(2)] for n in ("ps1", "ps3", "psY"))
        loaded, both, silu, hidden, y_ready, y_taken = (ph.sem(n) for n in ("loaded", "both", "silu", "hidden", "y_ready", "y_taken"))
        ph.credit()
        with nc.Block() as block:
            @block.sync
            def _(sync):
                for s in range(SHARED):
                    sync.dma_start(w1[:, s], ins["L0_ffn_sw1"][s].rearrange("(k p) f -> p k f", p=P)).then_inc(loaded, 16)
                    sync.dma_start(w3[:, s], ins["L0_ffn_sw3"][s].rearrange("(k p) f -> p k f", p=P)).then_inc(loaded, 16)
                    sync.dma_start(w2[:, s], ins["L0_ffn_sw2"][s].rearrange("(k p) f -> p k f", p=P)).then_inc(loaded, 16)

            @block.tensor
            def _(pe):
                pe.wait_ge(loaded, CREDIT + 16 * 3 * SHARED)
                with pe.Fori(0, B // Q) as i:
                    for j in range(NH):
                        s, f = divmod(j, FC)
                        pe.wait_ge(hidden, CREDIT + i * NH + max(j - 1, 0))
                        for w, ps in ((w1, ps1), (w3, ps3)):
                            for k in range(KD):
                                last = nc.tensor.matmul(ps[j % 2][:, 0:Q * S], w[:, s, k, f * P:(f + 1) * P],
                                                        core.xnT[:, k, bass.ds(i * Q * S, Q * S)], start=k == 0, stop=k == KD - 1)
                        last.then_inc(both, 1)
                    pe.wait_ge(hidden, CREDIT + (i + 1) * NH)
                    for q in range(Q):
                        pe.wait_ge(y_taken, CREDIT + i * Q + max(q - 1, 0))
                        for j in range(NH):
                            s, f = divmod(j, FC)
                            last = nc.tensor.matmul(psY[q % 2][0:S, 0:D], hid[:, j, q * S:(q + 1) * S], w2[:, s, f, :],
                                                    start=j == 0, stop=j == NH - 1)
                        last.then_inc(y_ready, 1)

            @block.scalar
            def _(act):
                with act.Fori(0, B // Q) as i:
                    for j in range(NH):
                        act.wait_ge(both, CREDIT + i * NH + j + 1)
                        act.wait_ge(hidden, CREDIT + i * NH + max(j - 1, 0))
                        nc.scalar.activation(act1[:, j % 2, :], ps1[j % 2][:, 0:Q * S], ACT.Silu).then_inc(silu, 1)

            @block.vector
            def _(dve):
                with dve.Fori(0, B // Q) as i:
                    dve.wait_ge(y_ready, CREDIT + i * Q)
                    for j in range(NH):
                        dve.wait_ge(silu, CREDIT + i * NH + j + 1)
                        nc.vector.tensor_tensor(hid[:, j, :], ps3[j % 2][:, 0:Q * S], act1[:, j % 2, :], ALU.mult).then_inc(hidden, 1)
                    for q in range(Q):
                        dve.wait_ge(y_ready, CREDIT + i * Q + q + 1)
                        nc.vector.tensor_scalar(acc[:, bass.ds(i * Q + q, 1), :].rearrange("p a d -> p (a d)"), psY[q % 2][0:S, 0:D],
                                                1.0 / SHARED, None, ALU.mult).then_inc(y_taken, 1)


def experts_phase(core, layer, tokens, blocks=None):
    nc, ins = core.nc, core.ins
    HALF = HALF0 if layer == 0 else BLK1 // 2
    SL = 2 * HALF
    NX = E0 if layer == 0 else NBLK1
    FF = FF0 if layer == 0 else FF1
    FC = FF // P
    result = core.result0 if layer == 0 else core.result1
    with Phase(core, f"experts{layer}") as ph:
        w1 = [ph.sb(f"w1_{q}", [P, KD, FF]) for q in range(2)]
        w2 = [ph.sb(f"w2_{q}", [P, FC, D]) for q in range(2)]
        xs = [ph.sb(f"xs{q}", [HALF, 2, D]) for q in range(2)]
        xsT = [ph.sb(f"xsT{q}", [P, KD, SL]) for q in range(2)]
        hid = [ph.sb(f"hid{q}", [P, FC, SL]) for q in range(2)]
        ys = [ph.sb(f"ys{q}", [HALF, 2, D]) for q in range(2)]
        act1 = ph.sb("act1", [P, 2, SL])
        ps1, ps3 = ([ph.ps(f"{n}{j}") for j in range(2)] for n in ("ps1", "ps3"))
        psX, psY = ([ph.ps(f"{n}{j}") for j in range(2)] for n in ("psX", "psY"))
        w_in, x_in = ([ph.plain(f"{n}{q}") for q in range(2)] for n in ("w_in", "x_in"))
        y_out, done = ([ph.sem(f"{n}{q}") for q in range(2)] for n in ("y_out", "done"))
        turned, xsT_ready, both, silu, hidden, y_ready, y_taken = (ph.sem(n) for n in (
            "turned", "xsT_ready", "both", "silu", "hidden", "y_ready", "y_taken"))
        passed, pool_passed, act_passed = ph.sem("passed"), ph.sem("pool_passed"), ph.sem("act_passed")
        if layer == 0:
            w3 = [ph.sb(f"w3_{q}", [P, KD, FF]) for q in range(2)]
        else:
            b1 = [ph.sb(f"b1_{q}", [P, FC]) for q in range(2)]
            b2 = [ph.sb(f"b2_{q}", [P, D]) for q in range(2)]
        NWHICH = 2 if layer == 0 else 4
        which = ph.sb("which", [P, 2, NWHICH, 1], I32)
        which_ready = ph.sem("which_ready")
        NW = 3 if layer == 0 else 4
        ph.credit()
        with nc.Block() as block:
            if layer == 0:
                @block.sync
                def _(sync):
                    with sync.Fori(0, NX // 2) as i:
                        for q in range(2):
                            sync.wait_ge(done[q], CREDIT + i)
                            sync.sem_inc(passed, 1)
                            for w, name in ((w1[q], "ew1"), (w3[q], "ew3"), (w2[q], "ew2")):
                                sync.dma_start(w[:], ins[f"L0_ffn_{name}"][bass.ds(2 * i + q, 1)].rearrange(
                                    "e (k p) f -> p (e k) f", p=P)).then_inc(w_in[q], 16)

            @block.gpsimd
            def _(pool):
                with pool.Fori(0, NX // 2) as i:
                    for q in range(2):
                        pool.wait_ge(done[q], CREDIT + i)
                        pool.sem_inc(pool_passed, 1)
                        for h in range(2):
                            pool.tensor_copy(which[0:HALF, q, h, :], tokens[0:HALF, bass.ds(4 * i + 2 * q + h, 1)]).then_inc(which_ready, 1)
                        if layer == 1:
                            for k in range(2):
                                pool.tensor_copy(which[:, q, 2 + k, :], blocks[:, k, bass.ds(2 * i + q, 1)]).then_inc(which_ready, 1)
                        pool.wait_ge(which_ready, CREDIT + (2 * i + q + 1) * NWHICH)
                        pool.sem_inc(pool_passed, 1)
                        for h in range(2):
                            pool.indirect_dma_start(xs[q][:, h, :], None, core.rows, bass.IndirectOffsetOnAxis(
                                ap=which[0:HALF, q, h, :], axis=0)).then_inc(x_in[q], 16)
                        if layer == 1:
                            for dst, src, k in ((w1[q][:].rearrange("p k f -> p (k f)"), ins["L1_ffn_w1"], 0),
                                                (b1[q][:], ins["L1_ffn_b1"], 0),
                                                (w2[q][:].rearrange("p k f -> p (k f)"), ins["L1_ffn_w2"], 0),
                                                (b2[q][:], ins["L1_ffn_b2"], 1)):
                                pool.indirect_dma_start(dst, None, src, bass.IndirectOffsetOnAxis(
                                    ap=which[:, q, 2 + k, :], axis=0)).then_inc(w_in[q], 16)

            @block.tensor
            def _(pe):
                with pe.Fori(0, NX // 2) as i:
                    for q in range(2):
                        n = 2 * i + q
                        pe.wait_ge(x_in[q], 32 * (i + 1))
                        pe.wait_ge(xsT_ready, CREDIT + n)
                        for k in range(KD):
                            for h in range(2):
                                last = nc.tensor.transpose(psX[q][:, k * SL + h * HALF:k * SL + (h + 1) * HALF],
                                                           xs[q][:, h, k * P:(k + 1) * P], core.ident[0:HALF, 0:HALF])
                        last.then_inc(turned, 1)
                        pe.wait_ge(w_in[q], 16 * NW * (i + 1))
                        pe.wait_ge(xsT_ready, CREDIT + n + 1)
                        for f in range(FC):
                            pe.wait_ge(hidden, CREDIT + n * FC + max(f - 1, 0))
                            for w, ps in ((w1, ps1), (w3, ps3)) if layer == 0 else ((w1, ps1),):
                                for k in range(KD):
                                    last = nc.tensor.matmul(ps[f % 2][:, 0:SL], w[q][:, k, f * P:(f + 1) * P],
                                                            xsT[q][:, k, :], start=k == 0, stop=k == KD - 1)
                            last.then_inc(both, 1)
                        pe.wait_ge(hidden, CREDIT + (n + 1) * FC)
                        pe.wait_ge(y_taken, CREDIT + n)
                        for h in range(2):
                            for f in range(FC):
                                last = nc.tensor.matmul(psY[q][0:HALF, h * D:(h + 1) * D], hid[q][:, f, h * HALF:(h + 1) * HALF],
                                                        w2[q][:, f, :], start=f == 0, stop=f == FC - 1)
                        last.then_inc(y_ready, 1)

            @block.scalar
            def _(act):
                with act.Fori(0, NX // 2) as i:
                    for q in range(2):
                        n = 2 * i + q
                        act.wait_ge(turned, CREDIT + n + 1)
                        nc.scalar.copy(xsT[q][:], psX[q][:, 0:KD * SL].rearrange("p (k s) -> p k s", k=KD)).then_inc(xsT_ready, 1)
                        for f in range(FC):
                            act.wait_ge(both, CREDIT + n * FC + f + 1)
                            if layer == 0:
                                act.wait_ge(hidden, CREDIT + n * FC + max(f - 1, 0))
                                nc.scalar.activation(act1[:, f % 2, :], ps1[f % 2][:, 0:SL], ACT.Silu).then_inc(silu, 1)
                            else:
                                act.wait_ge(y_ready, CREDIT + n)
                                nc.scalar.activation(hid[q][:, f, :], ps1[f % 2][:, 0:SL], ACT.Gelu,
                                                     bias=b1[q][:, f:f + 1]).then_inc(hidden, 1)
                        act.wait_ge(y_taken, CREDIT + n + 1)
                        act.sem_inc(act_passed, 1)
                        act.dma_start(result[bass.ds(n * SL, SL), :].rearrange("(h p) d -> p h d", p=HALF), ys[q][:]).then_inc(y_out[q], 16)
                for q in range(2):
                    act.wait_ge(y_out[q], CREDIT + 16 * (NX // 2))

            @block.vector
            def _(dve):
                with dve.Fori(0, NX // 2) as i:
                    for q in range(2):
                        n = 2 * i + q
                        if layer == 0:
                            dve.wait_ge(y_ready, CREDIT + n)
                            for f in range(FC):
                                dve.wait_ge(silu, CREDIT + n * FC + f + 1)
                                nc.vector.tensor_tensor(hid[q][:, f, :], ps3[f % 2][:, 0:SL], act1[:, f % 2, :], ALU.mult).then_inc(hidden, 1)
                        dve.wait_ge(y_out[q], CREDIT + 16 * i)
                        dve.wait_ge(y_ready, CREDIT + n + 1)
                        src = psY[q][0:HALF, 0:2 * D].rearrange("p (h d) -> p h d", h=2)
                        if layer == 0:
                            nc.vector.tensor_copy(ys[q][:], src).then_inc(y_taken, 1)
                        else:
                            nc.vector.tensor_tensor(ys[q][:], src, spread(b2[q][0:HALF, :], 2), ALU.add).then_inc(y_taken, 1)
                        dve.wait_ge(y_taken, CREDIT + n + 1)
                        dve.sem_inc(done[q], 1)


def combine_phase(core, layer, slots, weights, acc):
    nc, ins = core.nc, core.ins
    result = core.result0 if layer == 0 else core.result1
    with Phase(core, f"combine{layer}") as ph:
        ys = ph.sb("ys", [S, 2, B, D])
        sums = ph.sb("sums", [S, B, D])
        fetched, summed, loaded, stored = ph.plain("fetched"), ph.sem("summed"), ph.sem("loaded"), ph.sem("stored")
        stats_done, moments, rstd_ready, pool_steps, normed = (ph.sem(n) for n in ("stats_done", "moments", "rstd_ready", "pool_steps", "normed"))
        ln_w, ln_b = ph.sb("ln_w", [S, D]), ph.sb("ln_b", [S, D])
        stats, work = ph.sb("stats", [S, B, 6]), ph.sb("work", [S, 4, B])
        mean, rstd, t0, t1 = (work[:, k, :] for k in range(4))
        ph.credit()
        gate = core.gates[0:S, 2 + layer:3 + layer]

        def tile(buf, i):
            return buf[:, bass.ds(i, 1), :].rearrange("p a d -> p (a d)")

        with nc.Block() as block:
            @block.gpsimd
            def _(pool):
                for t in range(B):
                    for k in range(2):
                        pool.indirect_dma_start(ys[:, k, t, :], None, result,
                                                bass.IndirectOffsetOnAxis(ap=slots[:, k, t:t + 1], axis=0)).then_inc(fetched, 16)
                if layer == 1:
                    step = Steps(pool, pool_steps, CREDIT)
                    pool.wait_ge(moments, CREDIT + 6)
                    step.then(pool.tensor_scalar(t1, t1, LAST_EPS, None, ALU.add))
                    pool.tensor_tensor(rstd, t1, core.half[0:S, 0:B], ALU.pow).then_inc(rstd_ready, 1)

            @block.vector
            def _(dve):
                v = nc.vector
                dve.wait_ge(fetched, 16 * 2 * B)
                if layer == 1:
                    dve.wait_ge(loaded, CREDIT + 32)
                with dve.Fori(0, B) as t:
                    PER = 3
                    for k in range(2):
                        v.scalar_tensor_tensor(tile(sums, t), ys[:, k, bass.ds(t, 1), :].rearrange("p a d -> p (a d)"),
                                               weights[:, k, bass.ds(t, 1)], tile(acc if k == 0 else sums, t), ALU.mult, ALU.add).then_inc(summed, 1)
                        dve.wait_ge(summed, CREDIT + t * PER + k + 1)
                    if layer == 0:
                        v.scalar_tensor_tensor(tile(core.x, t), tile(sums, t), gate, tile(core.x, t), ALU.mult, ALU.add).then_inc(summed, 1)
                    else:
                        v.bn_stats(stats[:, t, :], tile(sums, t)).then_inc(summed, 1)
                if layer == 1:
                    dve.wait_ge(summed, CREDIT + PER * B)
                    step = Steps(dve, moments, CREDIT)
                    me, ve, mo, vo = (stats[:, :, k] for k in (1, 2, 4, 5))
                    step.then(v.tensor_tensor(mean, me, mo, ALU.add))
                    step.then(v.tensor_scalar(mean, mean, 0.5, None, ALU.mult))
                    step.then(v.tensor_tensor(t0, me, mo, ALU.subtract))
                    step.then(v.scalar_tensor_tensor(t0, t0, 0.25, t0, ALU.mult, ALU.mult))
                    step.then(v.tensor_tensor(t1, ve, vo, ALU.add))
                    step.then(v.scalar_tensor_tensor(t1, t1, 1.0 / D, t0, ALU.mult, ALU.add))
                    dve.wait_ge(rstd_ready, CREDIT + 1)
                    with dve.Fori(0, B) as t:
                        step = Steps(dve, normed, CREDIT + t * 4)
                        step.then(v.tensor_scalar(tile(sums, t), tile(sums, t), work[:, 0, bass.ds(t, 1)], work[:, 1, bass.ds(t, 1)],
                                                  ALU.subtract, ALU.mult))
                        step.then(v.tensor_tensor(tile(sums, t), tile(sums, t), ln_w[:], ALU.mult))
                        step.then(v.tensor_tensor(tile(sums, t), tile(sums, t), ln_b[:], ALU.add))
                        v.scalar_tensor_tensor(tile(core.x, t), tile(sums, t), gate, tile(core.x, t), ALU.mult, ALU.add).then_inc(normed, 1)

            @block.sync
            def _(sync):
                if layer == 1:
                    sync.dma_start(ln_w[:], ins["L1_ffn_ln_w"].partition_broadcast(S)).then_inc(loaded, 16)
                    sync.dma_start(ln_b[:], ins["L1_ffn_ln_b"].partition_broadcast(S)).then_inc(loaded, 16)
                    for h in range(2):
                        sync.wait_ge(normed, CREDIT + 4 * B * (h + 1) // 2)
                        sync.dma_start(core.out[8 * h:8 * h + 8].rearrange("b s d -> s b d"), core.x[:, 8 * h:8 * h + 8, :]).then_inc(stored, 16)
                    sync.wait_ge(stored, CREDIT + 32)




def program(nc, ins, out):
    with ExitStack() as ctx:
        core = Core(nc, ctx, ins, out)
        setup_phase(core)
        weights = ctx.enter_context(nc.sbuf_tensor("weights", [S, 2, B], F32))
        slots = ctx.enter_context(nc.sbuf_tensor("slots", [S, 2, B], I32))
        blocks = ctx.enter_context(nc.sbuf_tensor("blocks", [P, 2, NBLK1], I32))
        place = ctx.enter_context(nc.sbuf_tensor("place", [S, 2, 2, B], F32))
        tokens = ctx.enter_context(nc.sbuf_tensor("tokens", [P, NBLK1 * BLK1 // P], I32))
        logits0 = ctx.enter_context(nc.sbuf_tensor("logits0", [S, B, E0], F32))
        logits1 = ctx.enter_context(nc.sbuf_tensor("logits1", [S, B, E1], F32))
        norm_phase(core, "norm_a0")
        attention_phase(core, 0)
        norm_phase(core, "norm_f0", (ins["L0_ffn_gate_w"], None, logits0))
        with ExitStack() as layer0:
            acc = layer0.enter_context(nc.sbuf_tensor("shared_acc", [S, B, D], F32))
            route_phase(core, 0, logits0[:], weights, slots, place)
            invert_phase(core, 0, place, tokens)
            shared_phase(core, acc)
            experts_phase(core, 0, tokens)
            combine_phase(core, 0, slots, weights, acc)
        norm_phase(core, "norm_a1")
        attention_phase(core, 1)
        norm_phase(core, "norm_f1", (ins["L1_ffn_router_w"], ins["L1_ffn_router_b"], logits1))
        route_phase(core, 1, logits1[:], weights, slots, place, blocks)
        invert_phase(core, 1, place, tokens)
        experts_phase(core, 1, tokens, blocks)
        combine_phase(core, 1, slots, weights, core.xn)


def kernel(**inputs):
    import numpy as np
    import concourse.bacc as bacc
    from concourse.bass_utils import run_bass_kernel_spmd

    lay = {
        "ctx_1024": lambda a: a.transpose(0, 2, 1),
        "L0_xattn_bq": lambda a: a.reshape(-1, P).T,
        "L0_xattn_bk": lambda a: a.reshape(-1, P).T,
        "L1_ffn_router_w": lambda a: a.T,
        "L1_ffn_w1": lambda a: a.transpose(0, 2, 1).reshape(E1, KD, P, FF1).transpose(0, 2, 1, 3).reshape(E1 * P, KD * FF1),
        "L1_ffn_b1": lambda a: a.reshape(E1, FF1 // P, P).transpose(0, 2, 1).reshape(E1 * P, FF1 // P),
        "L1_ffn_w2": lambda a: a.transpose(0, 2, 1).reshape(E1, FF1 // P, P, D).transpose(0, 2, 1, 3).reshape(E1 * P, FF1 // P * D),
    }
    nc = bacc.Bacc("TRN2", target_bir_lowering=False, num_devices=1)
    arrays, ins = {}, {}
    for name, value in inputs.items():
        a = np.asarray(value)
        a = np.ascontiguousarray(lay[name](a) if name in lay else a)
        arrays[f"in_{name}_dram"] = a
        ins[name] = nc.dram_tensor(f"in_{name}_dram", a.shape, mybir.dt.from_np(a.dtype), kind="ExternalInput").ap()
    out = nc.dram_tensor("out_dram", (B, S, D), F32, kind="ExternalOutput").ap()
    program(nc, ins, out)
    r = run_bass_kernel_spmd(nc, [arrays], core_ids=[0])
    return r.results[0]["out_dram"]
```

```python
from contextlib import ExitStack

import concourse.bass as bass
from concourse import mybir

ALU = mybir.AluOpType
ACT = mybir.ActivationFunctionType
AX = mybir.AxisListType
F32 = mybir.dt.float32
BF16 = mybir.dt.bfloat16
I32 = mybir.dt.int32
U8 = mybir.dt.uint8

P = 128
B, S, D = 16, 100, 256
N = B * S
KD = D // P
KEYS = 361
KEY_TILES = [(0, 128), (128, 128), (256, KEYS - 256)]
HEADS = 16
LN_EPS, RMS_EPS, LAST_EPS = 1e-5, 1e-5, 1e-12
CREDIT = 1
MASKED = 1e18
BIG = 1e30

E0, FF0, SHARED = 16, 512, 2
CAP0 = -(-N * 2 // E0 * 5 // 4)
HALF0 = CAP0 // 2
E1, FF1 = 8, 1024
BLK1 = 256
NBLK1 = (2 * N + E1 * (BLK1 - 1)) // BLK1
MAXB1 = -(-N // BLK1)


class Steps:

    def __init__(self, eng, sem, base=0):
        self.eng, self.sem, self.base, self.n = eng, sem, base, 0

    def then(self, ins):
        self.n += 1
        ins.then_inc(self.sem, 1)
        self.eng.wait_ge(self.sem, self.base + self.n)


def bcast(ap, n):
    return ap.unsqueeze(len(ap.shape)).to_broadcast([*ap.shape, n])


def spread(ap, n):
    return ap.unsqueeze(1).to_broadcast([ap.shape[0], n, *ap.shape[1:]])


class Core:

    def __init__(self, nc, ctx, ins, out):
        self.nc, self.ins, self.out = nc, ins, out

        def sb(name, shape, dt=F32):
            return ctx.enter_context(nc.sbuf_tensor(name, shape, dt))

        self.x = sb("x_tokens", [S, B, D])
        self.xn = None
        self.xnT = sb("x_normed_T", [P, KD, N])
        self.ident = sb("identity", [P, P])
        self.ones = sb("ones", [P, P])
        self.tri = sb("tri_before", [P, P])
        self.gates = sb("gates", [P, 4])
        self.half = sb("minus_half", [P, 64])
        self.rows = nc.dram_tensor("rows_dram", [N, D], F32, kind="Internal").ap()
        self.result0 = nc.dram_tensor("results0_dram", [E0 * CAP0 + P, D], F32, kind="Internal").ap()
        self.result1 = nc.dram_tensor("results1_dram", [NBLK1 * BLK1, D], F32, kind="Internal").ap()
        self.bounce = nc.dram_tensor("turn_dram", [3, 2, P, S], F32, kind="Internal").ap()


class Phase:

    def __init__(self, core, name):
        self.core, self.nc, self.name, self.ctx = core, core.nc, name, ExitStack()
        self.sems, self.all_sems = [], []

    def __enter__(self):
        return self

    def __exit__(self, *a):
        self.nc.clear_and_free_semaphores(self.all_sems)
        self.nc.all_engine_barrier()
        return self.ctx.__exit__(*a)

    def sb(self, name, shape, dt=F32):
        return self.ctx.enter_context(self.nc.sbuf_tensor(f"{self.name}_{name}", shape, dt))

    def ps(self, name, shape=(P, 512), dt=F32):
        return self.ctx.enter_context(self.nc.psum_tensor(f"{self.name}_{name}", list(shape), dt))

    def sem(self, name):
        s = self.plain(name)
        self.sems.append(s)
        return s

    def plain(self, name):
        s = self.nc.alloc_semaphore(f"{self.name}_{name}")
        self.all_sems.append(s)
        return s

    def credit(self, sems=None):
        with self.nc.Block() as block:
            @block.sync
            def _(sync):
                for s in sems or self.sems:
                    sync.sem_inc(s, CREDIT)


def setup_phase(core):
    nc = core.nc
    with Phase(core, "setup") as ph:
        zeros = ph.sb("zeros", [P, D])
        g_raw = ph.sb("g_raw", [P, 4])
        loaded, cleared = ph.sem("loaded"), ph.sem("cleared")
        zeros_ready, blanks, shapes = ph.sem("zeros_ready"), ph.sem("blanks"), ph.sem("shapes")
        gates_ready = ph.sem("gates_ready")
        with nc.Block() as block:
            @block.sync
            def _(sync):
                sync.dma_start(core.x[:], core.ins["x"].rearrange("b s d -> s b d")).then_inc(loaded, 16)
                for j, g in enumerate(("g_xattn", "g_ffn")):
                    sync.dma_start(g_raw[:, 2 * j:2 * j + 2], core.ins[g].partition_broadcast(P)).then_inc(loaded, 16)
                sync.wait_ge(zeros_ready, 1)
                sync.dma_start(core.result0[E0 * CAP0:], zeros[:]).then_inc(cleared, 16)
                sync.wait_ge(cleared, 16)
                sync.wait_ge(loaded, 48)

            @block.gpsimd
            def _(pool):
                pool.memset(core.ident[:], 0.0).then_inc(blanks, 1)
                pool.memset(core.tri[:], 0.0).then_inc(blanks, 1)
                pool.memset(core.ones[:], 1.0).then_inc(blanks, 1)
                pool.memset(core.half[:], -0.5).then_inc(blanks, 1)
                pool.wait_ge(blanks, 4)
                pool.affine_select(out=core.ident[:], in_=core.ident[:], compare_op=ALU.not_equal, fill=1.0,
                                   base=0, pattern=[[-1, P]], channel_multiplier=1).then_inc(shapes, 1)
                pool.affine_select(out=core.tri[:], in_=core.tri[:], compare_op=ALU.is_ge, fill=1.0,
                                   base=0, pattern=[[-1, P]], channel_multiplier=1).then_inc(shapes, 1)
                pool.wait_ge(shapes, 2)

            @block.vector
            def _(dve):
                nc.vector.memset(zeros[:], 0.0).then_inc(zeros_ready, 1)

            @block.scalar
            def _(act):
                act.wait_ge(loaded, 48)
                nc.scalar.activation(core.gates[:], g_raw[:], ACT.Tanh).then_inc(gates_ready, 1)
                act.wait_ge(gates_ready, 1)


def norm_phase(core, name, router=None):
    nc = core.nc
    with Phase(core, name) as ph:
        stats = ph.sb("stats", [S, B, 6])
        work = ph.sb("work", [S, 4, B])
        mean, rstd, t0, t1 = (work[:, k, :] for k in range(4))
        stage = ph.sb("stage", [S, 2, D])
        turned = ph.sb("turned", [P, 2, KD, S])
        psT = [ph.ps(f"psT{j}") for j in range(2)]
        psL = [ph.ps(f"psL{j}") for j in range(2)]
        stats_done, moments, rstd_ready = ph.sem("stats_done"), ph.sem("moments"), ph.sem("rstd_ready")
        normed, turned_ps, copied = ph.sem("normed"), ph.sem("turned_ps"), ph.sem("copied")
        scored, scores_copied, w_loaded = ph.sem("scored"), ph.sem("scores_copied"), ph.sem("w_loaded")
        pool_steps, kept = ph.sem("pool_steps"), ph.sem("kept")
        if router:
            w_dram, b_dram, logits = router
            E = logits.shape[2]
            w_sb = ph.sb("w", [P, KD, E])
            b_sb = ph.sb("b", [S, E])

        ph.credit()
        with nc.Block() as block:
            if router:
                @block.sync
                def _(sync):
                    sync.dma_start(w_sb[:], w_dram.rearrange("(k p) e -> p k e", p=P)).then_inc(w_loaded, 16)
                    if b_dram is not None:
                        sync.dma_start(b_sb[:], b_dram.partition_broadcast(S)).then_inc(w_loaded, 16)

            @block.vector
            def _(dve):
                with dve.Fori(0, B) as i:
                    nc.vector.bn_stats(stats[:, i, :], core.x[:, i, :]).then_inc(stats_done, 1)
                dve.wait_ge(stats_done, CREDIT + B)
                step = Steps(dve, moments, CREDIT)
                me, ve, mo, vo = (stats[:, :, k] for k in (1, 2, 4, 5))
                step.then(nc.vector.tensor_tensor(mean, me, mo, ALU.add))
                step.then(nc.vector.tensor_scalar(mean, mean, 0.5, None, ALU.mult))
                step.then(nc.vector.tensor_tensor(t0, me, mo, ALU.subtract))
                step.then(nc.vector.scalar_tensor_tensor(t0, t0, 0.25, t0, ALU.mult, ALU.mult))
                step.then(nc.vector.tensor_tensor(t1, ve, vo, ALU.add))
                step.then(nc.vector.scalar_tensor_tensor(t1, t1, 1.0 / D, t0, ALU.mult, ALU.add))
                dve.wait_ge(rstd_ready, CREDIT + 1)
                with dve.Fori(0, B // 2) as j:
                    for q in range(2):
                        dve.wait_ge(turned_ps, CREDIT + 2 * j)
                        if core.xn is not None:
                            dve.wait_ge(kept, CREDIT + 2 * j)
                        nc.vector.tensor_scalar(stage[:, q, :], core.x[:, 2 * j + q, :], work[:, 0, bass.ds(2 * j + q, 1)],
                                                work[:, 1, bass.ds(2 * j + q, 1)], ALU.subtract, ALU.mult).then_inc(normed, 1)
                    if router:
                        for q in range(2):
                            dve.wait_ge(scored, CREDIT + 2 * j + q + 1)
                            if b_dram is not None:
                                dve.wait_ge(w_loaded, CREDIT + 32)
                                nc.vector.tensor_tensor(logits[:, 2 * j + q, :], psL[q][0:S, 0:E], b_sb[:], ALU.add).then_inc(scores_copied, 1)
                            else:
                                nc.vector.tensor_copy(logits[:, 2 * j + q, :], psL[q][0:S, 0:E]).then_inc(scores_copied, 1)

            @block.gpsimd
            def _(pool):
                step = Steps(pool, pool_steps, CREDIT)
                pool.wait_ge(moments, CREDIT + 6)
                step.then(pool.tensor_scalar(t1, t1, LN_EPS, None, ALU.add))
                pool.tensor_tensor(rstd, t1, core.half[0:S, 0:B], ALU.pow).then_inc(rstd_ready, 1)

            @block.tensor
            def _(pe):
                if router:
                    pe.wait_ge(w_loaded, CREDIT + (32 if b_dram is not None else 16))
                with pe.Fori(0, B // 2) as j:
                    for q in range(2):
                        pe.wait_ge(normed, CREDIT + 2 * j + q + 1)
                        pe.wait_ge(copied, CREDIT + 2 * j)
                        for k in range(KD):
                            last = nc.tensor.transpose(psT[q][:, k * S:(k + 1) * S], stage[:, q, k * P:(k + 1) * P],
                                                       core.ident[0:S, 0:S])
                        last.then_inc(turned_ps, 1)
                    if router:
                        for q in range(2):
                            pe.wait_ge(copied, CREDIT + 2 * j + q + 1)
                            pe.wait_ge(scores_copied, CREDIT + 2 * j)
                            for k in range(KD):
                                last = nc.tensor.matmul(psL[q][0:S, 0:E], turned[:, q, k, :], w_sb[:, k, :],
                                                        start=k == 0, stop=k == KD - 1)
                            last.then_inc(scored, 1)

            @block.scalar
            def _(act):
                with act.Fori(0, B // 2) as j:
                    for q in range(2):
                        if core.xn is not None:
                            act.wait_ge(normed, CREDIT + 2 * j + q + 1)
                            nc.scalar.copy(core.xn[:, 2 * j + q, :], stage[:, q, :]).then_inc(kept, 1)
                    for q in range(2):
                        act.wait_ge(turned_ps, CREDIT + 2 * j + q + 1)
                        if router:
                            act.wait_ge(scored, CREDIT + 2 * j)
                        src = psT[q][:, 0:KD * S].rearrange("p (k s) -> p k s", k=KD)
                        nc.scalar.copy(core.xnT[:, :, bass.ds((2 * j + q) * S, S)], src)
                        nc.scalar.copy(turned[:, q, :, :], src).then_inc(copied, 1)


class Count:

    def __init__(self, base=0, odd=0):
        self.base, self.odd, self.n = base, odd, 0

    def next(self):
        n = self.n
        self.n += 1
        return self.base + n, (self.odd + n) % 2

    def one_before_last(self, n):
        if isinstance(n, int):
            return CREDIT + max(n - 1, 0)
        return CREDIT + n - 1


def three_products(nc, out, left, right, start, stop):
    (left_high, left_low), (right_high, right_low) = left, right
    nc.tensor.matmul(out, left_high, right_high, start=start, stop=False)
    nc.tensor.matmul(out, left_high, right_low, start=False, stop=False)
    return nc.tensor.matmul(out, left_low, right_high, start=False, stop=stop)


def attention_phase(core, layer):
    nc, ins = core.nc, core.ins
    pre = f"L{layer}_xattn_"
    DH = 16 if layer == 0 else 64
    W = HEADS * DH
    WC = W // P
    HALVES = max(1, W // 512)
    HW = min(W, 512)
    EVEN = KEYS + 1
    if layer == 0:
        QK = {0: [("q", 0)], 1: [("q", 1)], 2: [("k", 0)], 3: [("k", 1)]}
    else:
        QK = {0: [("q", 0, 0), ("q", 0, 1)]}
        for j in range(6):
            QK[j + 1] = [("k", j // 2, j % 2)]
        QK |= {8: [("tq", 0)], 9: [("tq", 1)], 11: [("tk", 0), ("tk", 1)], 12: [("tk", 2), ("tk", 3)],
               13: [("tk", 4), ("tk", 5)], 14: [("tk", 6)], 15: [("tk", 7)]}
        SCALE_AT = {5: 0, 7: 1, 9: 2, 10: 3}
    V = [("v", t, a) for t in range(3) for a in range(HALVES)]
    V1, V2, V3 = V[:HALVES], V[HALVES:2 * HALVES], V[2 * HALVES:]
    NQK = sum(map(len, QK.values()))
    PER = NQK + len(V) + HALVES + 1
    FIRST = NQK + 2 * HALVES

    with Phase(core, f"attn{layer}") as ph:
        R = mybir.dt.float32r
        wq = ph.sb("wq", [P, KD, W])
        wk, wv = ([ph.sb(f"{n}_{part}", [P, KD, W], R) for part in ("high", "low")] for n in ("wk", "wv"))
        wo = ph.sb("wo", [P, WC, D])
        ctx_raw = ph.sb("ctx_raw", [P, KD, KEYS])
        ctxT = [[ph.sb(f"ctxT{q}_{part}", [P, KD, EVEN], R) for part in ("high", "low")] for q in range(2)]
        kT = [ph.sb(f"kT{q}", [P, WC, KEYS]) for q in range(2)]
        v = [ph.sb(f"v{q}", [P, 3, W]) for q in range(2)]
        off = ph.sb("off", [S, KEYS])
        masked = ph.sb("masked", [S, 2, KEYS])
        probs = ph.sb("probs", [S, 2, KEYS])
        probsT = ph.sb("probsT", [P, 2, 3, S])
        least = ph.sb("least", [S, HEADS])
        total = ph.sb("total", [S, HEADS])
        inv = ph.sb("inv", [S, HEADS])
        o = ph.sb("o", [S, W])
        oT = ph.sb("oT", [P, WC, S])
        y = ph.sb("y", [S, D])
        IN_CHUNK = P // DH
        qT = [ph.sb(f"qT{q}", [P, WC, IN_CHUNK, S]) for q in range(2)]
        pick = ph.sb("pick", [P, IN_CHUNK])
        psP = [ph.ps(f"psP{j}") for j in range(2)]
        psS = [ph.ps(f"psS{j}") for j in range(2)]
        psT = [ph.ps(f"psT{j}") for j in range(2)]
        psO = ph.ps("psO", [P, 2, 512])
        names = ("w_in", "w_split", "split_high", "loaded", "ctx_in", "ctx_split", "ctx_free", "mask_in", "piece_ready", "piece_taken",
                 "off_ready", "scored", "masked_ready", "probs_ready", "probs_turned", "probsT_ready", "head_done",
                 "inv_ready", "o_scaled", "o_ready", "y_ready", "x_steps", "cleared", "const_steps", "ints_ready",
                 "sync_passed", "pool_passed", "mask_passed", "blank")
        (w_in, w_split, split_high, loaded, ctx_in, ctx_split, ctx_free, mask_in, piece_ready, piece_taken,
         off_ready, scored, masked_ready, probs_ready, probs_turned, probsT_ready, head_done,
         inv_ready, o_scaled, o_ready, y_ready, x_steps, cleared, const_steps, ints_ready,
         sync_passed, pool_passed, mask_passed, blank) = map(ph.sem, names)
        if layer == 0:
            stage = ph.sb("stage", [P, 4, W])
            raw_mask = ph.sb("raw_mask", [S, KEYS], U8)
            bq, bk = ph.sb("bq", [P, WC]), ph.sb("bk", [P, WC])
            bv, bo = ph.sb("bv", [S, D]), ph.sb("bo", [S, D])
            queries = ph.sb("queries", [P, WC, S])
            queries_ready, copies_ready = ph.sem("queries_ready"), ph.sem("copies_ready")
            consts, XS = 6, 2
        else:
            raw = ph.sb("raw", [P, 4, W])
            stage = raw
            square = ph.sb("square", [P, 2, HW])
            sums = ph.sb("sums", [P, 4, HEADS])
            rms = ph.sb("rms", [P, 4, HEADS])
            lens_i, lens = ph.sb("lens_i", [S, B], I32), ph.sb("lens", [S, B])
            key_i, key_no = ph.sb("key_i", [S, KEYS], I32), ph.sb("key_no", [S, KEYS])
            wcol, wk_col = ph.sb("wcol", [P, 1]), ph.sb("wk_col", [P, 1])
            xq = ph.sb("xq", [P, KD, S])
            summed, rms_steps, scaled, xq_ready = map(ph.sem, ("summed", "rms_steps", "scaled", "xq_ready"))
            consts, XS = 7, 1
        ph.credit()

        def pieces_of(b, q):
            return Count(FIRST + b * PER, (FIRST + q * PER) % 2)

        def steps(engine, step):
            with engine.Fori(0, B // 2 - 1) as i:
                step(2 * i, 0, 2 * i + 1)
                step(2 * i + 1, 1, 2 * i + 2)
            step(B - 2, 0, B - 1)
            step(B - 1, 1, None)

        with nc.Block() as block:
            @block.sync
            def _(sync):
                for n, name in enumerate(("Wk", "Wv")):
                    sync.dma_start(stage[:, 2 * n:2 * n + 2, :], ins[pre + name].rearrange("(k p) n -> p k n", p=P)).then_inc(w_in, 16)
                    sync.wait_ge(w_in, CREDIT + 16 * (n + 1))
                sync.dma_start(ctx_raw[:], ins["ctx_1024"][0].rearrange("(k p) n -> p k n", p=P)).then_inc(ctx_in, 16)
                sync.dma_start(wq[:], ins[pre + "Wq"].rearrange("(k p) n -> p k n", p=P)).then_inc(loaded, 16)
                sync.dma_start(wo[:], ins[pre + "Wo"].rearrange("(k p) n -> p k n", p=P)).then_inc(loaded, 16)
                if layer == 0:
                    for b, name in ((bq, "bq"), (bk, "bk")):
                        sync.dma_start(b[:], ins[pre + name]).then_inc(loaded, 16)
                    for b, name in ((bv, "bv"), (bo, "bo")):
                        sync.dma_start(b[:], ins[pre + name].partition_broadcast(S)).then_inc(loaded, 16)
                    sync.dma_start(raw_mask[:], ins["mask_BxSxS2_bk1"][0]).then_inc(mask_in, 16)
                else:
                    for half in range(2):
                        for b, name in ((wcol, "q_norm_w"), (wk_col, "k_norm_w")):
                            sync.dma_start(b[64 * half:64 * half + 64, :],
                                           ins[pre + name].rearrange("(p a) -> p a", a=1)).then_inc(loaded, 16)
                    sync.dma_start(lens_i[:], ins["_lenS2"].partition_broadcast(S)).then_inc(loaded, 16)
                with sync.Fori(1, B) as i:
                    sync.wait_ge(ctx_split, CREDIT + 2 * i)
                    sync.sem_inc(sync_passed, 1)
                    sync.dma_start(ctx_raw[:], ins["ctx_1024"][bass.ds(i, 1)].rearrange("b (k p) n -> p (b k) n", p=P)).then_inc(ctx_in, 16)
                    if layer == 0:
                        sync.wait_ge(off_ready, CREDIT + i)
                        sync.sem_inc(sync_passed, 1)
                        sync.dma_start(raw_mask[:], ins["mask_BxSxS2_bk1"][bass.ds(i, 1)].rearrange("b s n -> (b s) n")).then_inc(mask_in, 16)

            @block.tensor
            def _(pe):
                def piece(count, kind, b, q):
                    n, bank = count.next()
                    ps = psP[bank]
                    pe.wait_ge(piece_taken, count.one_before_last(n))
                    if kind[0] == "q" and layer == 0:
                        c = kind[1]
                        for k in range(KD):
                            last = nc.tensor.matmul(ps[:, 0:S], wq[:, k, c * P:(c + 1) * P], core.xnT[:, k, bass.ds(b * S, S)],
                                                    start=k == 0, stop=k == KD - 1)
                    elif kind[0] == "k" and layer == 0:
                        c = kind[1]
                        pe.wait_ge(ctx_split, CREDIT + 2 * (b + 1))
                        for k in range(KD):
                            last = three_products(nc, ps[:, 0:EVEN], [w[:, k, c * P:(c + 1) * P] for w in wk],
                                                  [x[:, k, :] for x in ctxT[q]], k == 0, k == KD - 1)
                    elif kind[0] == "q":
                        a = kind[2]
                        pe.wait_ge(xq_ready, CREDIT + b + 1)
                        for k in range(KD):
                            last = nc.tensor.matmul(ps[0:S, :], xq[:, k, :], wq[:, k, a * HW:(a + 1) * HW],
                                                    start=k == 0, stop=k == KD - 1)
                    elif kind[0] in "kv":
                        _, t, a = kind
                        k0, rows = KEY_TILES[t]
                        pe.wait_ge(ctx_split, CREDIT + 2 * (b + 1))
                        for k in range(KD):
                            last = three_products(nc, ps[0:rows, 0:HW], [x[:, k, k0:k0 + rows] for x in ctxT[q]],
                                                  [w[:, k, a * HW:(a + 1) * HW] for w in (wk if kind[0] == "k" else wv)],
                                                  k == 0, k == KD - 1)
                    elif kind[0] == "tq":
                        pe.wait_ge(scaled, CREDIT + 4 * b + 1)
                        for j in range(4):
                            c = 4 * kind[1] + j
                            last = nc.tensor.transpose(ps[:, j * S:(j + 1) * S], raw[0:S, 0, c * P:(c + 1) * P], core.ident[0:S, 0:S])
                    elif kind[0] == "tk":
                        pe.wait_ge(scaled, CREDIT + 4 * b + 4)
                        c = kind[1]
                        for t, (k0, rows) in enumerate(KEY_TILES):
                            last = nc.tensor.transpose(ps[:, k0:k0 + rows], raw[0:rows, 1 + t, c * P:(c + 1) * P],
                                                       core.ident[0:rows, 0:rows])
                    elif kind[0] == "o":
                        a = kind[1]
                        pe.wait_ge(o_ready, CREDIT + HALVES * b + a + 1)
                        for c in range(4 * a, min(4 * a + 4, WC)):
                            last = nc.tensor.transpose(ps[:, (c % 4) * S:(c % 4 + 1) * S], o[:, c * P:(c + 1) * P], core.ident[0:S, 0:S])
                    else:
                        pe.wait_ge(piece_taken, CREDIT + kind[1])
                        for c in range(WC):
                            last = nc.tensor.matmul(ps[0:S, 0:D], oT[:, c, :], wo[:, c, :], start=c == 0, stop=c == WC - 1)
                    last.then_inc(piece_ready, 1)

                def step(b, q, following):
                    count = pieces_of(b, q)
                    first = b * HEADS

                    def scores(h):
                        c, r = divmod(h, IN_CHUNK)
                        if h or not isinstance(b, int):
                            pe.wait_ge(masked_ready, CREDIT + first + max(h - 1, 0))
                        nc.tensor.matmul(psS[h % 2][0:S, 0:KEYS], qT[q][:, c, r, :], kT[q][:, c, :], start=True, stop=True).then_inc(scored, 1)

                    def turn(h):
                        pe.wait_ge(probs_ready, CREDIT + first + h + 1)
                        pe.wait_ge(probsT_ready, CREDIT + first + max(h - 1, 0))
                        for t, (k0, n) in enumerate(KEY_TILES):
                            last = nc.tensor.transpose(psT[h % 2][0:n, t * S:(t + 1) * S], probs[:, h % 2, k0:k0 + n],
                                                       core.ident[0:S, 0:S])
                        last.then_inc(probs_turned, 1)

                    def values(h):
                        if h == 0:
                            pe.wait_ge(piece_taken, CREDIT + count.base + HALVES)
                            pe.wait_ge(o_ready, CREDIT + HALVES * b)
                        pe.wait_ge(probsT_ready, CREDIT + first + h + 1)
                        a, col = divmod(h * DH, 512)
                        for t, (k0, n) in enumerate(KEY_TILES):
                            last = nc.tensor.matmul(psO[0:S, a, col:col + DH], probsT[0:n, h % 2, t, :],
                                                    v[q][0:n, t, h * DH:(h + 1) * DH], start=t == 0, stop=t == 2)
                        last.then_inc(head_done, 1)

                    pe.wait_ge(piece_taken, CREDIT + count.base - (HALVES + HALVES + 1 + HALVES if not isinstance(b, int) or b else 2 * HALVES))
                    if layer == 0:
                        pe.wait_ge(copies_ready, CREDIT + WC * (b + 1))
                    scores(0)
                    for h in range(HEADS):
                        if h + 1 < HEADS:
                            scores(h + 1)
                        if h == 0:
                            for kind in V3:
                                piece(count, kind, b, q)
                        if following is not None:
                            for kind in QK.get(h, ()):
                                piece(count, kind, following, 1 - q)
                        turn(h)
                        if h:
                            values(h - 1)
                    values(HEADS - 1)
                    if following is not None:
                        for kind in V1:
                            piece(count, kind, following, 1 - q)
                    for a in range(HALVES):
                        piece(count, ("o", a), b, q)
                    turned = count.base + count.n
                    if following is not None:
                        for kind in V2:
                            piece(count, kind, following, 1 - q)
                    piece(count, ("out", turned), b, q)

                pe.wait_ge(loaded, CREDIT + 16 * consts)
                pe.wait_ge(w_split, CREDIT + 4)
                pe.wait_ge(cleared, CREDIT + 1)
                count = Count()
                for kind in [k for h in sorted(QK) for k in QK[h]] + V1 + V2:
                    piece(count, kind, 0, 0)
                steps(pe, step)

            @block.scalar
            def _(act):
                def take(count, kind, b, q):
                    n, bank = count.next()
                    ps = psP[bank]
                    act.wait_ge(piece_ready, CREDIT + n + 1)
                    copy = nc.scalar.copy
                    if kind[0] == "q" and layer == 0:
                        c = kind[1]
                        act.wait_ge(copies_ready, CREDIT + WC * b)
                        nc.scalar.activation(queries[:, c, :], ps[:, 0:S], ACT.Identity, scale=-DH ** -0.5,
                                             bias=bq[:, c:c + 1]).then_inc(queries_ready, 1)
                        act.wait_ge(queries_ready, CREDIT + WC * b + c + 1)
                        act.sem_inc(piece_taken, 1)
                        return
                    elif kind[0] == "k" and layer == 0:
                        c = kind[1]
                        last = nc.scalar.activation(kT[q][:, c, :], ps[:, 0:KEYS], ACT.Identity, bias=bk[:, c:c + 1])
                    elif kind[0] in "qk":
                        t = 0 if kind[0] == "q" else 1 + kind[1]
                        a = kind[2]
                        rows = S if t == 0 else KEY_TILES[t - 1][1]
                        before = 8 * b + 2 * t + a
                        copy(raw[0:rows, t, a * HW:(a + 1) * HW], ps[0:rows, :])
                        if not (isinstance(before, int) and before < 2):
                            act.wait_ge(summed, CREDIT + before - 1)
                        last = nc.scalar.activation(square[0:rows, a, :], ps[0:rows, :], ACT.Square)
                    elif kind[0] == "v":
                        _, t, a = kind
                        rows = KEY_TILES[t][1]
                        last = copy(v[q][0:rows, t, a * HW:(a + 1) * HW], ps[0:rows, 0:HW])
                    elif kind[0] == "tq":
                        for r in range(2):
                            last = nc.scalar.activation(qT[q][:, 4 * kind[1]:4 * kind[1] + 4, r, :],
                                                        ps[:, 0:4 * S].rearrange("p (c s) -> p c s", c=4), ACT.Identity,
                                                        scale=pick[:, r:r + 1])
                    elif kind[0] == "tk":
                        last = copy(kT[q][:, kind[1], :], ps[:, 0:KEYS])
                    elif kind[0] == "o":
                        a, m = kind[1], min(4, WC)
                        last = copy(oT[:, 4 * a:4 * a + m, :], ps[:, 0:m * S].rearrange("p (c s) -> p c s", c=m))
                    else:
                        act.wait_ge(x_steps, CREDIT + XS * b)
                        nc.scalar.mul(y[:], ps[0:S, 0:D], core.gates[0:S, layer:layer + 1]).then_inc(y_ready, 1)
                        act.wait_ge(y_ready, CREDIT + b + 1)
                        act.sem_inc(piece_taken, 1)
                        return
                    last.then_inc(piece_taken, 1)

                def stand_queries(b, count):
                    nc.scalar.copy(xq[:], core.xnT[:, :, bass.ds(b * S, S)]).then_inc(xq_ready, 1)

                def step(b, q, following):
                    count = pieces_of(b, q)
                    first = b * HEADS

                    def exp(h):
                        act.wait_ge(masked_ready, CREDIT + first + h + 1)
                        act.wait_ge(probs_turned, CREDIT + first + max(h - 1, 0))
                        if h == 0:
                            act.wait_ge(inv_ready, CREDIT + b)
                        nc.scalar.activation(probs[:, h % 2, :], masked[:, h % 2, :], ACT.Exp, bias=least[:, h:h + 1],
                                             scale=-1.0, accum_out=total[:, h:h + 1]).then_inc(probs_ready, 1)

                    exp(0)
                    for h in range(HEADS):
                        if h + 1 < HEADS:
                            exp(h + 1)
                        if h == 0:
                            for kind in V3:
                                take(count, kind, b, q)
                            if layer == 1 and following is not None:
                                stand_queries(following, count)
                        if following is not None:
                            for kind in QK.get(h, ()):
                                take(count, kind, following, 1 - q)
                    if following is not None:
                        for kind in V1:
                            take(count, kind, following, 1 - q)
                    for a in range(HALVES):
                        take(count, ("o", a), b, q)
                    if following is not None:
                        for kind in V2:
                            take(count, kind, following, 1 - q)
                    take(count, ("out",), b, q)

                for n, w in enumerate((wk, wv)):
                    act.wait_ge(w_in, CREDIT + 16 * (n + 1))
                    nc.scalar.copy(w[0][:], stage[:, 2 * n:2 * n + 2, :]).then_inc(split_high, 1)
                act.wait_ge(const_steps, CREDIT + (2 if layer == 0 else 4))
                act.wait_ge(w_split, CREDIT + 4)
                if layer == 1:
                    stand_queries(0, None)
                count = Count()
                for kind in [k for h in sorted(QK) for k in QK[h]] + V1 + V2:
                    take(count, kind, 0, 0)
                steps(act, step)

            @block.gpsimd
            def _(pool):
                def split(b, q):
                    pool.wait_ge(ctx_in, CREDIT + 16 * (b + 1))
                    pool.sem_inc(pool_passed, 1)
                    if not (isinstance(b, int) and b < 2):
                        pool.wait_ge(piece_ready, CREDIT + FIRST + (b - 2) * PER + HALVES)
                        pool.sem_inc(pool_passed, 1)
                    pool.tensor_copy(ctxT[q][0][:, :, 0:KEYS], ctx_raw[:]).then_inc(ctx_split, 1)
                    pool.wait_ge(ctx_split, CREDIT + 2 * b + 1)
                    pool.tensor_tensor(ctxT[q][1][:, :, 0:KEYS], ctx_raw[:], ctxT[q][0][:, :, 0:KEYS].bitcast(F32), ALU.subtract).then_inc(ctx_split, 1)

                def copy_queries(b, q):
                    for c in range(WC):
                        pool.wait_ge(queries_ready, CREDIT + WC * b + c + 1)
                        pool.sem_inc(pool_passed, 1)
                        pool.tensor_tensor(qT[q][:, c, :, :], spread(queries[:, c, :], IN_CHUNK), bcast(pick[:], S),
                                           ALU.mult).then_inc(copies_ready, 1)

                def norms(b, q):
                    if layer == 0:
                        return copy_queries(b, q)
                    count = Steps(pool, rms_steps, CREDIT + 8 * b)
                    for t in range(4):
                        rows = S if t == 0 else KEY_TILES[t - 1][1]
                        pool.wait_ge(summed, CREDIT + 8 * b + 2 * t + 2)
                        pool.sem_inc(pool_passed, 1)
                        count.then(pool.tensor_scalar(rms[0:rows, t, :], sums[0:rows, t, :], 1.0 / DH, RMS_EPS, ALU.mult, ALU.add))
                        count.then(pool.tensor_tensor(rms[0:rows, t, :], rms[0:rows, t, :], core.half[0:rows, 0:HEADS], ALU.pow))

                def add_output(b):
                    pool.wait_ge(y_ready, CREDIT + b + 1)
                    pool.sem_inc(pool_passed, 1)
                    row = core.x[:, bass.ds(b, 1), :].rearrange("p a d -> p (a d)")
                    count = Steps(pool, x_steps, CREDIT + XS * b)
                    if layer == 0:
                        count.then(pool.tensor_tensor(row, row, bo[:], ALU.add))
                        pool.sem_inc(pool_passed, 1)
                    pool.tensor_tensor(row, row, y[:], ALU.add).then_inc(x_steps, 1)

                pool.memset(pick[:], 1.0).then_inc(blank, 1)
                pool.wait_ge(blank, CREDIT + 1)
                pool.affine_select(out=pick[:], in_=pick[:], compare_op=ALU.is_ge, fill=0.0,
                                   base=0, pattern=[[-DH, IN_CHUNK]], channel_multiplier=1).then_inc(blank, 1)
                pool.wait_ge(blank, CREDIT + 2)
                pool.affine_select(out=pick[:], in_=pick[:], compare_op=ALU.is_ge, fill=0.0,
                                   base=DH - 1, pattern=[[DH, IN_CHUNK]], channel_multiplier=-1).then_inc(ints_ready, 1)
                if layer == 1:
                    pool.iota(key_i[:], [[1, KEYS]], base=0, channel_multiplier=0).then_inc(ints_ready, 1)
                for q in range(2):
                    for x in ctxT[q]:
                        pool.memset(x[:, :, KEYS:EVEN].bitcast(F32), 0.0).then_inc(blank, 1)
                if layer == 0:
                    pool.wait_ge(const_steps, CREDIT + 2)
                    pool.wait_ge(ints_ready, CREDIT + 1)
                split(0, 0)
                norms(0, 0)
                split(1, 1)
                with pool.Fori(0, B // 2 - 1) as i:
                    for q in range(2):
                        norms(2 * i + q + 1, 1 - q)
                        split(2 * i + q + 2, q)
                        add_output(2 * i + q)
                norms(B - 1, 1)
                add_output(B - 2)
                add_output(B - 1)

            @block.vector
            def _(dve):
                gate = core.gates[0:S, layer:layer + 1]
                for n, w in enumerate((wk, wv)):
                    dve.wait_ge(split_high, CREDIT + n + 1)
                    nc.vector.tensor_tensor(w[1][:], stage[:, 2 * n:2 * n + 2, :], w[0][:].bitcast(F32), ALU.subtract).then_inc(w_split, 2)
                dve.wait_ge(loaded, CREDIT + 16 * consts)
                dve.wait_ge(ints_ready, CREDIT + 1 + layer)
                const = Steps(dve, const_steps, CREDIT)
                if layer == 0:
                    const.then(nc.vector.tensor_scalar(bq[:], bq[:], -DH ** -0.5, None, ALU.mult))
                    const.then(nc.vector.tensor_scalar(bo[:], bo[:], gate, None, ALU.mult))
                else:
                    const.then(nc.vector.scalar_tensor_tensor(wcol[:], wcol[:], -DH ** -0.5, wk_col[:], ALU.mult, ALU.mult))
                    const.then(nc.vector.tensor_copy(lens[:], lens_i[:]))
                    const.then(nc.vector.tensor_copy(key_no[:], key_i[:]))
                    const.then(nc.vector.tensor_scalar(pick[:], pick[:], wcol[:], None, ALU.mult))
                for j in range(2):
                    const.then(nc.vector.memset(psT[j][:], 0.0))
                dve.sem_inc(cleared, 1)

                def sum_squares(b, t, a):
                    rows = S if t == 0 else KEY_TILES[t - 1][1]
                    n = 2 * t + a
                    if isinstance(b, int) and b == 0:
                        dve.wait_ge(piece_taken, CREDIT + n + 1)
                    else:
                        dve.wait_ge(piece_taken, CREDIT + FIRST + (b - 1) * PER + HALVES + n + 1)
                    nc.vector.tensor_reduce(sums[0:rows, t, a * 8:(a + 1) * 8],
                                            square[0:rows, a, :].rearrange("p (h d) -> p h d", d=DH),
                                            AX.X, ALU.add).then_inc(summed, 1)

                def scale(b, t):
                    rows = S if t == 0 else KEY_TILES[t - 1][1]
                    dve.wait_ge(rms_steps, CREDIT + 8 * b + 2 * (t + 1))
                    heads = raw[0:rows, t, :].rearrange("p (h d) -> p h d", d=DH)
                    nc.vector.tensor_tensor(heads, heads, bcast(rms[0:rows, t, :], DH), ALU.mult).then_inc(scaled, 1)

                def step(b, q, following):
                    first = b * HEADS
                    if layer == 0:
                        dve.wait_ge(mask_in, CREDIT + 16 * (b + 1))
                        nc.vector.tensor_scalar(off[:], raw_mask[:], MASKED, None, ALU.mult).then_inc(off_ready, 1)
                    else:
                        length = lens[:, b:b + 1] if isinstance(b, int) else lens[:, bass.ds(b, 1)]
                        nc.vector.tensor_scalar(off[:], key_no[:], length, MASKED, ALU.is_ge, ALU.mult).then_inc(off_ready, 1)

                    def mask(h):
                        dve.wait_ge(scored, CREDIT + first + h + 1)
                        if h == 0:
                            dve.wait_ge(off_ready, CREDIT + b + 1)
                        dve.wait_ge(probs_ready, CREDIT + first + max(h - 1, 0))
                        dve.sem_inc(mask_passed, 1)
                        nc.vector.tensor_tensor_reduce(masked[:, h % 2, :], psS[h % 2][0:S, 0:KEYS], off[:], 1.0, 3e38,
                                                       ALU.add, ALU.min, least[:, h:h + 1]).then_inc(masked_ready, 1)

                    def copy_probs(h):
                        dve.wait_ge(probs_turned, CREDIT + first + h + 1)
                        dve.wait_ge(head_done, CREDIT + first + max(h - 1, 0))
                        nc.vector.tensor_copy(probsT[:, h % 2, :, :],
                                              psT[h % 2][:, 0:3 * S].rearrange("p (t s) -> p t s", t=3)).then_inc(probsT_ready, 1)

                    mask(0)
                    for h in range(HEADS):
                        if h + 1 < HEADS:
                            mask(h + 1)
                        copy_probs(h)
                        if layer == 1 and following is not None:
                            for kind in QK.get(h, ()):
                                if kind[0] in "qk":
                                    sum_squares(following, 0 if kind[0] == "q" else 1 + kind[1], kind[2])
                            if h in SCALE_AT:
                                scale(following, SCALE_AT[h])
                    dve.wait_ge(probs_ready, CREDIT + first + HEADS)
                    nc.vector.reciprocal(inv[:], total[:]).then_inc(inv_ready, 1)
                    dve.wait_ge(inv_ready, CREDIT + b + 1)
                    dve.wait_ge(head_done, CREDIT + first + HEADS)
                    for a in range(HALVES):
                        nh = HW // DH
                        ins_ = nc.vector.tensor_tensor(o[:, a * HW:(a + 1) * HW].rearrange("p (h d) -> p h d", d=DH),
                                                       psO[0:S, a, 0:HW].rearrange("p (h d) -> p h d", d=DH),
                                                       bcast(inv[:, a * nh:(a + 1) * nh], DH), ALU.mult)
                        if layer == 0:
                            ins_.then_inc(o_scaled, 1)
                            dve.wait_ge(o_scaled, CREDIT + b + 1)
                            nc.vector.tensor_tensor(o[:], o[:], bv[:], ALU.add).then_inc(o_ready, 1)
                        else:
                            ins_.then_inc(o_ready, 1)

                if layer == 1:
                    for t in range(4):
                        for a in range(2):
                            sum_squares(0, t, a)
                    for t in range(4):
                        scale(0, t)
                steps(dve, step)


def slot_shape(layer):
    return (HALF0, 2 * E0) if layer == 0 else (P, NBLK1 * BLK1 // P)


def route_phase(core, layer, logits, weights, slots, place, blocks=None):
    nc, ins = core.nc, core.ins
    E = E0 if layer == 0 else E1
    with Phase(core, f"route{layer}") as ph:
        sc, hot1, hot2, work = (ph.sb(n, [S, B, E]) for n in ("sc", "hot1", "hot2", "work"))
        rev, rev_i = ph.sb("rev", [P, E]), ph.sb("rev_i", [P, E], I32)
        top = ph.sb("top", [S, 8, B])
        m1, m2, r1, r2, t0, t1, t2, t3 = (top[:, k, :] for k in range(8))
        steps, ints, exped, asked_exp, loaded = (ph.sem(n) for n in ("steps", "ints", "exped", "asked_exp", "loaded"))
        counted, to_count = ph.sem("counted"), ph.sem("to_count")
        gate_b = ph.sb("gate_b", [S, E])
        if layer == 0:
            trash_i, trash = ph.sb("trash_i", [P, 1], I32), ph.sb("trash", [P, 1])
            turned = ph.sb("turned", [P, 3, 2, S])
            wT = ph.sb("wT", [E0, N])
            hotT = ph.sb("hotT", [E0, 2, N])
            stage = ph.sb("stage", [E0, 2, S])
            before = ph.sb("before", [S, 2 * N])
            above = ph.sb("above", [S, 2, 4, 400], BF16)
            rank = ph.sb("rank", [S, 2, B])
            staged, selected, ranked, before_ready = (ph.sem(n) for n in ("staged", "selected", "ranked", "before_ready"))
            out_turned, bounced, back, blank = (ph.sem(n) for n in ("out_turned", "bounced", "back", "blank"))
        else:
            part_i = ph.sb("part_i", [S, B], I32)
            tot = ph.sb("tot", [P, 3, B, E1])
            cnt = ph.sb("cnt", [P, 6, E1])
            jrow_i, jrow = ph.sb("jrow_i", [P, NBLK1], I32), ph.sb("jrow", [P, NBLK1])
            cmp = ph.sb("cmp", [P, NBLK1, E1])
            be = ph.sb("be", [P, 2, NBLK1])
            row_i, row = ph.sb("row_i", [P, 1], I32), ph.sb("row", [P, 1])
        carried = []
        with ExitStack() as first:
            psA, psB = (first.enter_context(nc.psum_tensor(f"route{layer}_{n}", [P, 512], F32)) for n in ("psA", "psB"))
            with nc.Block() as block:
                @block.sync
                def _(sync):
                    if layer == 0:
                        sync.dma_start(gate_b[:], ins["L0_ffn_gate_b"].partition_broadcast(S)).then_inc(loaded, 16)
                        sync.wait_ge(out_turned, 2)
                        for q in range(3):
                            for h in range(2):
                                sync.dma_start(core.bounce[q, h], turned[:, q, h, :]).then_inc(bounced, 16)
                        sync.wait_ge(bounced, 96)
                        back_view = core.bounce.rearrange("q h (t e) m -> q e (h t) m", e=E0)
                        sync.dma_start(wT[:].rearrange("e (t m) -> e t m", m=S), back_view[0]).then_inc(back, 16)
                        for k in range(2):
                            sync.dma_start(hotT[:, k, :].rearrange("e (t m) -> e t m", m=S), back_view[1 + k]).then_inc(back, 16)
                        sync.wait_ge(back, 48)

                @block.gpsimd
                def _(pool):
                    pool.iota(rev_i[:], [[-1, E]], base=E, channel_multiplier=0).then_inc(ints, 1)
                    if layer == 0:
                        pool.iota(trash_i[:], [[0, 1]], base=E0 * CAP0, channel_multiplier=1).then_inc(ints, 1)
                        pool.memset(before[:], 0.0).then_inc(blank, 1)
                        pool.wait_ge(blank, 1)
                        pool.affine_select(out=before[:], in_=before[:], compare_op=ALU.is_ge, fill=-1e-38,
                                           base=-N, pattern=[[1, 2 * N]], channel_multiplier=-1).then_inc(before_ready, 1)
                    else:
                        pool.iota(jrow_i[:], [[1, NBLK1]], base=0, channel_multiplier=0).then_inc(ints, 1)
                        pool.iota(row_i[:], [[0, 1]], base=0, channel_multiplier=1).then_inc(ints, 1)

                @block.scalar
                def _(act):
                    act.wait_ge(asked_exp, 1)
                    if layer == 0:
                        nc.scalar.activation(sc[:], work[:], ACT.Exp).then_inc(exped, 1)
                        act.wait_ge(counted, 1)
                        for q in range(3):
                            ps = (psA, psB)[q // 2]
                            ins_ = nc.scalar.copy(turned[:, q, :, :], ps[:, (q % 2) * 2 * S:(q % 2 + 1) * 2 * S].rearrange("p (h s) -> p h s", h=2))
                            if q:
                                ins_.then_inc(out_turned, 1)
                    else:
                        nc.scalar.activation(t1, t0, ACT.Exp).then_inc(exped, 1)

                @block.tensor
                def _(pe):
                    pe.wait_ge(to_count, 1)
                    if layer == 0:
                        for q, src in enumerate((work, hot1, hot2)):
                            for h in range(2):
                                a = ((q % 2) * 2 + h) * S
                                last = nc.tensor.transpose((psA, psB)[q // 2][:, a:a + S],
                                                           src[:, 8 * h:8 * h + 8, :].rearrange("p t e -> p (t e)"), core.ident[0:S, 0:S])
                    else:
                        a = work[:].rearrange("p t e -> p (t e)")
                        nc.tensor.matmul(psA[0:S, 0:B * E1], core.tri[0:S, 0:S], a, start=True, stop=True)
                        last = nc.tensor.matmul(psB[:, 0:B * E1], core.ones[0:S, :], a, start=True, stop=True)
                    last.then_inc(counted, 1)

                @block.vector
                def _(dve):
                    v = nc.vector
                    step = Steps(dve, steps)
                    carried.append(step)
                    dve.wait_ge(ints, 2 if layer == 0 else 3)
                    step.then(v.tensor_copy(rev[:], rev_i[:]))
                    if layer == 0:
                        step.then(v.tensor_copy(trash[:], trash_i[:]))
                        step.then(v.tensor_reduce(m1, logits, AX.X, ALU.max))
                        v.tensor_tensor(work[:], logits, bcast(m1, E), ALU.subtract).then_inc(asked_exp, 1)
                        dve.wait_ge(exped, 1)
                        step.then(v.tensor_reduce(t0, sc[:], AX.X, ALU.add))
                        step.then(v.reciprocal(t0, t0))
                        step.then(v.tensor_tensor(sc[:], sc[:], bcast(t0, E), ALU.mult))
                        dve.wait_ge(loaded, 16)
                        step.then(v.tensor_tensor(sc[:], sc[:], spread(gate_b[:], B), ALU.add))
                    else:
                        step.then(v.tensor_copy(jrow[:], jrow_i[:]))
                        step.then(v.tensor_copy(row[:], row_i[:]))
                        step.then(v.tensor_copy(sc[:], logits))
                    for m, r, hot in ((m1, r1, hot1), (m2, r2, hot2)):
                        step.then(v.tensor_reduce(m, sc[:], AX.X, ALU.max))
                        step.then(v.tensor_tensor(work[:], sc[:], bcast(m, E), ALU.is_equal))
                        step.then(v.tensor_tensor(work[:], work[:], spread(rev[0:S, :], B), ALU.mult))
                        step.then(v.tensor_reduce(r, work[:], AX.X, ALU.max))
                        step.then(v.tensor_tensor(hot[:], spread(rev[0:S, :], B), bcast(r, E), ALU.is_equal))
                        step.then(v.scalar_tensor_tensor(sc[:], hot[:], -BIG, sc[:], ALU.mult, ALU.add))
                    if layer == 0:
                        for k, hot in enumerate((hot1, hot2)):
                            step.then(v.tensor_tensor(work[:], hot[:], logits, ALU.mult))
                            step.then(v.tensor_reduce(weights[:, k, :], work[:], AX.X, ALU.add))
                        step.then(v.tensor_tensor(sc[:], hot1[:], hot2[:], ALU.add))
                        step.then(v.tensor_tensor(work[:], sc[:], logits, ALU.mult))
                        step.then(v.tensor_scalar(sc[:], sc[:], -1.0, BIG, ALU.add, ALU.mult))
                        v.tensor_tensor(work[:], work[:], sc[:], ALU.add).then_inc(to_count, 1)
                    else:
                        v.tensor_tensor(t0, m2, m1, ALU.subtract).then_inc(asked_exp, 1)
                        dve.wait_ge(exped, 1)
                        step.then(v.tensor_scalar(t2, t1, 1.0, None, ALU.add))
                        step.then(v.reciprocal(weights[:, 0, :], t2))
                        step.then(v.tensor_tensor(weights[:, 1, :], t1, weights[:, 0, :], ALU.mult))
                        v.tensor_tensor(work[:], hot1[:], hot2[:], ALU.add).then_inc(to_count, 1)
                        dve.wait_ge(counted, 1)
                        each = psB[:, 0:B * E1].rearrange("p (t e) -> p t e", e=E1)
                        inside = psA[0:S, 0:B * E1].rearrange("p (t e) -> p t e", e=E1)
                        step.then(v.tensor_copy(tot[:, 0], each))
                        a, b = 0, 1
                        for sh in (1, 2, 4, 8):
                            step.then(v.tensor_copy(tot[:, b, 0:sh], tot[:, a, 0:sh]))
                            step.then(v.tensor_tensor(tot[:, b, sh:], tot[:, a, sh:], tot[:, a, 0:B - sh], ALU.add))
                            a, b = b, a
                        count, nb, c0, c1, start, base = (cnt[:, k, :] for k in range(6))
                        step.then(v.tensor_copy(count, tot[:, a, B - 1]))
                        step.then(v.tensor_tensor(tot[:, 2], tot[:, a], each, ALU.subtract))
                        step.then(v.tensor_scalar(nb, count, 0.0, None, ALU.is_gt))
                        for j in range(1, MAXB1):
                            step.then(v.scalar_tensor_tensor(nb, count, float(BLK1 * j), nb, ALU.is_gt, ALU.add))
                        step.then(v.tensor_copy(c0, nb))
                        for sh in (1, 2, 4):
                            step.then(v.tensor_copy(c1[:, 0:sh], c0[:, 0:sh]))
                            step.then(v.tensor_tensor(c1[:, sh:], c0[:, sh:], c0[:, 0:E1 - sh], ALU.add))
                            c0, c1 = c1, c0
                        step.then(v.tensor_tensor(start, c0, nb, ALU.subtract))
                        step.then(v.tensor_scalar(base, start, float(BLK1), None, ALU.mult))
                        step.then(v.tensor_tensor(work[:], tot[0:S, 2], inside, ALU.add))
                        step.then(v.tensor_tensor(work[:], work[:], spread(base[0:S, :], B), ALU.add))
                        for k, hot in enumerate((hot1, hot2)):
                            step.then(v.tensor_tensor(sc[:], hot[:], work[:], ALU.mult))
                            step.then(v.tensor_reduce(t3, sc[:], AX.X, ALU.add))
                            step.then(v.tensor_copy(slots[:, k, :], t3))
                            for j, (op, by) in enumerate(((ALU.bitwise_and, P - 1), (ALU.logical_shift_right, 7))):
                                step.then(v.tensor_scalar(part_i[:], slots[:, k, :], by, None, op))
                                step.then(v.tensor_copy(place[:, j, k, :], part_i[:]))
                        step.then(v.tensor_tensor(cmp[:], bcast(jrow[:], E1), spread(c0, NBLK1), ALU.is_ge))
                        step.then(v.tensor_reduce(be[:, 0, :], cmp[:], AX.X, ALU.add))
                        step.then(v.tensor_scalar(be[:, 0, :], be[:, 0, :], float(E1 - 1), None, ALU.min))
                        step.then(v.tensor_scalar(be[:, 1, :], be[:, 0, :], float(P), row[:, 0:1], ALU.mult, ALU.add))
                        step.then(v.tensor_copy(blocks[:, 0, :], be[:, 1, :]))
                        step.then(v.tensor_copy(blocks[:, 1, :], be[:, 0, :]))
        if layer == 1:
            return

        psW = [ph.ps(f"psW{k}", [P, 4, 512]) for k in range(2)]
        ph.credit((staged, selected, ranked))
        with nc.Block() as block:
            @block.scalar
            def _(act):
                with act.Fori(0, B) as t:
                    act.wait_ge(selected, CREDIT + 2 * t)
                    nc.scalar.copy(stage[:], hotT[:, :, bass.ds(t * S, S)]).then_inc(staged, 1)

            @block.tensor
            def _(pe):
                with pe.Fori(0, B) as t:
                    pe.wait_ge(staged, CREDIT + t + 1)
                    for k in range(2):
                        pe.wait_ge(ranked, CREDIT + 2 * t)
                        for a in range(4):
                            last = nc.tensor.matmul(psW[k][0:S, a, 0:400], stage[:, k, :], wT[:, 400 * a:400 * a + 400],
                                                    start=True, stop=True)
                        last.then_inc(selected, 1)

            @block.vector
            def _(dve):
                v = nc.vector
                with dve.Fori(0, B) as t:
                    for k in range(2):
                        dve.wait_ge(ranked, CREDIT + 2 * t)
                        dve.wait_ge(selected, CREDIT + 2 * t + k + 1)
                        v.scalar_tensor_tensor(above[:, k], psW[k][0:S, :, 0:400], weights[:, k, bass.ds(t, 1)],
                                               before[:, bass.ds(N - t * S, N)].rearrange("p (a m) -> p a m", a=4),
                                               ALU.subtract, ALU.is_gt, accum_out=rank[:, k, bass.ds(t, 1)]).then_inc(ranked, 1)
                dve.wait_ge(ranked, CREDIT + 2 * B)
                step = Steps(dve, steps, carried[0].n)
                for k, r in enumerate((r1, r2)):
                    step.then(v.tensor_scalar(t1, rank[:, k, :], float(HALF0), None, ALU.is_ge))
                    step.then(v.scalar_tensor_tensor(place[:, 0, k, :], t1, -float(HALF0), rank[:, k, :], ALU.mult, ALU.add))
                    step.then(v.scalar_tensor_tensor(t2, r, -2.0, t1, ALU.mult, ALU.add))
                    step.then(v.tensor_scalar(t3, rank[:, k, :], float(CAP0), 2.0 * E0, ALU.is_ge, ALU.mult))
                    step.then(v.scalar_tensor_tensor(place[:, 1, k, :], t2, 2.0 * E0, t3, ALU.add, ALU.add))
                    step.then(v.tensor_scalar(t0, r, -float(CAP0), float(E0 * CAP0), ALU.mult, ALU.add))
                    step.then(v.tensor_tensor(t0, t0, rank[:, k, :], ALU.add))
                    step.then(v.tensor_scalar(t1, rank[:, k, :], float(CAP0), None, ALU.is_lt))
                    step.then(v.tensor_scalar(t0, t0, trash[0:S, :], None, ALU.subtract))
                    step.then(v.tensor_tensor(t0, t0, t1, ALU.mult))
                    step.then(v.tensor_scalar(t0, t0, trash[0:S, :], None, ALU.add))
                    step.then(v.tensor_copy(slots[:, k, :], t0))
                    step.then(v.tensor_tensor(weights[:, k, :], weights[:, k, :], t1, ALU.mult))


def invert_phase(core, layer, place, tokens):
    nc = core.nc
    LO, HI = slot_shape(layer)
    with Phase(core, f"invert{layer}") as ph:
        lo_i, lo_row = ph.sb("lo_i", [S, P], I32), ph.sb("lo_row", [S, P])
        id_i, ids = ph.sb("id_i", [S, B], I32), ph.sb("ids", [S, B])
        hot_lo, hot_hi = ph.sb("hot_lo", [S, 2 * B, LO]), ph.sb("hot_hi", [S, 2 * B, HI])
        psI = ph.ps("psI")
        ints, steps, hot_ready, found, stored = (ph.sem(n) for n in ("ints", "steps", "hot_ready", "found", "stored"))
        with nc.Block() as block:
            @block.sync
            def _(sync):
                sync.dma_start(core.rows.rearrange("(b s) d -> s b d", s=S), core.xn[:]).then_inc(stored, 16)
                sync.wait_ge(stored, 16)

            @block.gpsimd
            def _(pool):
                pool.iota(lo_i[:], [[1, P]], base=0, channel_multiplier=0).then_inc(ints, 1)
                pool.iota(id_i[:], [[S, B]], base=0, channel_multiplier=1).then_inc(ints, 1)

            @block.vector
            def _(dve):
                v = nc.vector
                step = Steps(dve, steps)
                dve.wait_ge(ints, 2)
                step.then(v.tensor_copy(lo_row[:], lo_i[:]))
                step.then(v.tensor_copy(ids[:], id_i[:]))
                lo, hi = (place[:, j].rearrange("p k t -> p (k t)") for j in range(2))
                v.tensor_tensor(hot_lo[:], spread(lo_row[:, 0:LO], 2 * B), bcast(lo, LO), ALU.is_equal).then_inc(hot_ready, 1)
                step.then(v.tensor_tensor(hot_hi[:], spread(lo_row[:, 0:HI], 2 * B), bcast(hi, HI), ALU.is_equal))
                for k in range(2):
                    h = hot_hi[:, k * B:(k + 1) * B, :]
                    v.tensor_tensor(h, h, bcast(ids[:], HI), ALU.mult).then_inc(hot_ready, 1)
                dve.wait_ge(found, 1)
                step.then(v.tensor_copy(tokens[0:LO, 0:HI], psI[0:LO, 0:HI]))

            @block.tensor
            def _(pe):
                pe.wait_ge(hot_ready, 3)
                for j in range(2 * B):
                    last = nc.tensor.matmul(psI[0:LO, 0:HI], hot_lo[:, j, :], hot_hi[:, j, :], start=j == 0, stop=j == 2 * B - 1)
                last.then_inc(found, 1)


def shared_phase(core, acc):
    nc, ins = core.nc, core.ins
    FC, Q = FF0 // P, 4
    NH = 2 * FC
    with Phase(core, "shared") as ph:
        w1, w3 = (ph.sb(n, [P, SHARED, KD, FF0]) for n in ("w1", "w3"))
        w2 = ph.sb("w2", [P, SHARED, FC, D])
        act1 = ph.sb("act1", [P, 2, Q * S])
        hid = ph.sb("hid", [P, NH, Q * S])
        ps1, ps3, psY = ([ph.ps(f"{n}{j}") for j in range(2)] for n in ("ps1", "ps3", "psY"))
        loaded, both, silu, hidden, y_ready, y_taken = (ph.sem(n) for n in ("loaded", "both", "silu", "hidden", "y_ready", "y_taken"))
        ph.credit()
        with nc.Block() as block:
            @block.sync
            def _(sync):
                for s in range(SHARED):
                    sync.dma_start(w1[:, s], ins["L0_ffn_sw1"][s].rearrange("(k p) f -> p k f", p=P)).then_inc(loaded, 16)
                    sync.dma_start(w3[:, s], ins["L0_ffn_sw3"][s].rearrange("(k p) f -> p k f", p=P)).then_inc(loaded, 16)
                    sync.dma_start(w2[:, s], ins["L0_ffn_sw2"][s].rearrange("(k p) f -> p k f", p=P)).then_inc(loaded, 16)

            @block.tensor
            def _(pe):
                pe.wait_ge(loaded, CREDIT + 16 * 3 * SHARED)
                with pe.Fori(0, B // Q) as i:
                    for j in range(NH):
                        s, f = divmod(j, FC)
                        pe.wait_ge(hidden, CREDIT + i * NH + max(j - 1, 0))
                        for w, ps in ((w1, ps1), (w3, ps3)):
                            for k in range(KD):
                                last = nc.tensor.matmul(ps[j % 2][:, 0:Q * S], w[:, s, k, f * P:(f + 1) * P],
                                                        core.xnT[:, k, bass.ds(i * Q * S, Q * S)], start=k == 0, stop=k == KD - 1)
                        last.then_inc(both, 1)
                    pe.wait_ge(hidden, CREDIT + (i + 1) * NH)
                    for q in range(Q):
                        pe.wait_ge(y_taken, CREDIT + i * Q + max(q - 1, 0))
                        for j in range(NH):
                            s, f = divmod(j, FC)
                            last = nc.tensor.matmul(psY[q % 2][0:S, 0:D], hid[:, j, q * S:(q + 1) * S], w2[:, s, f, :],
                                                    start=j == 0, stop=j == NH - 1)
                        last.then_inc(y_ready, 1)

            @block.scalar
            def _(act):
                with act.Fori(0, B // Q) as i:
                    for j in range(NH):
                        act.wait_ge(both, CREDIT + i * NH + j + 1)
                        act.wait_ge(hidden, CREDIT + i * NH + max(j - 1, 0))
                        nc.scalar.activation(act1[:, j % 2, :], ps1[j % 2][:, 0:Q * S], ACT.Silu).then_inc(silu, 1)

            @block.vector
            def _(dve):
                with dve.Fori(0, B // Q) as i:
                    dve.wait_ge(y_ready, CREDIT + i * Q)
                    for j in range(NH):
                        dve.wait_ge(silu, CREDIT + i * NH + j + 1)
                        nc.vector.tensor_tensor(hid[:, j, :], ps3[j % 2][:, 0:Q * S], act1[:, j % 2, :], ALU.mult).then_inc(hidden, 1)
                    for q in range(Q):
                        dve.wait_ge(y_ready, CREDIT + i * Q + q + 1)
                        nc.vector.tensor_scalar(acc[:, bass.ds(i * Q + q, 1), :].rearrange("p a d -> p (a d)"), psY[q % 2][0:S, 0:D],
                                                1.0 / SHARED, None, ALU.mult).then_inc(y_taken, 1)


def experts_phase(core, layer, tokens, blocks=None):
    nc, ins = core.nc, core.ins
    HALF = HALF0 if layer == 0 else BLK1 // 2
    SL = 2 * HALF
    NX = E0 if layer == 0 else NBLK1
    FF = FF0 if layer == 0 else FF1
    FC = FF // P
    result = core.result0 if layer == 0 else core.result1
    with Phase(core, f"experts{layer}") as ph:
        w1 = [ph.sb(f"w1_{q}", [P, KD, FF]) for q in range(2)]
        w2 = [ph.sb(f"w2_{q}", [P, FC, D]) for q in range(2)]
        xs = [ph.sb(f"xs{q}", [HALF, 2, D]) for q in range(2)]
        xsT = [ph.sb(f"xsT{q}", [P, KD, SL]) for q in range(2)]
        hid = [ph.sb(f"hid{q}", [P, FC, SL]) for q in range(2)]
        ys = [ph.sb(f"ys{q}", [HALF, 2, D]) for q in range(2)]
        act1 = ph.sb("act1", [P, 2, SL])
        ps1, ps3 = ([ph.ps(f"{n}{j}") for j in range(2)] for n in ("ps1", "ps3"))
        psX, psY = ([ph.ps(f"{n}{j}") for j in range(2)] for n in ("psX", "psY"))
        w_in, x_in = ([ph.plain(f"{n}{q}") for q in range(2)] for n in ("w_in", "x_in"))
        y_out, done = ([ph.sem(f"{n}{q}") for q in range(2)] for n in ("y_out", "done"))
        turned, xsT_ready, both, silu, hidden, y_ready, y_taken = (ph.sem(n) for n in (
            "turned", "xsT_ready", "both", "silu", "hidden", "y_ready", "y_taken"))
        passed, pool_passed, act_passed = ph.sem("passed"), ph.sem("pool_passed"), ph.sem("act_passed")
        if layer == 0:
            w3 = [ph.sb(f"w3_{q}", [P, KD, FF]) for q in range(2)]
        else:
            b1 = [ph.sb(f"b1_{q}", [P, FC]) for q in range(2)]
            b2 = [ph.sb(f"b2_{q}", [P, D]) for q in range(2)]
        NWHICH = 2 if layer == 0 else 4
        which = ph.sb("which", [P, 2, NWHICH, 1], I32)
        which_ready = ph.sem("which_ready")
        NW = 3 if layer == 0 else 4
        ph.credit()
        with nc.Block() as block:
            if layer == 0:
                @block.sync
                def _(sync):
                    with sync.Fori(0, NX // 2) as i:
                        for q in range(2):
                            sync.wait_ge(done[q], CREDIT + i)
                            sync.sem_inc(passed, 1)
                            for w, name in ((w1[q], "ew1"), (w3[q], "ew3"), (w2[q], "ew2")):
                                sync.dma_start(w[:], ins[f"L0_ffn_{name}"][bass.ds(2 * i + q, 1)].rearrange(
                                    "e (k p) f -> p (e k) f", p=P)).then_inc(w_in[q], 16)

            @block.gpsimd
            def _(pool):
                with pool.Fori(0, NX // 2) as i:
                    for q in range(2):
                        pool.wait_ge(done[q], CREDIT + i)
                        pool.sem_inc(pool_passed, 1)
                        for h in range(2):
                            pool.tensor_copy(which[0:HALF, q, h, :], tokens[0:HALF, bass.ds(4 * i + 2 * q + h, 1)]).then_inc(which_ready, 1)
                        if layer == 1:
                            for k in range(2):
                                pool.tensor_copy(which[:, q, 2 + k, :], blocks[:, k, bass.ds(2 * i + q, 1)]).then_inc(which_ready, 1)
                        pool.wait_ge(which_ready, CREDIT + (2 * i + q + 1) * NWHICH)
                        pool.sem_inc(pool_passed, 1)
                        for h in range(2):
                            pool.indirect_dma_start(xs[q][:, h, :], None, core.rows, bass.IndirectOffsetOnAxis(
                                ap=which[0:HALF, q, h, :], axis=0)).then_inc(x_in[q], 16)
                        if layer == 1:
                            for dst, src, k in ((w1[q][:].rearrange("p k f -> p (k f)"), ins["L1_ffn_w1"], 0),
                                                (b1[q][:], ins["L1_ffn_b1"], 0),
                                                (w2[q][:].rearrange("p k f -> p (k f)"), ins["L1_ffn_w2"], 0),
                                                (b2[q][:], ins["L1_ffn_b2"], 1)):
                                pool.indirect_dma_start(dst, None, src, bass.IndirectOffsetOnAxis(
                                    ap=which[:, q, 2 + k, :], axis=0)).then_inc(w_in[q], 16)

            @block.tensor
            def _(pe):
                with pe.Fori(0, NX // 2) as i:
                    for q in range(2):
                        n = 2 * i + q
                        pe.wait_ge(x_in[q], 32 * (i + 1))
                        pe.wait_ge(xsT_ready, CREDIT + n)
                        for k in range(KD):
                            for h in range(2):
                                last = nc.tensor.transpose(psX[q][:, k * SL + h * HALF:k * SL + (h + 1) * HALF],
                                                           xs[q][:, h, k * P:(k + 1) * P], core.ident[0:HALF, 0:HALF])
                        last.then_inc(turned, 1)
                        pe.wait_ge(w_in[q], 16 * NW * (i + 1))
                        pe.wait_ge(xsT_ready, CREDIT + n + 1)
                        for f in range(FC):
                            pe.wait_ge(hidden, CREDIT + n * FC + max(f - 1, 0))
                            for w, ps in ((w1, ps1), (w3, ps3)) if layer == 0 else ((w1, ps1),):
                                for k in range(KD):
                                    last = nc.tensor.matmul(ps[f % 2][:, 0:SL], w[q][:, k, f * P:(f + 1) * P],
                                                            xsT[q][:, k, :], start=k == 0, stop=k == KD - 1)
                            last.then_inc(both, 1)
                        pe.wait_ge(hidden, CREDIT + (n + 1) * FC)
                        pe.wait_ge(y_taken, CREDIT + n)
                        for h in range(2):
                            for f in range(FC):
                                last = nc.tensor.matmul(psY[q][0:HALF, h * D:(h + 1) * D], hid[q][:, f, h * HALF:(h + 1) * HALF],
                                                        w2[q][:, f, :], start=f == 0, stop=f == FC - 1)
                        last.then_inc(y_ready, 1)

            @block.scalar
            def _(act):
                with act.Fori(0, NX // 2) as i:
                    for q in range(2):
                        n = 2 * i + q
                        act.wait_ge(turned, CREDIT + n + 1)
                        nc.scalar.copy(xsT[q][:], psX[q][:, 0:KD * SL].rearrange("p (k s) -> p k s", k=KD)).then_inc(xsT_ready, 1)
                        for f in range(FC):
                            act.wait_ge(both, CREDIT + n * FC + f + 1)
                            if layer == 0:
                                act.wait_ge(hidden, CREDIT + n * FC + max(f - 1, 0))
                                nc.scalar.activation(act1[:, f % 2, :], ps1[f % 2][:, 0:SL], ACT.Silu).then_inc(silu, 1)
                            else:
                                act.wait_ge(y_ready, CREDIT + n)
                                nc.scalar.activation(hid[q][:, f, :], ps1[f % 2][:, 0:SL], ACT.Gelu,
                                                     bias=b1[q][:, f:f + 1]).then_inc(hidden, 1)
                        act.wait_ge(y_taken, CREDIT + n + 1)
                        act.sem_inc(act_passed, 1)
                        act.dma_start(result[bass.ds(n * SL, SL), :].rearrange("(h p) d -> p h d", p=HALF), ys[q][:]).then_inc(y_out[q], 16)
                for q in range(2):
                    act.wait_ge(y_out[q], CREDIT + 16 * (NX // 2))

            @block.vector
            def _(dve):
                with dve.Fori(0, NX // 2) as i:
                    for q in range(2):
                        n = 2 * i + q
                        if layer == 0:
                            dve.wait_ge(y_ready, CREDIT + n)
                            for f in range(FC):
                                dve.wait_ge(silu, CREDIT + n * FC + f + 1)
                                nc.vector.tensor_tensor(hid[q][:, f, :], ps3[f % 2][:, 0:SL], act1[:, f % 2, :], ALU.mult).then_inc(hidden, 1)
                        dve.wait_ge(y_out[q], CREDIT + 16 * i)
                        dve.wait_ge(y_ready, CREDIT + n + 1)
                        src = psY[q][0:HALF, 0:2 * D].rearrange("p (h d) -> p h d", h=2)
                        if layer == 0:
                            nc.vector.tensor_copy(ys[q][:], src).then_inc(y_taken, 1)
                        else:
                            nc.vector.tensor_tensor(ys[q][:], src, spread(b2[q][0:HALF, :], 2), ALU.add).then_inc(y_taken, 1)
                        dve.wait_ge(y_taken, CREDIT + n + 1)
                        dve.sem_inc(done[q], 1)


def combine_phase(core, layer, slots, weights, acc):
    nc, ins = core.nc, core.ins
    result = core.result0 if layer == 0 else core.result1
    with Phase(core, f"combine{layer}") as ph:
        ys = ph.sb("ys", [S, 2, B, D])
        sums = ph.sb("sums", [S, B, D])
        fetched, summed, loaded, stored = ph.plain("fetched"), ph.sem("summed"), ph.sem("loaded"), ph.sem("stored")
        stats_done, moments, rstd_ready, pool_steps, normed = (ph.sem(n) for n in ("stats_done", "moments", "rstd_ready", "pool_steps", "normed"))
        ln_w, ln_b = ph.sb("ln_w", [S, D]), ph.sb("ln_b", [S, D])
        stats, work = ph.sb("stats", [S, B, 6]), ph.sb("work", [S, 4, B])
        mean, rstd, t0, t1 = (work[:, k, :] for k in range(4))
        ph.credit()
        gate = core.gates[0:S, 2 + layer:3 + layer]

        def tile(buf, i):
            return buf[:, bass.ds(i, 1), :].rearrange("p a d -> p (a d)")

        with nc.Block() as block:
            @block.gpsimd
            def _(pool):
                for t in range(B):
                    for k in range(2):
                        pool.indirect_dma_start(ys[:, k, t, :], None, result,
                                                bass.IndirectOffsetOnAxis(ap=slots[:, k, t:t + 1], axis=0)).then_inc(fetched, 16)
                if layer == 1:
                    step = Steps(pool, pool_steps, CREDIT)
                    pool.wait_ge(moments, CREDIT + 6)
                    step.then(pool.tensor_scalar(t1, t1, LAST_EPS, None, ALU.add))
                    pool.tensor_tensor(rstd, t1, core.half[0:S, 0:B], ALU.pow).then_inc(rstd_ready, 1)

            @block.vector
            def _(dve):
                v = nc.vector
                dve.wait_ge(fetched, 16 * 2 * B)
                if layer == 1:
                    dve.wait_ge(loaded, CREDIT + 32)
                with dve.Fori(0, B) as t:
                    PER = 3
                    for k in range(2):
                        v.scalar_tensor_tensor(tile(sums, t), ys[:, k, bass.ds(t, 1), :].rearrange("p a d -> p (a d)"),
                                               weights[:, k, bass.ds(t, 1)], tile(acc if k == 0 else sums, t), ALU.mult, ALU.add).then_inc(summed, 1)
                        dve.wait_ge(summed, CREDIT + t * PER + k + 1)
                    if layer == 0:
                        v.scalar_tensor_tensor(tile(core.x, t), tile(sums, t), gate, tile(core.x, t), ALU.mult, ALU.add).then_inc(summed, 1)
                    else:
                        v.bn_stats(stats[:, t, :], tile(sums, t)).then_inc(summed, 1)
                if layer == 1:
                    dve.wait_ge(summed, CREDIT + PER * B)
                    step = Steps(dve, moments, CREDIT)
                    me, ve, mo, vo = (stats[:, :, k] for k in (1, 2, 4, 5))
                    step.then(v.tensor_tensor(mean, me, mo, ALU.add))
                    step.then(v.tensor_scalar(mean, mean, 0.5, None, ALU.mult))
                    step.then(v.tensor_tensor(t0, me, mo, ALU.subtract))
                    step.then(v.scalar_tensor_tensor(t0, t0, 0.25, t0, ALU.mult, ALU.mult))
                    step.then(v.tensor_tensor(t1, ve, vo, ALU.add))
                    step.then(v.scalar_tensor_tensor(t1, t1, 1.0 / D, t0, ALU.mult, ALU.add))
                    dve.wait_ge(rstd_ready, CREDIT + 1)
                    with dve.Fori(0, B) as t:
                        step = Steps(dve, normed, CREDIT + t * 4)
                        step.then(v.tensor_scalar(tile(sums, t), tile(sums, t), work[:, 0, bass.ds(t, 1)], work[:, 1, bass.ds(t, 1)],
                                                  ALU.subtract, ALU.mult))
                        step.then(v.tensor_tensor(tile(sums, t), tile(sums, t), ln_w[:], ALU.mult))
                        step.then(v.tensor_tensor(tile(sums, t), tile(sums, t), ln_b[:], ALU.add))
                        v.scalar_tensor_tensor(tile(core.x, t), tile(sums, t), gate, tile(core.x, t), ALU.mult, ALU.add).then_inc(normed, 1)

            @block.sync
            def _(sync):
                if layer == 1:
                    sync.dma_start(ln_w[:], ins["L1_ffn_ln_w"].partition_broadcast(S)).then_inc(loaded, 16)
                    sync.dma_start(ln_b[:], ins["L1_ffn_ln_b"].partition_broadcast(S)).then_inc(loaded, 16)
                    for h in range(2):
                        sync.wait_ge(normed, CREDIT + 4 * B * (h + 1) // 2)
                        sync.dma_start(core.out[8 * h:8 * h + 8].rearrange("b s d -> s b d"), core.x[:, 8 * h:8 * h + 8, :]).then_inc(stored, 16)
                    sync.wait_ge(stored, CREDIT + 32)




def program(nc, ins, out):
    with ExitStack() as ctx:
        core = Core(nc, ctx, ins, out)
        setup_phase(core)
        weights = ctx.enter_context(nc.sbuf_tensor("weights", [S, 2, B], F32))
        slots = ctx.enter_context(nc.sbuf_tensor("slots", [S, 2, B], I32))
        blocks = ctx.enter_context(nc.sbuf_tensor("blocks", [P, 2, NBLK1], I32))
        place = ctx.enter_context(nc.sbuf_tensor("place", [S, 2, 2, B], F32))
        tokens = ctx.enter_context(nc.sbuf_tensor("tokens", [P, NBLK1 * BLK1 // P], I32))
        logits0 = ctx.enter_context(nc.sbuf_tensor("logits0", [S, B, E0], F32))
        logits1 = ctx.enter_context(nc.sbuf_tensor("logits1", [S, B, E1], F32))
        norm_phase(core, "norm_a0")
        attention_phase(core, 0)
        with ExitStack() as layer0:
            core.xn = layer0.enter_context(nc.sbuf_tensor("x_normed0", [S, B, D], F32))
            acc = layer0.enter_context(nc.sbuf_tensor("shared_acc", [S, B, D], F32))
            norm_phase(core, "norm_f0", (ins["L0_ffn_gate_w"], None, logits0))
            route_phase(core, 0, logits0[:], weights, slots, place)
            invert_phase(core, 0, place, tokens)
            shared_phase(core, acc)
            experts_phase(core, 0, tokens)
            combine_phase(core, 0, slots, weights, acc)
        core.xn = None
        norm_phase(core, "norm_a1")
        attention_phase(core, 1)
        with ExitStack() as layer1:
            core.xn = layer1.enter_context(nc.sbuf_tensor("x_normed1", [S, B, D], F32))
            norm_phase(core, "norm_f1", (ins["L1_ffn_router_w"], ins["L1_ffn_router_b"], logits1))
            route_phase(core, 1, logits1[:], weights, slots, place, blocks)
            invert_phase(core, 1, place, tokens)
            experts_phase(core, 1, tokens, blocks)
            combine_phase(core, 1, slots, weights, core.xn)


def kernel(**inputs):
    import numpy as np
    import concourse.bacc as bacc
    from concourse.bass_utils import run_bass_kernel_spmd

    lay = {
        "ctx_1024": lambda a: a.transpose(0, 2, 1),
        "L0_xattn_bq": lambda a: a.reshape(-1, P).T,
        "L0_xattn_bk": lambda a: a.reshape(-1, P).T,
        "L1_ffn_router_w": lambda a: a.T,
        "L1_ffn_w1": lambda a: a.transpose(0, 2, 1).reshape(E1, KD, P, FF1).transpose(0, 2, 1, 3).reshape(E1 * P, KD * FF1),
        "L1_ffn_b1": lambda a: a.reshape(E1, FF1 // P, P).transpose(0, 2, 1).reshape(E1 * P, FF1 // P),
        "L1_ffn_w2": lambda a: a.transpose(0, 2, 1).reshape(E1, FF1 // P, P, D).transpose(0, 2, 1, 3).reshape(E1 * P, FF1 // P * D),
    }
    nc = bacc.Bacc("TRN2", target_bir_lowering=False, num_devices=1)
    arrays, ins = {}, {}
    for name, value in inputs.items():
        a = np.asarray(value)
        a = np.ascontiguousarray(lay[name](a) if name in lay else a)
        arrays[f"in_{name}_dram"] = a
        ins[name] = nc.dram_tensor(f"in_{name}_dram", a.shape, mybir.dt.from_np(a.dtype), kind="ExternalInput").ap()
    out = nc.dram_tensor("out_dram", (B, S, D), F32, kind="ExternalOutput").ap()
    program(nc, ins, out)
    r = run_bass_kernel_spmd(nc, [arrays], core_ids=[0])
    return r.results[0]["out_dram"]
```

```python
from contextlib import ExitStack

import concourse.bass as bass
from concourse import mybir

ALU = mybir.AluOpType
ACT = mybir.ActivationFunctionType
AX = mybir.AxisListType
F32 = mybir.dt.float32
BF16 = mybir.dt.bfloat16
I32 = mybir.dt.int32
U8 = mybir.dt.uint8

P = 128
B, S, D = 16, 100, 256
N = B * S
KD = D // P
KEYS = 361
KEY_TILES = [(0, 128), (128, 128), (256, KEYS - 256)]
HEADS = 16
LN_EPS, RMS_EPS, LAST_EPS = 1e-5, 1e-5, 1e-12
CREDIT = 1
MASKED = 1e18
BIG = 1e30

E0, FF0, SHARED = 16, 512, 2
CAP0 = -(-N * 2 // E0 * 5 // 4)
HALF0 = CAP0 // 2
E1, FF1 = 8, 1024
BLK1 = 256
NBLK1 = (2 * N + E1 * (BLK1 - 1)) // BLK1
MAXB1 = -(-N // BLK1)


class Steps:

    def __init__(self, eng, sem, base=0):
        self.eng, self.sem, self.base, self.n = eng, sem, base, 0

    def then(self, ins):
        self.n += 1
        ins.then_inc(self.sem, 1)
        self.eng.wait_ge(self.sem, self.base + self.n)


def bcast(ap, n):
    return ap.unsqueeze(len(ap.shape)).to_broadcast([*ap.shape, n])


def spread(ap, n):
    return ap.unsqueeze(1).to_broadcast([ap.shape[0], n, *ap.shape[1:]])


class Core:

    def __init__(self, nc, ctx, ins, out):
        self.nc, self.ins, self.out = nc, ins, out

        def sb(name, shape, dt=F32):
            return ctx.enter_context(nc.sbuf_tensor(name, shape, dt))

        self.x = sb("x_tokens", [S, B, D])
        self.xn = None
        self.xnT = sb("x_normed_T", [P, KD, N])
        self.ident = sb("identity", [P, P])
        self.ones = sb("ones", [P, P])
        self.tri = sb("tri_before", [P, P])
        self.gates = sb("gates", [P, 4])
        self.half = sb("minus_half", [P, 64])
        self.rows = nc.dram_tensor("rows_dram", [N, D], F32, kind="Internal").ap()
        self.result0 = nc.dram_tensor("results0_dram", [E0 * CAP0 + P, D], F32, kind="Internal").ap()
        self.result1 = nc.dram_tensor("results1_dram", [NBLK1 * BLK1, D], F32, kind="Internal").ap()
        self.bounce = nc.dram_tensor("turn_dram", [5, 2, P, S], BF16, kind="Internal").ap()


class Phase:

    def __init__(self, core, name):
        self.core, self.nc, self.name, self.ctx = core, core.nc, name, ExitStack()
        self.sems, self.all_sems = [], []

    def __enter__(self):
        return self

    def __exit__(self, *a):
        self.nc.clear_and_free_semaphores(self.all_sems)
        self.nc.all_engine_barrier()
        return self.ctx.__exit__(*a)

    def sb(self, name, shape, dt=F32):
        return self.ctx.enter_context(self.nc.sbuf_tensor(f"{self.name}_{name}", shape, dt))

    def ps(self, name, shape=(P, 512), dt=F32):
        return self.ctx.enter_context(self.nc.psum_tensor(f"{self.name}_{name}", list(shape), dt))

    def sem(self, name):
        s = self.plain(name)
        self.sems.append(s)
        return s

    def plain(self, name):
        s = self.nc.alloc_semaphore(f"{self.name}_{name}")
        self.all_sems.append(s)
        return s

    def credit(self, sems=None):
        with self.nc.Block() as block:
            @block.sync
            def _(sync):
                for s in sems or self.sems:
                    sync.sem_inc(s, CREDIT)


class AttentionWeights:

    def __init__(self, core, ctx, layer):
        nc, W = core.nc, HEADS * (16, 64)[layer]
        self.core, self.pre = core, f"L{layer}_xattn_"
        self.raw, self.wq, self.wo = (ctx.enter_context(nc.sbuf_tensor(f"{self.pre}{n}", shape, F32)) for n, shape in (
            ("raw", [P, 4, W]), ("wq", [P, KD, W]), ("wo", [P, W // P, D])))
        self.kv_in = [nc.alloc_semaphore(f"{self.pre}{n}_in") for n in ("Wk", "Wv")]
        self.qo_in = nc.alloc_semaphore(f"{self.pre}WqWo_in")

    def load(self, sync):
        def dram(name):
            return self.core.ins[self.pre + name].rearrange("(k p) n -> p k n", p=P)

        for n, name in enumerate(("Wk", "Wv")):
            sync.dma_start(self.raw[:, 2 * n:2 * n + 2, :], dram(name)).then_inc(self.kv_in[n], 16)
        for buf, name in ((self.wq, "Wq"), (self.wo, "Wo")):
            sync.dma_start(buf[:], dram(name)).then_inc(self.qo_in, 16)


class SharedWeights:

    def __init__(self, core, ctx):
        self.core, nc = core, core.nc
        self.w1, self.w3, self.w2 = (ctx.enter_context(nc.sbuf_tensor(f"shared_{n}", shape, F32)) for n, shape in (
            ("w1", [P, SHARED, KD, FF0]), ("w3", [P, SHARED, KD, FF0]), ("w2", [P, SHARED, FF0 // P, D])))
        self.loaded = nc.alloc_semaphore("shared_loaded")

    def load(self, sync):
        for s in range(SHARED):
            for buf, name in ((self.w1, "sw1"), (self.w3, "sw3"), (self.w2, "sw2")):
                sync.dma_start(buf[:, s], self.core.ins[f"L0_ffn_{name}"][s].rearrange("(k p) f -> p k f", p=P)).then_inc(self.loaded, 16)


class Ranking:
    STEPS, HALF = 16, N // 2

    def __init__(self, core, ctx):
        self.core, self.nc = core, core.nc

        def sb(name, shape, dt=F32):
            return ctx.enter_context(core.nc.sbuf_tensor(f"ranking_{name}", shape, dt))

        self.wT = sb("wT", [3 * E0, N], BF16)
        self.hotT = sb("hotT", [3 * E0, 2, N], BF16)
        self.before = sb("before", [S, 2 * N])
        self.above = sb("above", [S, self.HALF], BF16)
        self.counts = sb("counts", [S, 2, 2, B])
        self.trash, self.r1, self.r2 = sb("trash", [P, 1]), sb("r1", [S, B]), sb("r2", [S, B])
        self.temps = sb("temps", [S, 5, B])

    def use(self, ph, weights):
        self.ps, self.weights = ph.ps("psR", [P, 2, 512]), weights
        self.selected, self.ranked, self.passed = ph.sem("selected"), ph.sem("ranked"), ph.sem("passed")

    def which(self, n, u):
        return n * self.STEPS + u, n * 4 + u // 4, u // 2 % 2, u % 2

    def select(self, pe, n, u):
        number, tile, k, half = self.which(n, u)
        pe.wait_ge(self.ranked, CREDIT + number)
        pe.sem_inc(self.passed, 1)
        for a in range(2):
            first = half * self.HALF + a * 400
            last = self.nc.tensor.matmul(self.ps[0:S, a, 0:400], self.hotT[:, k, bass.ds(tile * S, S)],
                                         self.wT[:, first:first + 400], start=True, stop=True)
        last.then_inc(self.selected, 1)

    def compare(self, dve, n, u):
        number, tile, k, half = self.which(n, u)
        dve.wait_ge(self.selected, CREDIT + number + 1)
        self.nc.vector.scalar_tensor_tensor(
            self.above[:].rearrange("p (a m) -> p a m", a=2), self.ps[0:S, :, 0:400], self.weights[:, k, bass.ds(tile, 1)],
            self.before[:, bass.ds(N - tile * S + half * self.HALF, self.HALF)].rearrange("p (a m) -> p a m", a=2),
            ALU.subtract, ALU.is_gt, accum_out=self.counts[:, half, k, bass.ds(tile, 1)]).then_inc(self.ranked, 1)

    def place(self, v, step, slots, place):
        weights = self.weights
        t0, t1, t2, t3, rank = (self.temps[:, k, :] for k in range(5))
        for k, r in enumerate((self.r1[:], self.r2[:])):
            step.then(v.tensor_tensor(rank, self.counts[:, 0, k, :], self.counts[:, 1, k, :], ALU.add))
            step.then(v.tensor_scalar(t1, rank, float(HALF0), None, ALU.is_ge))
            step.then(v.scalar_tensor_tensor(place[:, 0, k, :], t1, -float(HALF0), rank, ALU.mult, ALU.add))
            step.then(v.scalar_tensor_tensor(t2, r, -2.0, t1, ALU.mult, ALU.add))
            step.then(v.tensor_scalar(t3, rank, float(CAP0), 2.0 * E0, ALU.is_ge, ALU.mult))
            step.then(v.scalar_tensor_tensor(place[:, 1, k, :], t2, 2.0 * E0, t3, ALU.add, ALU.add))
            step.then(v.tensor_scalar(t0, r, -float(CAP0), float(E0 * CAP0), ALU.mult, ALU.add))
            step.then(v.tensor_tensor(t0, t0, rank, ALU.add))
            step.then(v.tensor_scalar(t1, rank, float(CAP0), None, ALU.is_lt))
            step.then(v.tensor_scalar(t0, t0, self.trash[0:S, :], None, ALU.subtract))
            step.then(v.tensor_tensor(t0, t0, t1, ALU.mult))
            step.then(v.tensor_scalar(t0, t0, self.trash[0:S, :], None, ALU.add))
            step.then(v.tensor_copy(slots[:, k, :], t0))
            step.then(v.tensor_tensor(weights[:, k, :], weights[:, k, :], t1, ALU.mult))


def setup_phase(core):
    nc = core.nc
    with Phase(core, "setup") as ph:
        zeros = ph.sb("zeros", [P, D])
        g_raw = ph.sb("g_raw", [P, 4])
        loaded, cleared = ph.sem("loaded"), ph.sem("cleared")
        zeros_ready, blanks, shapes = ph.sem("zeros_ready"), ph.sem("blanks"), ph.sem("shapes")
        gates_ready = ph.sem("gates_ready")
        with nc.Block() as block:
            @block.sync
            def _(sync):
                sync.dma_start(core.x[:], core.ins["x"].rearrange("b s d -> s b d")).then_inc(loaded, 16)
                for j, g in enumerate(("g_xattn", "g_ffn")):
                    sync.dma_start(g_raw[:, 2 * j:2 * j + 2], core.ins[g].partition_broadcast(P)).then_inc(loaded, 16)
                sync.wait_ge(zeros_ready, 1)
                sync.dma_start(core.result0[E0 * CAP0:], zeros[:]).then_inc(cleared, 16)
                sync.wait_ge(cleared, 16)
                sync.wait_ge(loaded, 48)

            @block.gpsimd
            def _(pool):
                pool.memset(core.ident[:], 0.0).then_inc(blanks, 1)
                pool.memset(core.tri[:], 0.0).then_inc(blanks, 1)
                pool.memset(core.ones[:], 1.0).then_inc(blanks, 1)
                pool.memset(core.half[:], -0.5).then_inc(blanks, 1)
                pool.wait_ge(blanks, 4)
                pool.affine_select(out=core.ident[:], in_=core.ident[:], compare_op=ALU.not_equal, fill=1.0,
                                   base=0, pattern=[[-1, P]], channel_multiplier=1).then_inc(shapes, 1)
                pool.affine_select(out=core.tri[:], in_=core.tri[:], compare_op=ALU.is_ge, fill=1.0,
                                   base=0, pattern=[[-1, P]], channel_multiplier=1).then_inc(shapes, 1)
                pool.wait_ge(shapes, 2)

            @block.vector
            def _(dve):
                nc.vector.memset(zeros[:], 0.0).then_inc(zeros_ready, 1)

            @block.scalar
            def _(act):
                act.wait_ge(loaded, 48)
                nc.scalar.activation(core.gates[:], g_raw[:], ACT.Tanh).then_inc(gates_ready, 1)
                act.wait_ge(gates_ready, 1)


def norm_phase(core, name, router=None, following=None):
    nc = core.nc
    with Phase(core, name) as ph:
        stats = ph.sb("stats", [S, B, 6])
        work = ph.sb("work", [S, 4, B])
        mean, rstd, t0, t1 = (work[:, k, :] for k in range(4))
        stage = ph.sb("stage", [S, 2, D])
        turned = ph.sb("turned", [P, 2, KD, S])
        psT = [ph.ps(f"psT{j}") for j in range(2)]
        psL = [ph.ps(f"psL{j}") for j in range(2)]
        stats_done, moments, rstd_ready = ph.sem("stats_done"), ph.sem("moments"), ph.sem("rstd_ready")
        normed, turned_ps, copied = ph.sem("normed"), ph.sem("turned_ps"), ph.sem("copied")
        scored, scores_copied, w_loaded = ph.sem("scored"), ph.sem("scores_copied"), ph.sem("w_loaded")
        pool_steps, kept, bank_out = ph.sem("pool_steps"), ph.sem("kept"), ph.sem("bank_out")
        if router:
            w_dram, b_dram, logits = router
            E = logits.shape[2]
            w_sb = ph.sb("w", [P, KD, E])
            b_sb = ph.sb("b", [S, E])

        ph.credit()
        with nc.Block() as block:
            @block.sync
            def _(sync):
                if router:
                    sync.dma_start(w_sb[:], w_dram.rearrange("(k p) e -> p k e", p=P)).then_inc(w_loaded, 16)
                    if b_dram is not None:
                        sync.dma_start(b_sb[:], b_dram.partition_broadcast(S)).then_inc(w_loaded, 16)
                if following is not None:
                    following.load(sync)

            @block.vector
            def _(dve):
                with dve.Fori(0, B) as i:
                    nc.vector.bn_stats(stats[:, i, :], core.x[:, i, :]).then_inc(stats_done, 1)
                dve.wait_ge(stats_done, CREDIT + B)
                step = Steps(dve, moments, CREDIT)
                me, ve, mo, vo = (stats[:, :, k] for k in (1, 2, 4, 5))
                step.then(nc.vector.tensor_tensor(mean, me, mo, ALU.add))
                step.then(nc.vector.tensor_scalar(mean, mean, 0.5, None, ALU.mult))
                step.then(nc.vector.tensor_tensor(t0, me, mo, ALU.subtract))
                step.then(nc.vector.scalar_tensor_tensor(t0, t0, 0.25, t0, ALU.mult, ALU.mult))
                step.then(nc.vector.tensor_tensor(t1, ve, vo, ALU.add))
                step.then(nc.vector.scalar_tensor_tensor(t1, t1, 1.0 / D, t0, ALU.mult, ALU.add))
                dve.wait_ge(rstd_ready, CREDIT + 1)

                def norm(j):
                    for q in range(2):
                        t = 2 * j + q
                        dve.wait_ge(turned_ps, CREDIT + 2 * j)
                        if core.xn is not None:
                            dve.wait_ge(kept, CREDIT + 2 * j)
                        at = slice(t, t + 1) if isinstance(j, int) else bass.ds(t, 1)
                        nc.vector.tensor_scalar(stage[:, q, :], core.x[:, at, :].rearrange("p a d -> p (a d)"), work[:, 0, at],
                                                work[:, 1, at], ALU.subtract, ALU.mult).then_inc(normed, 1)

                def take_logits(j):
                    for q in range(2):
                        t = 2 * j + q
                        dve.wait_ge(scored, CREDIT + t + 1)
                        dst = logits[:, t, :]
                        if b_dram is not None:
                            dve.wait_ge(w_loaded, CREDIT + 32)
                            nc.vector.tensor_tensor(dst, psL[q][0:S, 0:E], b_sb[:], ALU.add).then_inc(scores_copied, 1)
                        else:
                            nc.vector.tensor_copy(dst, psL[q][0:S, 0:E]).then_inc(scores_copied, 1)

                norm(0)
                with dve.Fori(1, B // 2) as j:
                    norm(j)
                    if router:
                        take_logits(j - 1)
                if router:
                    take_logits(B // 2 - 1)

            @block.gpsimd
            def _(pool):
                step = Steps(pool, pool_steps, CREDIT)
                pool.wait_ge(moments, CREDIT + 6)
                step.then(pool.tensor_scalar(t1, t1, LN_EPS, None, ALU.add))
                pool.tensor_tensor(rstd, t1, core.half[0:S, 0:B], ALU.pow).then_inc(rstd_ready, 1)

            @block.tensor
            def _(pe):
                if router:
                    pe.wait_ge(w_loaded, CREDIT + (32 if b_dram is not None else 16))

                def turn(j):
                    for q in range(2):
                        pe.wait_ge(normed, CREDIT + 2 * j + q + 1)
                        pe.wait_ge(bank_out, CREDIT + 2 * j)
                        for k in range(KD):
                            last = nc.tensor.transpose(psT[q][:, k * S:(k + 1) * S], stage[:, q, k * P:(k + 1) * P],
                                                       core.ident[0:S, 0:S])
                        last.then_inc(turned_ps, 1)

                def score(j):
                    for q in range(2):
                        pe.wait_ge(copied, CREDIT + 2 * j + q + 1)
                        pe.wait_ge(scores_copied, CREDIT + 2 * j)
                        for k in range(KD):
                            last = nc.tensor.matmul(psL[q][0:S, 0:E], turned[:, q, k, :], w_sb[:, k, :],
                                                    start=k == 0, stop=k == KD - 1)
                        last.then_inc(scored, 1)

                turn(0)
                with pe.Fori(1, B // 2) as j:
                    if router:
                        score(j - 1)
                    turn(j)
                if router:
                    score(B // 2 - 1)

            @block.scalar
            def _(act):
                with act.Fori(0, B // 2) as j:
                    for q in range(2):
                        if core.xn is not None:
                            act.wait_ge(normed, CREDIT + 2 * j + q + 1)
                            nc.scalar.copy(core.xn[:, 2 * j + q, :], stage[:, q, :]).then_inc(kept, 1)
                    for q in range(2):
                        act.wait_ge(turned_ps, CREDIT + 2 * j + q + 1)
                        src = psT[q][:, 0:KD * S].rearrange("p (k s) -> p k s", k=KD)
                        if router:
                            act.wait_ge(scored, CREDIT + 2 * j)
                            nc.scalar.copy(turned[:, q, :, :], src).then_inc(copied, 1)
                        nc.scalar.copy(core.xnT[:, :, bass.ds((2 * j + q) * S, S)], src).then_inc(bank_out, 1)


class TableLoad:

    def __init__(self, ph, function):
        self.nc, self.half, self.function = ph.nc, ph.core.half, function
        self.scratch, self.done = ph.sb("table_scratch", [P, 1]), ph.sem("table_done")

    def ahead(self, act, n):
        act.wait_ge(self.done, CREDIT + n)
        self.nc.scalar.activation(self.scratch[:], self.half[:, 0:1], self.function).then_inc(self.done, 2)


class Count:

    def __init__(self, base=0, odd=0):
        self.base, self.odd, self.n = base, odd, 0

    def next(self):
        n = self.n
        self.n += 1
        return self.base + n, (self.odd + n) % 2

    def one_before_last(self, n):
        if isinstance(n, int):
            return CREDIT + max(n - 1, 0)
        return CREDIT + n - 1


def three_products(nc, out, left, right, start, stop):
    (left_high, left_low), (right_high, right_low) = left, right
    nc.tensor.matmul(out, left_high, right_high, start=start, stop=False)
    nc.tensor.matmul(out, left_high, right_low, start=False, stop=False)
    return nc.tensor.matmul(out, left_low, right_high, start=False, stop=stop)


def attention_phase(core, layer, given):
    nc, ins = core.nc, core.ins
    pre = f"L{layer}_xattn_"
    DH = 16 if layer == 0 else 64
    W = HEADS * DH
    WC = W // P
    HALVES = max(1, W // 512)
    HW = min(W, 512)
    EVEN = KEYS + 1
    if layer == 0:
        QK = {0: [("q", 0)], 1: [("q", 1)], 2: [("k", 0)], 3: [("k", 1)]}
    else:
        QK = {0: [("q", 0, 0), ("q", 0, 1)]}
        for j in range(6):
            QK[j + 1] = [("k", j // 2, j % 2)]
        QK |= {8: [("tq", 0)], 9: [("tq", 1)], 11: [("tk", 0), ("tk", 1)], 12: [("tk", 2), ("tk", 3)],
               13: [("tk", 4), ("tk", 5)], 14: [("tk", 6)], 15: [("tk", 7)]}
        SCALE_AT = {5: 0, 7: 1, 8: 2, 9: 3}
    V = [("v", t, a) for t in range(3) for a in range(HALVES)]
    V1, V2, V3 = V[:HALVES], V[HALVES:2 * HALVES], V[2 * HALVES:]
    BEFORE_O, AFTER_O = (V2, []) if layer == 0 else (V2[:1], V2[1:])
    AHEAD = 2 if layer == 0 else 1
    NQK = sum(map(len, QK.values()))
    PER = NQK + len(V) + HALVES + 1
    FIRST = NQK + 2 * HALVES

    with Phase(core, f"attn{layer}") as ph:
        R = mybir.dt.float32r
        wq, wo, stage = given.wq, given.wo, given.raw
        wk, wv = ([ph.sb(f"{n}_{part}", [P, KD, W], R) for part in ("high", "low")] for n in ("wk", "wv"))
        ctx_raw = ph.sb("ctx_raw", [P, KD, KEYS])
        ctxT = [[ph.sb(f"ctxT{q}_{part}", [P, KD, EVEN], R) for part in ("high", "low")] for q in range(2)]
        PARTS = ("high", "low") if layer == 0 else ("whole",)
        T = R if layer == 0 else F32
        kT = [[ph.sb(f"kT{q}_{part}", [P, WC, EVEN if layer == 0 else KEYS], T) for part in PARTS] for q in range(2)]
        v = [ph.sb(f"v{q}", [P, 3, W]) for q in range(2)]
        off = ph.sb("off", [S, KEYS])
        masked = ph.sb("masked", [S, 2, KEYS])
        probs = ph.sb("probs", [S, 2, KEYS])
        probsT = ph.sb("probsT", [P, 2, 3, S])
        least = ph.sb("least", [S, HEADS])
        total = ph.sb("total", [S, HEADS])
        inv = ph.sb("inv", [S, HEADS])
        o = ph.sb("o", [S, W])
        oT = ph.sb("oT", [P, WC, S])
        y = ph.sb("y", [S, D])
        table = TableLoad(ph, ACT.Exp)
        IN_CHUNK = P // DH
        qT = [[ph.sb(f"qT{q}_{part}", [P, WC, IN_CHUNK, S], T) for part in PARTS] for q in range(2)]
        pick = ph.sb("pick", [P, IN_CHUNK])
        psP = [ph.ps(f"psP{j}") for j in range(2)]
        psS = [ph.ps(f"psS{j}") for j in range(AHEAD + 1)]
        psT = [ph.ps(f"psT{j}") for j in range(2)]
        psO = ph.ps("psO", [P, HALVES, 512])
        names = ("w_split", "split_high", "loaded", "ctx_in", "ctx_split", "mask_in", "piece_ready", "piece_taken",
                 "off_ready", "scored", "masked_ready", "probs_ready", "probs_turned", "probsT_ready", "head_done",
                 "inv_ready", "o_scaled", "o_ready", "y_ready", "x_steps", "cleared", "const_steps", "ints_ready",
                 "sync_passed", "pool_passed", "mask_passed", "blank")
        (w_split, split_high, loaded, ctx_in, ctx_split, mask_in, piece_ready, piece_taken,
         off_ready, scored, masked_ready, probs_ready, probs_turned, probsT_ready, head_done,
         inv_ready, o_scaled, o_ready, y_ready, x_steps, cleared, const_steps, ints_ready,
         sync_passed, pool_passed, mask_passed, blank) = map(ph.sem, names)
        if layer == 0:
            raw_mask = ph.sb("raw_mask", [S, KEYS], U8)
            bq, bk = ph.sb("bq", [P, WC]), ph.sb("bk", [P, WC])
            bv, bo = ph.sb("bv", [S, D]), ph.sb("bo", [S, D])
            queries, keys = ph.sb("queries", [P, WC, S]), ph.sb("keys", [P, WC, KEYS])
            query_parts = [ph.sb(f"query_{part}", [P, WC, S], R) for part in PARTS]
            queries_ready, queries_split, copies_ready, keys_ready, keys_split = (ph.sem(n) for n in (
                "queries_ready", "queries_split", "copies_ready", "keys_ready", "keys_split"))
            consts, XS = 4, 2
        else:
            raw = given.raw
            square = ph.sb("square", [P, 2, HW])
            sums = ph.sb("sums", [P, 4, HEADS])
            rms = ph.sb("rms", [P, 4, HEADS])
            lens_i, lens = ph.sb("lens_i", [S, B], I32), ph.sb("lens", [S, B])
            key_i, key_no = ph.sb("key_i", [S, KEYS], I32), ph.sb("key_no", [S, KEYS])
            wcol, wk_col = ph.sb("wcol", [P, 1]), ph.sb("wk_col", [P, 1])
            xq = ph.sb("xq", [P, KD, S])
            summed, rms_steps, scaled, xq_ready = map(ph.sem, ("summed", "rms_steps", "scaled", "xq_ready"))
            consts, XS = 5, 1
        ph.credit()

        def pieces_of(b, q):
            return Count(FIRST + b * PER, (FIRST + q * PER) % 2)

        def steps(engine, step):
            with engine.Fori(0, B // 2 - 1) as i:
                step(2 * i, 0, 2 * i + 1)
                step(2 * i + 1, 1, 2 * i + 2)
            step(B - 2, 0, B - 1)
            step(B - 1, 1, None)

        with nc.Block() as block:
            @block.sync
            def _(sync):
                sync.dma_start(ctx_raw[:], ins["ctx_1024"][0].rearrange("(k p) n -> p k n", p=P)).then_inc(ctx_in, 16)
                if layer == 0:
                    for b, name in ((bq, "bq"), (bk, "bk")):
                        sync.dma_start(b[:], ins[pre + name]).then_inc(loaded, 16)
                    for b, name in ((bv, "bv"), (bo, "bo")):
                        sync.dma_start(b[:], ins[pre + name].partition_broadcast(S)).then_inc(loaded, 16)
                    sync.dma_start(raw_mask[:], ins["mask_BxSxS2_bk1"][0]).then_inc(mask_in, 16)
                else:
                    for half in range(2):
                        for b, name in ((wcol, "q_norm_w"), (wk_col, "k_norm_w")):
                            sync.dma_start(b[64 * half:64 * half + 64, :],
                                           ins[pre + name].rearrange("(p a) -> p a", a=1)).then_inc(loaded, 16)
                    sync.dma_start(lens_i[:], ins["_lenS2"].partition_broadcast(S)).then_inc(loaded, 16)
                with sync.Fori(1, B) as i:
                    sync.wait_ge(ctx_split, CREDIT + 2 * i)
                    sync.sem_inc(sync_passed, 1)
                    sync.dma_start(ctx_raw[:], ins["ctx_1024"][bass.ds(i, 1)].rearrange("b (k p) n -> p (b k) n", p=P)).then_inc(ctx_in, 16)
                    if layer == 0:
                        sync.wait_ge(off_ready, CREDIT + i)
                        sync.sem_inc(sync_passed, 1)
                        sync.dma_start(raw_mask[:], ins["mask_BxSxS2_bk1"][bass.ds(i, 1)].rearrange("b s n -> (b s) n")).then_inc(mask_in, 16)

            @block.tensor
            def _(pe):
                def piece(count, kind, b, q):
                    n, bank = count.next()
                    ps = psP[bank]
                    pe.wait_ge(piece_taken, count.one_before_last(n))
                    if kind[0] == "q" and layer == 0:
                        c = kind[1]
                        for k in range(KD):
                            last = nc.tensor.matmul(ps[:, 0:S], wq[:, k, c * P:(c + 1) * P], core.xnT[:, k, bass.ds(b * S, S)],
                                                    start=k == 0, stop=k == KD - 1)
                    elif kind[0] == "k" and layer == 0:
                        c = kind[1]
                        pe.wait_ge(ctx_split, CREDIT + 2 * (b + 1))
                        for k in range(KD):
                            last = three_products(nc, ps[:, 0:EVEN], [w[:, k, c * P:(c + 1) * P] for w in wk],
                                                  [x[:, k, :] for x in ctxT[q]], k == 0, k == KD - 1)
                    elif kind[0] == "q":
                        a = kind[2]
                        pe.wait_ge(xq_ready, CREDIT + b + 1)
                        for k in range(KD):
                            last = nc.tensor.matmul(ps[0:S, :], xq[:, k, :], wq[:, k, a * HW:(a + 1) * HW],
                                                    start=k == 0, stop=k == KD - 1)
                    elif kind[0] in "kv":
                        _, t, a = kind
                        k0, rows = KEY_TILES[t]
                        pe.wait_ge(ctx_split, CREDIT + 2 * (b + 1))
                        for k in range(KD):
                            last = three_products(nc, ps[0:rows, 0:HW], [x[:, k, k0:k0 + rows] for x in ctxT[q]],
                                                  [w[:, k, a * HW:(a + 1) * HW] for w in (wk if kind[0] == "k" else wv)],
                                                  k == 0, k == KD - 1)
                    elif kind[0] == "tq":
                        pe.wait_ge(scaled, CREDIT + 4 * b + 1)
                        for j in range(4):
                            c = 4 * kind[1] + j
                            last = nc.tensor.transpose(ps[:, j * S:(j + 1) * S], raw[0:S, 0, c * P:(c + 1) * P], core.ident[0:S, 0:S])
                    elif kind[0] == "tk":
                        pe.wait_ge(scaled, CREDIT + 4 * b + 4)
                        c = kind[1]
                        for t, (k0, rows) in enumerate(KEY_TILES):
                            last = nc.tensor.transpose(ps[:, k0:k0 + rows], raw[0:rows, 1 + t, c * P:(c + 1) * P],
                                                       core.ident[0:rows, 0:rows])
                    elif kind[0] == "o":
                        a = kind[1]
                        pe.wait_ge(o_ready, CREDIT + HALVES * b + a + 1)
                        for c in range(4 * a, min(4 * a + 4, WC)):
                            last = nc.tensor.transpose(ps[:, (c % 4) * S:(c % 4 + 1) * S], o[:, c * P:(c + 1) * P], core.ident[0:S, 0:S])
                    else:
                        pe.wait_ge(piece_taken, CREDIT + kind[1])
                        for c in range(WC):
                            last = nc.tensor.matmul(ps[0:S, 0:D], oT[:, c, :], wo[:, c, :], start=c == 0, stop=c == WC - 1)
                    last.then_inc(piece_ready, 1)

                def step(b, q, following):
                    count = pieces_of(b, q)
                    first = b * HEADS

                    def scores(h):
                        c, r = divmod(h, IN_CHUNK)
                        if h or not isinstance(b, int):
                            pe.wait_ge(masked_ready, CREDIT + first + max(h - AHEAD, 0))
                        if layer == 0:
                            last = three_products(nc, psS[h % (AHEAD + 1)][0:S, 0:EVEN], [part[:, c, r, :] for part in qT[q]],
                                                  [part[:, c, :] for part in kT[q]], True, True)
                        else:
                            last = nc.tensor.matmul(psS[h % (AHEAD + 1)][0:S, 0:KEYS], qT[q][0][:, c, r, :], kT[q][0][:, c, :], start=True, stop=True)
                        last.then_inc(scored, 1)

                    def turn(h):
                        pe.wait_ge(probs_ready, CREDIT + first + h + 1)
                        pe.wait_ge(probsT_ready, CREDIT + first + max(h - 1, 0))
                        for t, (k0, n) in enumerate(KEY_TILES):
                            last = nc.tensor.transpose(psT[h % 2][0:n, t * S:(t + 1) * S], probs[:, h % 2, k0:k0 + n],
                                                       core.ident[0:S, 0:S])
                        last.then_inc(probs_turned, 1)

                    def values(h):
                        if h == 0:
                            pe.wait_ge(piece_taken, CREDIT + count.base + HALVES)
                            pe.wait_ge(o_ready, CREDIT + HALVES * b)
                        pe.wait_ge(probsT_ready, CREDIT + first + h + 1)
                        a, col = divmod(h * DH, 512)
                        for t, (k0, n) in enumerate(KEY_TILES):
                            last = nc.tensor.matmul(psO[0:S, a, col:col + DH], probsT[0:n, h % 2, t, :],
                                                    v[q][0:n, t, h * DH:(h + 1) * DH], start=t == 0, stop=t == 2)
                        last.then_inc(head_done, 1)

                    pe.wait_ge(piece_taken, CREDIT + count.base - (HALVES + HALVES + 1 + HALVES if not isinstance(b, int) or b else 2 * HALVES))
                    if layer == 0:
                        pe.wait_ge(copies_ready, CREDIT + 2 * WC * (b + 1))
                        pe.wait_ge(keys_split, CREDIT + WC * (b + 1))
                    for h in range(AHEAD):
                        scores(h)
                    for h in range(HEADS):
                        if h + AHEAD < HEADS:
                            scores(h + AHEAD)
                        if h == 0:
                            for kind in V3:
                                piece(count, kind, b, q)
                        if following is not None:
                            for kind in QK.get(h, ()):
                                piece(count, kind, following, 1 - q)
                        turn(h)
                        if h:
                            values(h - 1)
                    if following is not None:
                        for kind in V1:
                            piece(count, kind, following, 1 - q)
                    values(HEADS - 1)
                    for kind in BEFORE_O if following is not None else ():
                        piece(count, kind, following, 1 - q)
                    for a in range(HALVES):
                        piece(count, ("o", a), b, q)
                    turned = count.base + count.n
                    for kind in AFTER_O if following is not None else ():
                        piece(count, kind, following, 1 - q)
                    piece(count, ("out", turned), b, q)

                pe.wait_ge(loaded, CREDIT + 16 * consts)
                pe.wait_ge(given.qo_in, 32)
                pe.wait_ge(w_split, CREDIT + 4)
                pe.wait_ge(cleared, CREDIT + 1)
                count = Count()
                for kind in [k for h in sorted(QK) for k in QK[h]] + V1 + V2:
                    piece(count, kind, 0, 0)
                steps(pe, step)

            @block.scalar
            def _(act):
                def take(count, kind, b, q):
                    n, bank = count.next()
                    ps = psP[bank]
                    act.wait_ge(piece_ready, CREDIT + n + 1)
                    copy = nc.scalar.copy
                    if kind[0] == "q" and layer == 0:
                        c = kind[1]
                        act.wait_ge(copies_ready, CREDIT + 2 * WC * b)
                        nc.scalar.activation(queries[:, c, :], ps[:, 0:S], ACT.Identity, scale=-DH ** -0.5,
                                             bias=bq[:, c:c + 1]).then_inc(queries_ready, 1)
                        act.wait_ge(queries_ready, CREDIT + WC * b + c + 1)
                        act.sem_inc(piece_taken, 1)
                        return
                    elif kind[0] == "k" and layer == 0:
                        c = kind[1]
                        nc.scalar.activation(kT[q][0][:, c, 0:KEYS], ps[:, 0:KEYS], ACT.Identity, bias=bk[:, c:c + 1])
                        act.wait_ge(keys_split, CREDIT + WC * b)
                        nc.scalar.activation(keys[:, c, :], ps[:, 0:KEYS], ACT.Identity, bias=bk[:, c:c + 1]).then_inc(keys_ready, 1)
                        act.wait_ge(keys_ready, CREDIT + WC * b + c + 1)
                        act.sem_inc(piece_taken, 1)
                        return
                    elif kind[0] in "qk":
                        t = 0 if kind[0] == "q" else 1 + kind[1]
                        a = kind[2]
                        rows = S if t == 0 else KEY_TILES[t - 1][1]
                        before = 8 * b + 2 * t + a
                        copy(raw[0:rows, t, a * HW:(a + 1) * HW], ps[0:rows, :])
                        if not (isinstance(before, int) and before < 2):
                            act.wait_ge(summed, CREDIT + before - 1)
                        last = nc.scalar.activation(square[0:rows, a, :], ps[0:rows, :], ACT.Square)
                    elif kind[0] == "v":
                        _, t, a = kind
                        rows = KEY_TILES[t][1]
                        last = copy(v[q][0:rows, t, a * HW:(a + 1) * HW], ps[0:rows, 0:HW])
                    elif kind[0] == "tq":
                        for r in range(2):
                            last = nc.scalar.activation(qT[q][0][:, 4 * kind[1]:4 * kind[1] + 4, r, :],
                                                        ps[:, 0:4 * S].rearrange("p (c s) -> p c s", c=4), ACT.Identity,
                                                        scale=pick[:, r:r + 1])
                    elif kind[0] == "tk":
                        last = copy(kT[q][0][:, kind[1], :], ps[:, 0:KEYS])
                    elif kind[0] == "o":
                        a, m = kind[1], min(4, WC)
                        last = copy(oT[:, 4 * a:4 * a + m, :], ps[:, 0:m * S].rearrange("p (c s) -> p c s", c=m))
                    else:
                        act.wait_ge(x_steps, CREDIT + XS * b)
                        nc.scalar.mul(y[:], ps[0:S, 0:D], core.gates[0:S, layer:layer + 1]).then_inc(y_ready, 1)
                        act.wait_ge(y_ready, CREDIT + b + 1)
                        act.sem_inc(piece_taken, 1)
                        return
                    last.then_inc(piece_taken, 1)

                def stand_queries(b):
                    nc.scalar.copy(xq[:], core.xnT[:, :, bass.ds(b * S, S)]).then_inc(xq_ready, 1)

                def step(b, q, following):
                    count = pieces_of(b, q)
                    first = b * HEADS

                    def exp(h):
                        act.wait_ge(masked_ready, CREDIT + first + h + 1)
                        act.wait_ge(probs_turned, CREDIT + first + max(h - 1, 0))
                        if h == 0:
                            act.wait_ge(inv_ready, CREDIT + b)
                        nc.scalar.activation(probs[:, h % 2, :], masked[:, h % 2, :], ACT.Exp, bias=least[:, h:h + 1],
                                             scale=-1.0, accum_out=total[:, h:h + 1]).then_inc(probs_ready, 1)

                    if q == 0:
                        table.ahead(act, b)
                    exp(0)
                    if layer == 1 and following is not None:
                        stand_queries(following)
                    take(count, V3[0], b, q)
                    for h in range(HEADS):
                        if h + 1 < HEADS:
                            exp(h + 1)
                        if h == 0:
                            for kind in V3[1:]:
                                take(count, kind, b, q)
                        if following is not None:
                            for kind in QK.get(h, ()):
                                take(count, kind, following, 1 - q)
                    if following is not None:
                        for kind in V1 + BEFORE_O:
                            take(count, kind, following, 1 - q)
                    for a in range(HALVES):
                        take(count, ("o", a), b, q)
                    for kind in AFTER_O if following is not None else ():
                        take(count, kind, following, 1 - q)
                    take(count, ("out",), b, q)

                for n, w in enumerate((wk, wv)):
                    act.wait_ge(given.kv_in[n], 16)
                    nc.scalar.copy(w[0][:], stage[:, 2 * n:2 * n + 2, :]).then_inc(split_high, 1)
                act.wait_ge(const_steps, CREDIT + (2 if layer == 0 else 4))
                act.wait_ge(w_split, CREDIT + 4)
                if layer == 1:
                    stand_queries(0)
                count = Count()
                for kind in [k for h in sorted(QK) for k in QK[h]] + V1 + V2:
                    take(count, kind, 0, 0)
                steps(act, step)

            @block.gpsimd
            def _(pool):
                def split(b, q):
                    pool.wait_ge(ctx_in, CREDIT + 16 * (b + 1))
                    pool.sem_inc(pool_passed, 1)
                    if not (isinstance(b, int) and b < 2):
                        pool.wait_ge(piece_ready, CREDIT + FIRST + (b - 2) * PER + HALVES)
                        pool.sem_inc(pool_passed, 1)
                    pool.tensor_copy(ctxT[q][0][:, :, 0:KEYS], ctx_raw[:]).then_inc(ctx_split, 1)
                    pool.wait_ge(ctx_split, CREDIT + 2 * b + 1)
                    pool.tensor_tensor(ctxT[q][1][:, :, 0:KEYS], ctx_raw[:], ctxT[q][0][:, :, 0:KEYS].bitcast(F32), ALU.subtract).then_inc(ctx_split, 1)

                def split_scores(b, q):
                    for c in range(WC):
                        pool.wait_ge(queries_ready, CREDIT + WC * b + c + 1)
                        pool.sem_inc(pool_passed, 1)
                        step = Steps(pool, queries_split, CREDIT + 2 * (WC * b + c))
                        step.then(pool.tensor_copy(query_parts[0][:, c, :], queries[:, c, :]))
                        pool.sem_inc(pool_passed, 1)
                        step.then(pool.tensor_tensor(query_parts[1][:, c, :], queries[:, c, :], query_parts[0][:, c, :].bitcast(F32),
                                                     ALU.subtract))
                        pool.sem_inc(pool_passed, 1)
                        for part, copies in zip(query_parts, qT[q]):
                            pool.tensor_tensor(copies[:, c, :, :], spread(part[:, c, :].bitcast(F32), IN_CHUNK), bcast(pick[:], S),
                                               ALU.mult).then_inc(copies_ready, 1)
                    for c in range(WC):
                        pool.wait_ge(keys_ready, CREDIT + WC * b + c + 1)
                        pool.sem_inc(pool_passed, 1)
                        pool.tensor_tensor(kT[q][1][:, c, 0:KEYS], keys[:, c, :], kT[q][0][:, c, 0:KEYS].bitcast(F32),
                                           ALU.subtract).then_inc(keys_split, 1)

                def norms(b, q):
                    if layer == 0:
                        return split_scores(b, q)
                    count = Steps(pool, rms_steps, CREDIT + 8 * b)
                    for t in range(4):
                        rows = S if t == 0 else KEY_TILES[t - 1][1]
                        pool.wait_ge(summed, CREDIT + 8 * b + 2 * t + 2)
                        pool.sem_inc(pool_passed, 1)
                        count.then(pool.tensor_scalar(rms[0:rows, t, :], sums[0:rows, t, :], 1.0 / DH, RMS_EPS, ALU.mult, ALU.add))
                        count.then(pool.tensor_tensor(rms[0:rows, t, :], rms[0:rows, t, :], core.half[0:rows, 0:HEADS], ALU.pow))

                def add_output(b):
                    pool.wait_ge(y_ready, CREDIT + b + 1)
                    pool.sem_inc(pool_passed, 1)
                    row = core.x[:, bass.ds(b, 1), :].rearrange("p a d -> p (a d)")
                    count = Steps(pool, x_steps, CREDIT + XS * b)
                    if layer == 0:
                        count.then(pool.tensor_tensor(row, row, bo[:], ALU.add))
                        pool.sem_inc(pool_passed, 1)
                    pool.tensor_tensor(row, row, y[:], ALU.add).then_inc(x_steps, 1)

                pool.memset(pick[:], 1.0).then_inc(blank, 1)
                pool.wait_ge(blank, CREDIT + 1)
                pool.affine_select(out=pick[:], in_=pick[:], compare_op=ALU.is_ge, fill=0.0,
                                   base=0, pattern=[[-DH, IN_CHUNK]], channel_multiplier=1).then_inc(blank, 1)
                pool.wait_ge(blank, CREDIT + 2)
                pool.affine_select(out=pick[:], in_=pick[:], compare_op=ALU.is_ge, fill=0.0,
                                   base=DH - 1, pattern=[[DH, IN_CHUNK]], channel_multiplier=-1).then_inc(ints_ready, 1)
                if layer == 1:
                    pool.iota(key_i[:], [[1, KEYS]], base=0, channel_multiplier=0).then_inc(ints_ready, 1)
                for q in range(2):
                    for x in ctxT[q] + (kT[q] if layer == 0 else []):
                        pool.memset(x[:, :, KEYS:EVEN].bitcast(F32), 0.0).then_inc(blank, 1)
                if layer == 0:
                    pool.wait_ge(const_steps, CREDIT + 2)
                    pool.wait_ge(ints_ready, CREDIT + 1)
                split(0, 0)
                norms(0, 0)
                split(1, 1)
                with pool.Fori(0, B // 2 - 1) as i:
                    for q in range(2):
                        norms(2 * i + q + 1, 1 - q)
                        split(2 * i + q + 2, q)
                        add_output(2 * i + q)
                norms(B - 1, 1)
                add_output(B - 2)
                add_output(B - 1)

            @block.vector
            def _(dve):
                gate = core.gates[0:S, layer:layer + 1]
                for n, w in enumerate((wk, wv)):
                    dve.wait_ge(split_high, CREDIT + n + 1)
                    nc.vector.tensor_tensor(w[1][:], stage[:, 2 * n:2 * n + 2, :], w[0][:].bitcast(F32), ALU.subtract).then_inc(w_split, 2)
                dve.wait_ge(loaded, CREDIT + 16 * consts)
                dve.wait_ge(ints_ready, CREDIT + 1 + layer)
                const = Steps(dve, const_steps, CREDIT)
                if layer == 0:
                    const.then(nc.vector.tensor_scalar(bq[:], bq[:], -DH ** -0.5, None, ALU.mult))
                    const.then(nc.vector.tensor_scalar(bo[:], bo[:], gate, None, ALU.mult))
                else:
                    const.then(nc.vector.scalar_tensor_tensor(wcol[:], wcol[:], -DH ** -0.5, wk_col[:], ALU.mult, ALU.mult))
                    const.then(nc.vector.tensor_copy(lens[:], lens_i[:]))
                    const.then(nc.vector.tensor_copy(key_no[:], key_i[:]))
                    const.then(nc.vector.tensor_scalar(pick[:], pick[:], wcol[:], None, ALU.mult))
                for j in range(2):
                    const.then(nc.vector.memset(psT[j][:], 0.0))
                dve.sem_inc(cleared, 1)

                def sum_squares(b, t, a):
                    rows = S if t == 0 else KEY_TILES[t - 1][1]
                    n = 2 * t + a
                    if isinstance(b, int) and b == 0:
                        dve.wait_ge(piece_taken, CREDIT + n + 1)
                    else:
                        dve.wait_ge(piece_taken, CREDIT + FIRST + (b - 1) * PER + HALVES + n + 1)
                    nc.vector.tensor_reduce(sums[0:rows, t, a * 8:(a + 1) * 8],
                                            square[0:rows, a, :].rearrange("p (h d) -> p h d", d=DH),
                                            AX.X, ALU.add).then_inc(summed, 1)

                def scale(b, t):
                    rows = S if t == 0 else KEY_TILES[t - 1][1]
                    dve.wait_ge(rms_steps, CREDIT + 8 * b + 2 * (t + 1))
                    heads = raw[0:rows, t, :].rearrange("p (h d) -> p h d", d=DH)
                    nc.vector.tensor_tensor(heads, heads, bcast(rms[0:rows, t, :], DH), ALU.mult).then_inc(scaled, 1)

                def step(b, q, following):
                    first = b * HEADS
                    if layer == 0:
                        dve.wait_ge(mask_in, CREDIT + 16 * (b + 1))
                        nc.vector.tensor_scalar(off[:], raw_mask[:], MASKED, None, ALU.mult).then_inc(off_ready, 1)
                    else:
                        length = lens[:, b:b + 1] if isinstance(b, int) else lens[:, bass.ds(b, 1)]
                        nc.vector.tensor_scalar(off[:], key_no[:], length, MASKED, ALU.is_ge, ALU.mult).then_inc(off_ready, 1)

                    def mask(h):
                        dve.wait_ge(scored, CREDIT + first + h + 1)
                        if h == 0:
                            dve.wait_ge(off_ready, CREDIT + b + 1)
                        dve.wait_ge(probs_ready, CREDIT + first + max(h - 1, 0))
                        dve.sem_inc(mask_passed, 1)
                        nc.vector.tensor_tensor_reduce(masked[:, h % 2, :], psS[h % (AHEAD + 1)][0:S, 0:KEYS], off[:], 1.0, 3e38,
                                                       ALU.add, ALU.min, least[:, h:h + 1]).then_inc(masked_ready, 1)

                    def copy_probs(h):
                        dve.wait_ge(probs_turned, CREDIT + first + h + 1)
                        dve.wait_ge(head_done, CREDIT + first + max(h - 1, 0))
                        nc.vector.tensor_copy(probsT[:, h % 2, :, :],
                                              psT[h % 2][:, 0:3 * S].rearrange("p (t s) -> p t s", t=3)).then_inc(probsT_ready, 1)

                    mask(0)
                    for h in range(HEADS):
                        if h + 1 < HEADS:
                            mask(h + 1)
                        copy_probs(h)
                        if layer == 1 and following is not None:
                            for kind in QK.get(h - 1, ()):
                                if kind[0] in "qk":
                                    sum_squares(following, 0 if kind[0] == "q" else 1 + kind[1], kind[2])
                            if h in SCALE_AT:
                                scale(following, SCALE_AT[h])
                    dve.wait_ge(probs_ready, CREDIT + first + HEADS)
                    nc.vector.reciprocal(inv[:], total[:]).then_inc(inv_ready, 1)
                    dve.wait_ge(inv_ready, CREDIT + b + 1)
                    dve.wait_ge(head_done, CREDIT + first + HEADS)
                    for a in range(HALVES):
                        nh = HW // DH
                        ins_ = nc.vector.tensor_tensor(o[:, a * HW:(a + 1) * HW].rearrange("p (h d) -> p h d", d=DH),
                                                       psO[0:S, a, 0:HW].rearrange("p (h d) -> p h d", d=DH),
                                                       bcast(inv[:, a * nh:(a + 1) * nh], DH), ALU.mult)
                        if layer == 0:
                            ins_.then_inc(o_scaled, 1)
                            dve.wait_ge(o_scaled, CREDIT + b + 1)
                            nc.vector.tensor_tensor(o[:], o[:], bv[:], ALU.add).then_inc(o_ready, 1)
                        else:
                            ins_.then_inc(o_ready, 1)

                if layer == 1:
                    for t in range(4):
                        for a in range(2):
                            sum_squares(0, t, a)
                    for t in range(4):
                        scale(0, t)
                steps(dve, step)


def slot_shape(layer):
    return (HALF0, 2 * E0) if layer == 0 else (P, NBLK1 * BLK1 // P)


def route_phase(core, layer, logits, weights, slots, place, blocks=None, ranking=None, following=None):
    nc, ins = core.nc, core.ins
    E = E0 if layer == 0 else E1
    with Phase(core, f"route{layer}") as ph:
        sc, hot1, hot2, work = (ph.sb(n, [S, B, E]) for n in ("sc", "hot1", "hot2", "work"))
        rev, rev_i = ph.sb("rev", [P, E]), ph.sb("rev_i", [P, E], I32)
        top = ph.sb("top", [S, 8, B])
        m1, m2, r1, r2, t0, t1, t2, t3 = (top[:, k, :] for k in range(8))
        steps, ints, exped, asked_exp, loaded = (ph.sem(n) for n in ("steps", "ints", "exped", "asked_exp", "loaded"))
        counted, to_count = ph.sem("counted"), ph.sem("to_count")
        gate_b = ph.sb("gate_b", [S, E])
        if layer == 0:
            trash_i = ph.sb("trash_i", [P, 1], I32)
            trash, before, wT, hotT, r1, r2 = ranking.trash, ranking.before, ranking.wT, ranking.hotT, ranking.r1[:], ranking.r2[:]
            turned = ph.sb("turned", [P, 5, 2, S], BF16)
            rest = ph.sb("rest", [P, 2, S])
            parts_ready = ph.sem("parts_ready")
            before_ready, rows_stored = ph.sem("before_ready"), ph.sem("rows_stored")
            out_turned, bounced, back, blank = (ph.sem(n) for n in ("out_turned", "bounced", "back", "blank"))
        else:
            part_i = ph.sb("part_i", [S, B], I32)
            tot = ph.sb("tot", [P, 3, B, E1])
            cnt = ph.sb("cnt", [P, 6, E1])
            jrow_i, jrow = ph.sb("jrow_i", [P, NBLK1], I32), ph.sb("jrow", [P, NBLK1])
            cmp = ph.sb("cmp", [P, NBLK1, E1])
            be = ph.sb("be", [P, 2, NBLK1])
            row_i, row = ph.sb("row_i", [P, 1], I32), ph.sb("row", [P, 1])
        with ExitStack() as first:
            psA, psB = (first.enter_context(nc.psum_tensor(f"route{layer}_{n}", [P, 512], F32)) for n in ("psA", "psB"))
            with nc.Block() as block:
                @block.sync
                def _(sync):
                    if layer == 0:
                        sync.dma_start(gate_b[:], ins["L0_ffn_gate_b"].partition_broadcast(S)).then_inc(loaded, 16)
                        sync.dma_start(core.rows.rearrange("(b s) d -> s b d", s=S), core.xn[:]).then_inc(rows_stored, 16)
                        sync.wait_ge(rows_stored, 16)
                        for what, ready, count in (((3, 4), out_turned, 2), ((0, 1, 2), parts_ready, 1)):
                            sync.wait_ge(ready, count)
                            for q in what:
                                sync.dma_start(core.bounce[q].rearrange("h p m -> p h m"), turned[:, q]).then_inc(bounced, 16)
                        sync.wait_ge(bounced, 16 * 5)
                        back_view = core.bounce.rearrange("q h (t e) m -> q e (h t) m", e=E0)
                        for part in range(3):
                            rows = slice(part * E0, (part + 1) * E0)
                            sync.dma_start(wT[rows].rearrange("e (t m) -> e t m", m=S), back_view[part]).then_inc(back, 16)
                            for k in range(2):
                                sync.dma_start(hotT[rows, k, :].rearrange("e (t m) -> e t m", m=S), back_view[3 + k]).then_inc(back, 16)
                        following.load(sync)
                        sync.wait_ge(back, 16 * 9)

                @block.gpsimd
                def _(pool):
                    pool.iota(rev_i[:], [[-1, E]], base=E, channel_multiplier=0).then_inc(ints, 1)
                    if layer == 0:
                        pool.iota(trash_i[:], [[0, 1]], base=E0 * CAP0, channel_multiplier=1).then_inc(ints, 1)
                        pool.memset(before[:], 0.0).then_inc(blank, 1)
                        pool.wait_ge(blank, 1)
                        pool.affine_select(out=before[:], in_=before[:], compare_op=ALU.is_ge, fill=-2e-38,
                                           base=-N, pattern=[[1, 2 * N]], channel_multiplier=-1).then_inc(before_ready, 1)
                    else:
                        pool.iota(jrow_i[:], [[1, NBLK1]], base=0, channel_multiplier=0).then_inc(ints, 1)
                        pool.iota(row_i[:], [[0, 1]], base=0, channel_multiplier=1).then_inc(ints, 1)

                @block.scalar
                def _(act):
                    act.wait_ge(asked_exp, 1)
                    if layer == 0:
                        nc.scalar.activation(sc[:], work[:], ACT.Exp).then_inc(exped, 1)
                        act.wait_ge(counted, 1)
                        for k, ps in enumerate((psB[:, 0:2 * S], psB[:, 2 * S:4 * S])):
                            nc.scalar.copy(turned[:, 3 + k], ps.rearrange("p (h s) -> p h s", h=2)).then_inc(out_turned, 1)
                    else:
                        nc.scalar.activation(t1, t0, ACT.Exp).then_inc(exped, 1)

                @block.tensor
                def _(pe):
                    pe.wait_ge(to_count, 1)
                    if layer == 0:
                        for q, src in enumerate((work, hot1, hot2)):
                            for h in range(2):
                                ps, a = (psA, h * S) if q == 0 else (psB, ((q - 1) * 2 + h) * S)
                                last = nc.tensor.transpose(ps[:, a:a + S],
                                                           src[:, 8 * h:8 * h + 8, :].rearrange("p t e -> p (t e)"), core.ident[0:S, 0:S])
                    else:
                        a = work[:].rearrange("p t e -> p (t e)")
                        nc.tensor.matmul(psA[0:S, 0:B * E1], core.tri[0:S, 0:S], a, start=True, stop=True)
                        last = nc.tensor.matmul(psB[:, 0:B * E1], core.ones[0:S, :], a, start=True, stop=True)
                    last.then_inc(counted, 1)

                @block.vector
                def _(dve):
                    v = nc.vector
                    step = Steps(dve, steps)
                    dve.wait_ge(ints, 2 if layer == 0 else 3)
                    step.then(v.tensor_copy(rev[:], rev_i[:]))
                    if layer == 0:
                        step.then(v.tensor_copy(trash[:], trash_i[:]))
                        step.then(v.tensor_reduce(m1, logits, AX.X, ALU.max))
                        v.tensor_tensor(work[:], logits, bcast(m1, E), ALU.subtract).then_inc(asked_exp, 1)
                        dve.wait_ge(exped, 1)
                        step.then(v.tensor_reduce(t0, sc[:], AX.X, ALU.add))
                        step.then(v.reciprocal(t0, t0))
                        step.then(v.tensor_tensor(sc[:], sc[:], bcast(t0, E), ALU.mult))
                        dve.wait_ge(loaded, 16)
                        step.then(v.tensor_tensor(sc[:], sc[:], spread(gate_b[:], B), ALU.add))
                    else:
                        step.then(v.tensor_copy(jrow[:], jrow_i[:]))
                        step.then(v.tensor_copy(row[:], row_i[:]))
                        step.then(v.tensor_copy(sc[:], logits))
                    for m, r, hot in ((m1, r1, hot1), (m2, r2, hot2)):
                        step.then(v.tensor_reduce(m, sc[:], AX.X, ALU.max))
                        step.then(v.tensor_tensor(work[:], sc[:], bcast(m, E), ALU.is_equal))
                        step.then(v.tensor_tensor(work[:], work[:], spread(rev[0:S, :], B), ALU.mult))
                        step.then(v.tensor_reduce(r, work[:], AX.X, ALU.max))
                        step.then(v.tensor_tensor(hot[:], spread(rev[0:S, :], B), bcast(r, E), ALU.is_equal))
                        step.then(v.scalar_tensor_tensor(sc[:], hot[:], -BIG, sc[:], ALU.mult, ALU.add))
                    if layer == 0:
                        for k, hot in enumerate((hot1, hot2)):
                            step.then(v.tensor_tensor(work[:], hot[:], logits, ALU.mult))
                            step.then(v.tensor_reduce(weights[:, k, :], work[:], AX.X, ALU.add))
                        step.then(v.tensor_tensor(sc[:], hot1[:], hot2[:], ALU.add))
                        step.then(v.tensor_tensor(work[:], sc[:], logits, ALU.mult))
                        step.then(v.tensor_scalar(sc[:], sc[:], -1.0, BIG, ALU.add, ALU.mult))
                        v.tensor_tensor(work[:], work[:], sc[:], ALU.add).then_inc(to_count, 1)
                        dve.wait_ge(counted, 1)
                        step.then(v.tensor_copy(turned[:, 0], psA[:, 0:2 * S].rearrange("p (h s) -> p h s", h=2)))
                        step.then(v.tensor_tensor(rest[:], psA[:, 0:2 * S].rearrange("p (h s) -> p h s", h=2), turned[:, 0], ALU.subtract))
                        step.then(v.tensor_copy(turned[:, 1], rest[:]))
                        v.tensor_tensor(turned[:, 2], rest[:], turned[:, 1], ALU.subtract).then_inc(parts_ready, 1)
                    else:
                        v.tensor_tensor(t0, m2, m1, ALU.subtract).then_inc(asked_exp, 1)
                        dve.wait_ge(exped, 1)
                        step.then(v.tensor_scalar(t2, t1, 1.0, None, ALU.add))
                        step.then(v.reciprocal(weights[:, 0, :], t2))
                        step.then(v.tensor_tensor(weights[:, 1, :], t1, weights[:, 0, :], ALU.mult))
                        v.tensor_tensor(work[:], hot1[:], hot2[:], ALU.add).then_inc(to_count, 1)
                        dve.wait_ge(counted, 1)
                        each = psB[:, 0:B * E1].rearrange("p (t e) -> p t e", e=E1)
                        inside = psA[0:S, 0:B * E1].rearrange("p (t e) -> p t e", e=E1)
                        step.then(v.tensor_copy(tot[:, 0], each))
                        a, b = 0, 1
                        for sh in (1, 2, 4, 8):
                            step.then(v.tensor_copy(tot[:, b, 0:sh], tot[:, a, 0:sh]))
                            step.then(v.tensor_tensor(tot[:, b, sh:], tot[:, a, sh:], tot[:, a, 0:B - sh], ALU.add))
                            a, b = b, a
                        count, nb, c0, c1, start, base = (cnt[:, k, :] for k in range(6))
                        step.then(v.tensor_copy(count, tot[:, a, B - 1]))
                        step.then(v.tensor_tensor(tot[:, 2], tot[:, a], each, ALU.subtract))
                        step.then(v.tensor_scalar(nb, count, 0.0, None, ALU.is_gt))
                        for j in range(1, MAXB1):
                            step.then(v.scalar_tensor_tensor(nb, count, float(BLK1 * j), nb, ALU.is_gt, ALU.add))
                        step.then(v.tensor_copy(c0, nb))
                        for sh in (1, 2, 4):
                            step.then(v.tensor_copy(c1[:, 0:sh], c0[:, 0:sh]))
                            step.then(v.tensor_tensor(c1[:, sh:], c0[:, sh:], c0[:, 0:E1 - sh], ALU.add))
                            c0, c1 = c1, c0
                        step.then(v.tensor_tensor(start, c0, nb, ALU.subtract))
                        step.then(v.tensor_scalar(base, start, float(BLK1), None, ALU.mult))
                        step.then(v.tensor_tensor(work[:], tot[0:S, 2], inside, ALU.add))
                        step.then(v.tensor_tensor(work[:], work[:], spread(base[0:S, :], B), ALU.add))
                        for k, hot in enumerate((hot1, hot2)):
                            step.then(v.tensor_tensor(sc[:], hot[:], work[:], ALU.mult))
                            step.then(v.tensor_reduce(t3, sc[:], AX.X, ALU.add))
                            step.then(v.tensor_copy(slots[:, k, :], t3))
                            for j, (op, by) in enumerate(((ALU.bitwise_and, P - 1), (ALU.logical_shift_right, 7))):
                                step.then(v.tensor_scalar(part_i[:], slots[:, k, :], by, None, op))
                                step.then(v.tensor_copy(place[:, j, k, :], part_i[:]))
                        step.then(v.tensor_tensor(cmp[:], bcast(jrow[:], E1), spread(c0, NBLK1), ALU.is_ge))
                        step.then(v.tensor_reduce(be[:, 0, :], cmp[:], AX.X, ALU.add))
                        step.then(v.tensor_scalar(be[:, 0, :], be[:, 0, :], float(E1 - 1), None, ALU.min))
                        step.then(v.tensor_scalar(be[:, 1, :], be[:, 0, :], float(P), row[:, 0:1], ALU.mult, ALU.add))
                        step.then(v.tensor_copy(blocks[:, 0, :], be[:, 1, :]))
                        step.then(v.tensor_copy(blocks[:, 1, :], be[:, 0, :]))


def invert_phase(core, layer, place, tokens, slots=None, ranking=None):
    nc = core.nc
    LO, HI = slot_shape(layer)
    with Phase(core, f"invert{layer}") as ph:
        lo_i, lo_row = ph.sb("lo_i", [S, P], I32), ph.sb("lo_row", [S, P])
        id_i, ids = ph.sb("id_i", [S, B], I32), ph.sb("ids", [S, B])
        hot_lo, hot_hi = ph.sb("hot_lo", [S, 2 * B, LO]), ph.sb("hot_hi", [S, 2 * B, HI])
        psI = ph.ps("psI")
        ints, steps, hot_ready, found, stored = (ph.sem(n) for n in ("ints", "steps", "hot_ready", "found", "stored"))
        with nc.Block() as block:
            if layer == 1:
                @block.sync
                def _(sync):
                    sync.dma_start(core.rows.rearrange("(b s) d -> s b d", s=S), core.xn[:]).then_inc(stored, 16)
                    sync.wait_ge(stored, 16)

            @block.gpsimd
            def _(pool):
                pool.iota(lo_i[:], [[1, P]], base=0, channel_multiplier=0).then_inc(ints, 1)
                pool.iota(id_i[:], [[S, B]], base=0, channel_multiplier=1).then_inc(ints, 1)

            @block.vector
            def _(dve):
                v = nc.vector
                step = Steps(dve, steps)
                if layer == 0:
                    ranking.place(v, step, slots, place)
                dve.wait_ge(ints, 2)
                step.then(v.tensor_copy(lo_row[:], lo_i[:]))
                step.then(v.tensor_copy(ids[:], id_i[:]))
                lo, hi = (place[:, j].rearrange("p k t -> p (k t)") for j in range(2))
                v.tensor_tensor(hot_lo[:], spread(lo_row[:, 0:LO], 2 * B), bcast(lo, LO), ALU.is_equal).then_inc(hot_ready, 1)
                step.then(v.tensor_tensor(hot_hi[:], spread(lo_row[:, 0:HI], 2 * B), bcast(hi, HI), ALU.is_equal))
                for k in range(2):
                    h = hot_hi[:, k * B:(k + 1) * B, :]
                    v.tensor_tensor(h, h, bcast(ids[:], HI), ALU.mult).then_inc(hot_ready, 1)
                dve.wait_ge(found, 1)
                step.then(v.tensor_copy(tokens[0:LO, 0:HI], psI[0:LO, 0:HI]))

            @block.tensor
            def _(pe):
                pe.wait_ge(hot_ready, 3)
                for j in range(2 * B):
                    last = nc.tensor.matmul(psI[0:LO, 0:HI], hot_lo[:, j, :], hot_hi[:, j, :], start=j == 0, stop=j == 2 * B - 1)
                last.then_inc(found, 1)


def shared_phase(core, acc, given, ranking, weights):
    nc = core.nc
    R = mybir.dt.float32r
    FC, Q = FF0 // P, 4
    G = Q * S
    NH = 2 * FC
    with Phase(core, "shared") as ph:
        raw = (given.w1, given.w3, given.w2)
        w = [[ph.sb(f"w{n}_{part}", shape, R) for part in ("high", "low")] for n, shape in (
            (1, [P, SHARED, KD, FF0]), (3, [P, SHARED, KD, FF0]), (2, [P, SHARED, FC, D]))]
        x = [[ph.sb(f"x{q}_{part}", [P, KD, G], R) for part in ("high", "low")] for q in range(2)]
        act1, whole = ph.sb("act1", [P, 2, G]), ph.sb("whole", [P, 2, G])
        hid = [ph.sb(f"hid_{part}", [P, NH, G], R) for part in ("high", "low")]
        ps1, ps3, psY = ([ph.ps(f"{n}{j}") for j in range(2)] for n in ("ps1", "ps3", "psY"))
        w_high, w_low, x_split, both, silu, taken, hid_high, hidden, y_ready, y_taken = (ph.sem(n) for n in (
            "w_high", "w_low", "x_split", "both", "silu", "taken", "hid_high", "hidden", "y_ready", "y_taken"))
        ranking.use(ph, weights)
        RANKS = ranking.STEPS // 2
        assert RANKS == NH and RANKS == 2 * Q
        RANK_AT = (2, 6)
        ph.credit()
        with nc.Block() as block:
            @block.gpsimd
            def _(pool):
                for n in range(B // Q):
                    if n >= 2:
                        pool.wait_ge(both, CREDIT + (n - 1) * NH)
                    src = core.xnT[:, :, n * G:(n + 1) * G]
                    high, low = x[n % 2]
                    pool.tensor_copy(high[:], src).then_inc(x_split, 1)
                    pool.wait_ge(x_split, CREDIT + 2 * n + 1)
                    pool.tensor_tensor(low[:], src, high[:].bitcast(F32), ALU.subtract).then_inc(x_split, 1)

            @block.tensor
            def _(pe):
                with pe.Fori(0, B // Q // 2) as i:
                    for q in range(2):
                        n = 2 * i + q
                        pe.wait_ge(x_split, CREDIT + 2 * n + 2)
                        for j in range(NH):
                            s, f = divmod(j, FC)
                            pe.wait_ge(w_low, CREDIT + 3 * s + 2)
                            pe.wait_ge(taken, CREDIT + n * NH + max(j - 1, 0))
                            for wj, ps in ((w[0], ps1), (w[1], ps3)):
                                for k in range(KD):
                                    last = three_products(nc, ps[j % 2][:, 0:G], [part[:, s, k, f * P:(f + 1) * P] for part in wj],
                                                          [part[:, k, :] for part in x[q]], k == 0, k == KD - 1)
                            last.then_inc(both, 1)
                            ranking.select(pe, n, j)
                        pe.wait_ge(w_low, CREDIT + 3 * SHARED)
                        for t in range(Q):
                            pe.wait_ge(y_taken, CREDIT + n * Q + max(t - 1, 0))
                            for j in range(NH):
                                s, f = divmod(j, FC)
                                if j in RANK_AT:
                                    ranking.select(pe, n, RANKS + 2 * t + RANK_AT.index(j))
                                if t == 0:
                                    pe.wait_ge(hidden, CREDIT + n * NH + j + 1)
                                last = three_products(nc, psY[t % 2][0:S, 0:D], [part[:, j, t * S:(t + 1) * S] for part in hid],
                                                      [part[:, s, f, :] for part in w[2]], j == 0, j == NH - 1)
                            last.then_inc(y_ready, 1)

            @block.scalar
            def _(act):
                act.wait_ge(given.loaded, 16 * 3 * SHARED)
                for s in range(SHARED):
                    for buf, parts in zip(raw, w):
                        nc.scalar.copy(parts[0][:, s], buf[:, s]).then_inc(w_high, 1)
                with act.Fori(0, B // Q) as i:
                    for j in range(NH):
                        act.wait_ge(both, CREDIT + i * NH + j + 1)
                        nc.scalar.activation(act1[:, j % 2, :], ps1[j % 2][:, 0:G], ACT.Silu).then_inc(silu, 1)
                        act.wait_ge(y_ready, CREDIT + i * Q)
                        act.wait_ge(taken, CREDIT + i * NH + j + 1)
                        nc.scalar.copy(hid[0][:, j, :], whole[:, j % 2, :]).then_inc(hid_high, 1)

            @block.vector
            def _(dve):
                v = nc.vector
                n = 0
                for s in range(SHARED):
                    for buf, parts in zip(raw, w):
                        n += 1
                        dve.wait_ge(w_high, CREDIT + n)
                        v.tensor_tensor(parts[1][:, s], buf[:, s], parts[0][:, s].bitcast(F32), ALU.subtract).then_inc(w_low, 1)
                with dve.Fori(0, B // Q) as i:
                    for j in range(NH):
                        dve.wait_ge(silu, CREDIT + i * NH + j + 1)
                        v.tensor_tensor(whole[:, j % 2, :], ps3[j % 2][:, 0:G], act1[:, j % 2, :], ALU.mult).then_inc(taken, 1)
                        ranking.compare(dve, i, j)
                        dve.wait_ge(hid_high, CREDIT + i * NH + j + 1)
                        v.tensor_tensor(hid[1][:, j, :], whole[:, j % 2, :], hid[0][:, j, :].bitcast(F32), ALU.subtract).then_inc(hidden, 1)
                    for t in range(Q):
                        for u in range(2):
                            ranking.compare(dve, i, RANKS + 2 * t + u)
                        dve.wait_ge(y_ready, CREDIT + i * Q + t + 1)
                        v.tensor_scalar(acc[:, bass.ds(i * Q + t, 1), :].rearrange("p a d -> p (a d)"), psY[t % 2][0:S, 0:D],
                                        1.0 / SHARED, None, ALU.mult).then_inc(y_taken, 1)


def experts_phase(core, layer, tokens, blocks=None):
    nc, ins = core.nc, core.ins
    R = mybir.dt.float32r
    HALF = HALF0 if layer == 0 else BLK1 // 2
    SL = 2 * HALF
    NX = E0 if layer == 0 else NBLK1
    FF = FF0 if layer == 0 else FF1
    FC = FF // P
    result = core.result0 if layer == 0 else core.result1
    names = ("ew1", "ew3", "ew2") if layer == 0 else ("w1", "w2")
    NW = len(names)
    LOW_BY_DVE = 2 if layer == 0 else NW
    shapes = [[P, KD, FF]] * (NW - 1) + [[P, FC, D]]
    with Phase(core, f"experts{layer}") as ph:
        raw = [ph.sb(f"{n}_raw", sh) for n, sh in zip(names, shapes)]
        w = [[[ph.sb(f"{n}_{part}{q}", sh, R) for part in ("high", "low")] for n, sh in zip(names, shapes)] for q in range(2)]
        xs = [ph.sb(f"xs{q}", [HALF, 2, D]) for q in range(2)]
        xsT = [[ph.sb(f"xsT_{part}{q}", [P, KD, SL], R) for part in ("high", "low")] for q in range(2)]
        hid = [ph.sb(f"hid_{part}", [P, FC, SL], R) for part in ("high", "low")]
        whole = ph.sb("whole", [P, 2, SL])
        ys = [ph.sb(f"ys{q}", [HALF, 2, D]) for q in range(2)]
        ps1, psX, psY = ([ph.ps(f"{n}{j}") for j in range(2)] for n in ("ps1", "psX", "psY"))
        w_in = [ph.plain(f"w_in{j}") for j in range(NW)]
        x_in, b_in = ([ph.plain(f"{n}{q}") for q in range(2)] for n in ("x_in", "b_in"))
        w_high, w_low = ([ph.sem(f"{n}{j}") for j in range(NW)] for n in ("w_high", "w_low"))
        y_out, done, turned = ([ph.sem(f"{n}{q}") for q in range(2)] for n in ("y_out", "done", "turned"))
        xsT_high, xsT_low, multiplied, taken, hid_high, hidden, y_ready, y_taken = (ph.sem(n) for n in (
            "xsT_high", "xsT_low", "multiplied", "taken", "hid_high", "hidden", "y_ready", "y_taken"))
        passed, pool_passed, which_ready = (ph.sem(n) for n in ("passed", "pool_passed", "which_ready"))
        if layer == 0:
            ps3 = [ph.ps(f"ps3{j}") for j in range(2)]
            act1 = ph.sb("act1", [P, 2, SL])
            silu = ph.sem("silu")
        else:
            b1 = [ph.sb(f"b1_{q}", [P, FC]) for q in range(2)]
            b2 = [ph.sb(f"b2_{q}", [P, D]) for q in range(2)]
        which = ph.sb("which", [P, 2, 5, 1], I32)
        NWHICH = 2 if layer == 0 else 5
        table = TableLoad(ph, ACT.Silu if layer == 0 else ACT.Gelu)
        ph.credit()

        def steps(engine, step):
            with engine.Fori(0, NX // 2 - 1) as i:
                step(2 * i, i, 0, True)
                step(2 * i + 1, i, 1, True)
            step(NX - 2, NX // 2 - 1, 0, True)
            step(NX - 1, NX // 2 - 1, 1, False)

        with nc.Block() as block:
            @block.sync
            def _(sync):
                def load(n):
                    for j, name in enumerate(names if layer == 0 else ()):
                        sync.wait_ge(w_low[j], CREDIT + n)
                        sync.sem_inc(passed, 1)
                        sync.dma_start(raw[j][:], ins[f"L0_ffn_{name}"][bass.ds(n, 1)].rearrange(
                            "e (k p) f -> p (e k) f", p=P)).then_inc(w_in[j], 16)

                def store(n, q):
                    sync.wait_ge(y_taken, CREDIT + n + 1)
                    sync.sem_inc(passed, 1)
                    sync.dma_start(result[bass.ds(n * SL, SL), :].rearrange("(h p) d -> p h d", p=HALF), ys[q][:]).then_inc(y_out[q], 16)

                for n in range(2):
                    load(n)
                with sync.Fori(1, NX // 2) as i:
                    for q in range(2):
                        load(2 * i + q)
                        store(2 * i + q - 2, q)
                for q in range(2):
                    store(NX - 2 + q, q)
                for q in range(2):
                    sync.wait_ge(y_out[q], CREDIT + 16 * (NX // 2))

            @block.gpsimd
            def _(pool):
                def pick(n, q, first, cols, src, rows=P):
                    for k, col in enumerate(cols):
                        pool.tensor_copy(which[0:rows, q, first + k, :], src(col)).then_inc(which_ready, 1)
                    pool.wait_ge(which_ready, CREDIT + n * NWHICH + first + len(cols))
                    pool.sem_inc(pool_passed, 1)

                def rows_of(n, i, q):
                    pool.wait_ge(turned[q], CREDIT + i)
                    pool.sem_inc(pool_passed, 1)
                    pick(n, q, 0, (2 * n, 2 * n + 1), lambda col: tokens[0:HALF, bass.ds(col, 1)], HALF)
                    for h in range(2):
                        pool.indirect_dma_start(xs[q][:, h, :], None, core.rows, bass.IndirectOffsetOnAxis(
                            ap=which[0:HALF, q, h, :], axis=0)).then_inc(x_in[q], 16)

                def split(n, q):
                    for j in range(LOW_BY_DVE, NW):
                        pool.wait_ge(w_high[j], CREDIT + n + 1)
                        pool.sem_inc(pool_passed, 1)
                        pool.tensor_tensor(w[q][j][1][:], raw[j][:], w[q][j][0][:].bitcast(F32), ALU.subtract).then_inc(w_low[j], 1)

                if layer == 0:
                    for q in range(2):
                        rows_of(q, 0, q)
                    with pool.Fori(1, NX // 2) as i:
                        for q in range(2):
                            rows_of(2 * i + q, i, q)
                            split(2 * i + q - 2, q)
                    for q in range(2):
                        split(NX - 2 + q, q)
                    return
                with pool.Fori(0, NX // 2) as i:
                    for q in range(2):
                        n = 2 * i + q
                        rows_of(n, i, q)
                        for j, name in enumerate(names):
                            pool.wait_ge(w_low[j], CREDIT + n)
                            pool.sem_inc(pool_passed, 1)
                            if j == 0:
                                pick(n, q, 2, (n,), lambda col: blocks[:, 0, bass.ds(col, 1)])
                            pool.indirect_dma_start(raw[j][:].rearrange("p k f -> p (k f)"), None, ins[f"L1_ffn_{name}"],
                                                    bass.IndirectOffsetOnAxis(ap=which[:, q, 2, :], axis=0)).then_inc(w_in[j], 16)
                        pool.wait_ge(done[q], CREDIT + i)
                        pool.sem_inc(pool_passed, 1)
                        pick(n, q, 3, (0, 1), lambda k: blocks[:, k, bass.ds(n, 1)])
                        for k, (dst, name) in enumerate(((b1[q], "b1"), (b2[q], "b2"))):
                            pool.indirect_dma_start(dst[:], None, ins[f"L1_ffn_{name}"], bass.IndirectOffsetOnAxis(
                                ap=which[:, q, 3 + k, :], axis=0)).then_inc(b_in[q], 16)

            @block.tensor
            def _(pe):
                def turn(n, i, q):
                    pe.wait_ge(x_in[q], 32 * (i + 1))
                    if not isinstance(n, int) or n > 1:
                        pe.wait_ge(xsT_low, CREDIT + n - 1)
                    for k in range(KD):
                        for h in range(2):
                            last = nc.tensor.transpose(psX[q][:, k * SL + h * HALF:k * SL + (h + 1) * HALF],
                                                       xs[q][:, h, k * P:(k + 1) * P], core.ident[0:HALF, 0:HALF])
                    last.then_inc(turned[q], 1)

                def step(n, i, q, more):
                    pe.wait_ge(xsT_low, CREDIT + n + 1)
                    for j in range(NW - 1):
                        pe.wait_ge(w_low[j], CREDIT + n + 1)
                    for f in range(FC):
                        pe.wait_ge(taken, CREDIT + n * FC + max(f - 1, 0))
                        for j, ps in enumerate((ps1, ps3) if layer == 0 else (ps1,)):
                            for k in range(KD):
                                last = three_products(nc, ps[f % 2][:, 0:SL], [part[:, k, f * P:(f + 1) * P] for part in w[q][j]],
                                                      [part[:, k, :] for part in xsT[q]], k == 0, k == KD - 1)
                        last.then_inc(multiplied, 1)
                    if more:
                        turn(n + 1, i + q, 1 - q)
                    pe.wait_ge(w_low[-1], CREDIT + n + 1)
                    pe.wait_ge(y_taken, CREDIT + n)
                    for h in range(2):
                        for f in range(FC):
                            if h == 0:
                                pe.wait_ge(hidden, CREDIT + n * FC + f + 1)
                            last = three_products(nc, psY[q][0:HALF, h * D:(h + 1) * D],
                                                  [part[:, f, h * HALF:(h + 1) * HALF] for part in hid],
                                                  [part[:, f, :] for part in w[q][-1]], f == 0, f == FC - 1)
                    last.then_inc(y_ready, 1)

                turn(0, 0, 0)
                steps(pe, step)

            @block.scalar
            def _(act):
                def split(n, i, q):
                    act.wait_ge(turned[q], CREDIT + i + 1)
                    nc.scalar.copy(xsT[q][0][:], psX[q][:, 0:KD * SL].rearrange("p (k s) -> p k s", k=KD)).then_inc(xsT_high, 1)
                    for j in range(NW):
                        act.wait_ge(w_in[j], 16 * (n + 1))
                        if j == 0 and (not isinstance(n, int) or n > 1):
                            act.wait_ge(y_ready, CREDIT + n - 1)
                        nc.scalar.copy(w[q][j][0][:], raw[j][:]).then_inc(w_high[j], 1)

                def step(n, i, q, more):
                    if q == 0:
                        table.ahead(act, n)
                    if layer == 1:
                        act.wait_ge(b_in[q], 32 * (i + 1))
                    for f in range(FC):
                        act.wait_ge(multiplied, CREDIT + n * FC + f + 1)
                        if layer == 0:
                            nc.scalar.activation(act1[:, f % 2, :], ps1[f % 2][:, 0:SL], ACT.Silu).then_inc(silu, 1)
                            act.wait_ge(y_ready, CREDIT + n)
                            act.wait_ge(taken, CREDIT + n * FC + f + 1)
                            nc.scalar.copy(hid[0][:, f, :], whole[:, f % 2, :]).then_inc(hid_high, 1)
                        else:
                            act.wait_ge(hidden, CREDIT + n * FC + max(f - 1, 0))
                            nc.scalar.activation(whole[:, f % 2, :], ps1[f % 2][:, 0:SL], ACT.Gelu,
                                                 bias=b1[q][:, f:f + 1]).then_inc(taken, 1)
                    if more:
                        split(n + 1, i + q, 1 - q)

                split(0, 0, 0)
                steps(act, step)

            @block.vector
            def _(dve):
                v = nc.vector

                def split(n, i, q):
                    dve.wait_ge(xsT_high, CREDIT + n + 1)
                    v.tensor_tensor(xsT[q][1][:], psX[q][:, 0:KD * SL].rearrange("p (k s) -> p k s", k=KD),
                                    xsT[q][0][:].bitcast(F32), ALU.subtract).then_inc(xsT_low, 1)
                    for j in range(LOW_BY_DVE):
                        dve.wait_ge(w_high[j], CREDIT + n + 1)
                        v.tensor_tensor(w[q][j][1][:], raw[j][:], w[q][j][0][:].bitcast(F32), ALU.subtract).then_inc(w_low[j], 1)

                def step(n, i, q, more):
                    for f in range(FC):
                        if layer == 0:
                            dve.wait_ge(silu, CREDIT + n * FC + f + 1)
                            v.tensor_tensor(whole[:, f % 2, :], ps3[f % 2][:, 0:SL], act1[:, f % 2, :], ALU.mult).then_inc(taken, 1)
                        else:
                            if f == 0:
                                dve.wait_ge(y_ready, CREDIT + n)
                            dve.wait_ge(taken, CREDIT + n * FC + f + 1)
                            v.tensor_copy(hid[0][:, f, :], whole[:, f % 2, :]).then_inc(hid_high, 1)
                        dve.wait_ge(hid_high, CREDIT + n * FC + f + 1)
                        v.tensor_tensor(hid[1][:, f, :], whole[:, f % 2, :], hid[0][:, f, :].bitcast(F32), ALU.subtract).then_inc(hidden, 1)
                    if more:
                        split(n + 1, i + q, 1 - q)
                    dve.wait_ge(y_out[q], CREDIT + 16 * i)
                    dve.wait_ge(y_ready, CREDIT + n + 1)
                    src = psY[q][0:HALF, 0:2 * D].rearrange("p (h d) -> p h d", h=2)
                    if layer == 0:
                        v.tensor_copy(ys[q][:], src).then_inc(y_taken, 1)
                    else:
                        v.tensor_tensor(ys[q][:], src, spread(b2[q][0:HALF, :], 2), ALU.add).then_inc(y_taken, 1)
                    dve.wait_ge(y_taken, CREDIT + n + 1)
                    dve.sem_inc(done[q], 1)

                split(0, 0, 0)
                steps(dve, step)


def combine_phase(core, layer, slots, weights, acc):
    nc, ins = core.nc, core.ins
    result = core.result0 if layer == 0 else core.result1
    with Phase(core, f"combine{layer}") as ph:
        ys = ph.sb("ys", [S, 2, B, D])
        sums = ph.sb("sums", [S, B, D])
        GROUP = 2
        fetched = [ph.plain(f"fetched{g}") for g in range(B // GROUP)]
        summed, loaded, stored, gated = ph.sem("summed"), ph.sem("loaded"), ph.sem("stored"), ph.sem("gated")
        stats_done, moments, rstd_ready, pool_steps, normed = (ph.sem(n) for n in ("stats_done", "moments", "rstd_ready", "pool_steps", "normed"))
        ln_w, ln_b = ph.sb("ln_w", [S, D]), ph.sb("ln_b", [S, D])
        stats, work = ph.sb("stats", [S, B, 6]), ph.sb("work", [S, 4, B])
        mean, rstd, t0, t1 = (work[:, k, :] for k in range(4))
        ph.credit()
        gate = core.gates[0:S, 2 + layer:3 + layer]

        def tile(buf, i):
            return buf[:, bass.ds(i, 1), :].rearrange("p a d -> p (a d)")

        with nc.Block() as block:
            @block.gpsimd
            def _(pool):
                for t in range(B):
                    for k in range(2):
                        pool.indirect_dma_start(ys[:, k, t, :], None, result,
                                                bass.IndirectOffsetOnAxis(ap=slots[:, k, t:t + 1], axis=0)).then_inc(fetched[t // GROUP], 16)
                if layer == 1:
                    step = Steps(pool, pool_steps, CREDIT)
                    pool.wait_ge(moments, CREDIT + 6)
                    step.then(pool.tensor_scalar(t1, t1, LAST_EPS, None, ALU.add))
                    pool.tensor_tensor(rstd, t1, core.half[0:S, 0:B], ALU.pow).then_inc(rstd_ready, 1)

            @block.vector
            def _(dve):
                v = nc.vector
                PER = 3
                if layer == 1:
                    dve.wait_ge(loaded, CREDIT + 32)
                    for row in (ln_w, ln_b):
                        v.tensor_scalar(row[:], row[:], gate, None, ALU.mult).then_inc(gated, 1)
                    dve.wait_ge(gated, CREDIT + 2)
                    for t in range(B):
                        v.tensor_tensor(core.x[:, t, :], core.x[:, t, :], ln_b[:], ALU.add).then_inc(gated, 1)
                for group in range(B // GROUP):
                    dve.wait_ge(fetched[group], 16 * 2 * GROUP)
                    pair = range(group * GROUP, (group + 1) * GROUP)
                    for k in range(2):
                        for t in pair:
                            v.scalar_tensor_tensor(sums[:, t, :], ys[:, k, t, :], weights[:, k, t:t + 1],
                                                   (acc if k == 0 else sums)[:, t, :], ALU.mult, ALU.add).then_inc(summed, 1)
                        dve.wait_ge(summed, CREDIT + group * GROUP * PER + GROUP * (k + 1))
                    for t in pair:
                        if layer == 0:
                            v.scalar_tensor_tensor(core.x[:, t, :], sums[:, t, :], gate, core.x[:, t, :], ALU.mult, ALU.add).then_inc(summed, 1)
                        else:
                            v.bn_stats(stats[:, t, :], sums[:, t, :]).then_inc(summed, 1)
                if layer == 1:
                    dve.wait_ge(summed, CREDIT + PER * B)
                    step = Steps(dve, moments, CREDIT)
                    me, ve, mo, vo = (stats[:, :, k] for k in (1, 2, 4, 5))
                    step.then(v.tensor_tensor(mean, me, mo, ALU.add))
                    step.then(v.tensor_scalar(mean, mean, 0.5, None, ALU.mult))
                    step.then(v.tensor_tensor(t0, me, mo, ALU.subtract))
                    step.then(v.scalar_tensor_tensor(t0, t0, 0.25, t0, ALU.mult, ALU.mult))
                    step.then(v.tensor_tensor(t1, ve, vo, ALU.add))
                    step.then(v.scalar_tensor_tensor(t1, t1, 1.0 / D, t0, ALU.mult, ALU.add))
                    dve.wait_ge(rstd_ready, CREDIT + 1)
                    dve.wait_ge(gated, CREDIT + 2 + B)
                    with dve.Fori(0, B // 2) as j:
                        for q in range(2):
                            t = 2 * j + q
                            v.scalar_tensor_tensor(tile(sums, t), tile(sums, t), work[:, 0, bass.ds(t, 1)], ln_w[:],
                                                   ALU.subtract, ALU.mult).then_inc(normed, 1)
                        dve.wait_ge(normed, CREDIT + j * 4 + 2)
                        for q in range(2):
                            t = 2 * j + q
                            v.scalar_tensor_tensor(tile(core.x, t), tile(sums, t), work[:, 1, bass.ds(t, 1)], tile(core.x, t),
                                                   ALU.mult, ALU.add).then_inc(normed, 1)

            @block.sync
            def _(sync):
                if layer == 1:
                    sync.dma_start(ln_w[:], ins["L1_ffn_ln_w"].partition_broadcast(S)).then_inc(loaded, 16)
                    sync.dma_start(ln_b[:], ins["L1_ffn_ln_b"].partition_broadcast(S)).then_inc(loaded, 16)
                    PART = B // 4
                    for h in range(4):
                        tiles = slice(PART * h, PART * (h + 1))
                        sync.wait_ge(normed, CREDIT + 2 * PART * (h + 1))
                        sync.dma_start(core.out[tiles].rearrange("b s d -> s b d"), core.x[:, tiles, :]).then_inc(stored, 16)
                    sync.wait_ge(stored, CREDIT + 64)


def program(nc, ins, out):
    with ExitStack() as ctx:
        core = Core(nc, ctx, ins, out)
        setup_phase(core)
        weights = ctx.enter_context(nc.sbuf_tensor("weights", [S, 2, B], F32))
        slots = ctx.enter_context(nc.sbuf_tensor("slots", [S, 2, B], I32))
        blocks = ctx.enter_context(nc.sbuf_tensor("blocks", [P, 2, NBLK1], I32))
        place = ctx.enter_context(nc.sbuf_tensor("place", [S, 2, 2, B], F32))
        tokens = ctx.enter_context(nc.sbuf_tensor("tokens", [P, NBLK1 * BLK1 // P], I32))
        logits0 = ctx.enter_context(nc.sbuf_tensor("logits0", [S, B, E0], F32))
        logits1 = ctx.enter_context(nc.sbuf_tensor("logits1", [S, B, E1], F32))
        with ExitStack() as first:
            given = AttentionWeights(core, first, 0)
            norm_phase(core, "norm_a0", following=given)
            attention_phase(core, 0, given)
        with ExitStack() as layer0:
            acc = layer0.enter_context(nc.sbuf_tensor("shared_acc", [S, B, D], F32))
            with ExitStack() as routing:
                ranking = Ranking(core, routing)
                with ExitStack() as shared:
                    given = SharedWeights(core, shared)
                    with nc.sbuf_tensor("x_normed0", [S, B, D], F32) as core.xn:
                        norm_phase(core, "norm_f0", (ins["L0_ffn_gate_w"], None, logits0))
                        route_phase(core, 0, logits0[:], weights, slots, place, ranking=ranking, following=given)
                    shared_phase(core, acc, given, ranking, weights)
                invert_phase(core, 0, place, tokens, slots, ranking)
            experts_phase(core, 0, tokens)
            combine_phase(core, 0, slots, weights, acc)
        core.xn = None
        with ExitStack() as second:
            given = AttentionWeights(core, second, 1)
            norm_phase(core, "norm_a1", following=given)
            attention_phase(core, 1, given)
        with ExitStack() as layer1:
            core.xn = layer1.enter_context(nc.sbuf_tensor("x_normed1", [S, B, D], F32))
            norm_phase(core, "norm_f1", (ins["L1_ffn_router_w"], ins["L1_ffn_router_b"], logits1))
            route_phase(core, 1, logits1[:], weights, slots, place, blocks)
            invert_phase(core, 1, place, tokens)
            experts_phase(core, 1, tokens, blocks)
            combine_phase(core, 1, slots, weights, core.xn)


def kernel(**inputs):
    import numpy as np
    import concourse.bacc as bacc
    from concourse.bass_utils import run_bass_kernel_spmd

    lay = {
        "ctx_1024": lambda a: a.transpose(0, 2, 1),
        "L0_xattn_bq": lambda a: a.reshape(-1, P).T,
        "L0_xattn_bk": lambda a: a.reshape(-1, P).T,
        "L1_ffn_router_w": lambda a: a.T,
        "L1_ffn_w1": lambda a: a.transpose(0, 2, 1).reshape(E1, KD, P, FF1).transpose(0, 2, 1, 3).reshape(E1 * P, KD * FF1),
        "L1_ffn_b1": lambda a: a.reshape(E1, FF1 // P, P).transpose(0, 2, 1).reshape(E1 * P, FF1 // P),
        "L1_ffn_w2": lambda a: a.transpose(0, 2, 1).reshape(E1, FF1 // P, P, D).transpose(0, 2, 1, 3).reshape(E1 * P, FF1 // P * D),
    }
    nc = bacc.Bacc("TRN2", target_bir_lowering=False, num_devices=1)
    arrays, ins = {}, {}
    for name, value in inputs.items():
        a = np.asarray(value)
        a = np.ascontiguousarray(lay[name](a) if name in lay else a)
        arrays[f"in_{name}_dram"] = a
        ins[name] = nc.dram_tensor(f"in_{name}_dram", a.shape, mybir.dt.from_np(a.dtype), kind="ExternalInput").ap()
    out = nc.dram_tensor("out_dram", (B, S, D), F32, kind="ExternalOutput").ap()
    program(nc, ins, out)
    r = run_bass_kernel_spmd(nc, [arrays], core_ids=[0])
    return r.results[0]["out_dram"]
```
